# Optimizing a Trainium2 kernel written in Bass

```python
import numpy as np
import jax
import jax.numpy as jnp

def _softmax(x, axis=-1):
    return jax.nn.softmax(x, axis=axis)

def _gelu(x):
    return jax.nn.gelu(x, approximate=True)

def _silu(x):
    return jax.nn.silu(x)

def _sigmoid(x):
    return jax.nn.sigmoid(x)

def _layernorm(x, axis=-1, eps=1e-05):
    m = jnp.mean(x, axis=axis, keepdims=True)
    v = jnp.var(x, axis=axis, keepdims=True)
    return (x - m) / jnp.sqrt(v + eps)

def _scatter_add(tgt, idx, src, axis=0):
    return tgt.at[idx].add(src)

def _segment_sum(src, seg, n):
    return jax.ops.segment_sum(src, seg, n)
kernel_name = 'mk_gnn_resnorm_d4_gnn_r64_ef5f40'

def setup_inputs(seed: int=0):
    np.random.seed(seed)
    _w = jnp.asarray

    def _rec_inputs():
        import jax
        import jax.numpy as jnp
        _gk = jax.random.key(seed)
        x = -0.0002117 + 1 * jax.random.normal(jax.random.fold_in(_gk, 1), (50000, 256), jnp.float32)
        src = jax.random.randint(jax.random.fold_in(_gk, 2), (12500,), 0, 50000, jnp.int32)
        dst = jax.random.randint(jax.random.fold_in(_gk, 3), (12500,), 0, 50000, jnp.int32)
        _o = jnp.argsort(dst, stable=True)
        src = src[_o]
        dst = dst[_o]
        edge_attr_8 = -0.00019784 + 0.999804 * jax.random.normal(jax.random.fold_in(_gk, 12), (12500, 8), jnp.float32)
        edge_weight = jax.random.uniform(jax.random.fold_in(_gk, 14), (12500,), jnp.float32, 0.0, 1)
        return (x, src, dst, edge_attr_8, edge_weight)
    x, src, dst, edge_attr_8, edge_weight = _rec_inputs()

    def _L0_gnn_setup():
        import jax, jax.numpy as jnp
        import numpy as np
        N = 100000
        E = 50000
        DI = 256
        DO = 256
        BN_EPS = 1e-05

        def _bn_relu(h, gamma, beta):
            mean = jnp.mean(h, axis=0)
            var = jnp.var(h, axis=0)
            hn = (h - mean) * jax.lax.rsqrt(var + BN_EPS)
            return jax.nn.relu(hn * gamma + beta)
        key = jax.random.key(seed)
        ks = jax.random.split(key, 6)
        x = jax.random.normal(ks[0], (N, DI), dtype=jnp.float32)
        edge_row = jax.random.randint(ks[1], (E,), 0, N, dtype=jnp.int32)
        edge_col = jax.random.randint(ks[2], (E,), 0, N, dtype=jnp.int32)
        edge_vals = jnp.ones((E,), dtype=jnp.float32)
        eps = jnp.zeros((1,), dtype=jnp.float32)
        W1 = jax.random.normal(ks[3], (DI, DO), dtype=jnp.float32) * 0.05
        b1 = jnp.zeros((DO,), dtype=jnp.float32)
        g1 = jnp.ones((DO,), dtype=jnp.float32)
        be1 = jnp.zeros((DO,), dtype=jnp.float32)
        W2 = jax.random.normal(ks[4], (DO, DO), dtype=jnp.float32) * 0.05
        b2 = jnp.zeros((DO,), dtype=jnp.float32)
        g2 = jnp.ones((DO,), dtype=jnp.float32)
        be2 = jnp.zeros((DO,), dtype=jnp.float32)
        return {'x': x, 'edge_row': edge_row, 'edge_col': edge_col, 'edge_vals': edge_vals, 'eps': eps, 'W1': W1, 'b1': b1, 'g1': g1, 'be1': be1, 'W2': W2, 'b2': b2, 'g2': g2, 'be2': be2}
    _L0_gnn_all = _L0_gnn_setup()
    _L0_gnn_in = {k: v for k, v in _L0_gnn_all.items() if k in ('eps', 'W1', 'b1', 'g1', 'be1', 'W2', 'b2', 'g2', 'be2')}
    del _L0_gnn_all

    def _L1_gnn_setup():
        import jax, jax.numpy as jnp
        import numpy as np
        ALPHA = 0.2
        N_NODES = 100000
        N_EDGES = 25000
        NFEAT = 256
        HID = 64
        NHEADS = 4

        def _gat_head(x, src, dst, Wh, ah, n_nodes):
            hid = Wh.shape[1]
            h = x @ Wh
            h = jnp.where(jnp.isnan(h), 0.0, h)
            a1, a2 = (ah[0, :hid], ah[0, hid:])
            alpha_src = h @ a1
            alpha_dst = h @ a2
            s = alpha_src[src] + alpha_dst[dst]
            e = jnp.exp(-jax.nn.leaky_relu(s, ALPHA))
            e = jnp.where(jnp.isnan(e), 0.0, e)
            rowsum = jax.ops.segment_sum(e, src, num_segments=n_nodes)
            hp = jax.ops.segment_sum(e[:, None] * h[dst], src, num_segments=n_nodes)
            hp = jnp.where(jnp.isnan(hp), 0.0, hp)
            hp = hp / rowsum[:, None]
            hp = jnp.where(jnp.isnan(hp), 0.0, hp)
            return jax.nn.elu(hp)
        key = jax.random.key(seed)
        k1, k2, k3, k4 = jax.random.split(key, 4)
        x = jax.random.normal(k1, (N_NODES, NFEAT), dtype=jnp.float32)
        edge_index = jax.random.randint(k2, (2, N_EDGES), 0, N_NODES, dtype=jnp.int64)
        W = jax.random.normal(k3, (NHEADS, NFEAT, HID), dtype=jnp.float32) * (1.414 * np.sqrt(2.0 / (NFEAT + HID)))
        a = jax.random.normal(k4, (NHEADS, 1, 2 * HID), dtype=jnp.float32) * (1.414 * np.sqrt(2.0 / (1 + 2 * HID)))
        return {'x': x, 'edge_index': edge_index, 'W': W, 'a': a}
    _L1_gnn_all = _L1_gnn_setup()
    _L1_gnn_in = {k: v for k, v in _L1_gnn_all.items() if k in ('W', 'a')}
    del _L1_gnn_all

    def _L2_gnn_setup():
        import jax, jax.numpy as jnp
        import numpy as np
        N = 100000
        E = 12500
        FEAT = 256
        HEADS = 8
        HEAD_DIM = FEAT // HEADS
        SCALING = HEAD_DIM ** (-0.5)
        key = jax.random.key(seed)
        ks = jax.random.split(key, 8)
        w_scale = (2.0 / (FEAT + FEAT)) ** 0.5
        return {'nfeat': jax.random.normal(ks[0], (N, FEAT), dtype=jnp.float32), 'attn_bias': jax.random.normal(ks[1], (E, HEADS), dtype=jnp.float32), 'Wq': jax.random.normal(ks[2], (FEAT, FEAT), dtype=jnp.float32) * w_scale, 'Wk': jax.random.normal(ks[3], (FEAT, FEAT), dtype=jnp.float32) * w_scale, 'Wv': jax.random.normal(ks[4], (FEAT, FEAT), dtype=jnp.float32) * w_scale, 'Wo': jax.random.normal(ks[5], (FEAT, FEAT), dtype=jnp.float32) * w_scale, 'src': jax.random.randint(ks[6], (E,), 0, N, dtype=jnp.int32), 'dst': jax.random.randint(ks[7], (E,), 0, N, dtype=jnp.int32)}
    _L2_gnn_all = _L2_gnn_setup()
    _L2_gnn_in = {k: v for k, v in _L2_gnn_all.items() if k in ('Wq', 'Wk', 'Wv', 'Wo')}
    del _L2_gnn_all

    def _L3_gnn_setup():
        import jax, jax.numpy as jnp
        import numpy as np
        N = 100000
        E = 25000
        IN = 256
        H = 4
        C = 64
        key = jax.random.key(seed)
        k1, k2, k3, k4, k5, k6 = jax.random.split(key, 6)
        x = jax.random.normal(k1, (N, IN), dtype=jnp.float32)
        edge_index = jax.random.randint(k2, (2, E), 0, N, dtype=jnp.int64)
        W = jax.random.normal(k3, (IN, H * C), dtype=jnp.float32) * (1.0 / np.sqrt(IN))
        att_src = jax.random.normal(k4, (H, C), dtype=jnp.float32) * 0.1
        att_dst = jax.random.normal(k5, (H, C), dtype=jnp.float32) * 0.1
        bias = jax.random.normal(k6, (H * C,), dtype=jnp.float32) * 0.01
        return {'x': x, 'edge_index': edge_index, 'W': W, 'att_src': att_src, 'att_dst': att_dst, 'bias': bias}
    _L3_gnn_all = _L3_gnn_setup()
    _L3_gnn_in = {k: v for k, v in _L3_gnn_all.items() if k in ('W', 'att_src', 'att_dst', 'bias')}
    del _L3_gnn_all
    return {'x': x, 'src': src, 'dst': dst, 'edge_attr_8': edge_attr_8, 'edge_weight': edge_weight, 'L0_gnn_eps': _L0_gnn_in['eps'], 'L0_gnn_W1': _L0_gnn_in['W1'], 'L0_gnn_b1': _L0_gnn_in['b1'], 'L0_gnn_g1': _L0_gnn_in['g1'], 'L0_gnn_be1': _L0_gnn_in['be1'], 'L0_gnn_W2': _L0_gnn_in['W2'], 'L0_gnn_b2': _L0_gnn_in['b2'], 'L0_gnn_g2': _L0_gnn_in['g2'], 'L0_gnn_be2': _L0_gnn_in['be2'], 'L1_gnn_W': _L1_gnn_in['W'], 'L1_gnn_a': _L1_gnn_in['a'], 'L2_gnn_Wq': _L2_gnn_in['Wq'], 'L2_gnn_Wk': _L2_gnn_in['Wk'], 'L2_gnn_Wv': _L2_gnn_in['Wv'], 'L2_gnn_Wo': _L2_gnn_in['Wo'], 'L3_gnn_W': _L3_gnn_in['W'], 'L3_gnn_att_src': _L3_gnn_in['att_src'], 'L3_gnn_att_dst': _L3_gnn_in['att_dst'], 'L3_gnn_bias': _L3_gnn_in['bias']}

def reference(x, src, dst, edge_attr_8, edge_weight, L0_gnn_eps, L0_gnn_W1, L0_gnn_b1, L0_gnn_g1, L0_gnn_be1, L0_gnn_W2, L0_gnn_b2, L0_gnn_g2, L0_gnn_be2, L1_gnn_W, L1_gnn_a, L2_gnn_Wq, L2_gnn_Wk, L2_gnn_Wv, L2_gnn_Wo, L3_gnn_W, L3_gnn_att_src, L3_gnn_att_dst, L3_gnn_bias):
    import jax
    import jax.numpy as jnp

    def _L0_gnn_ref(x, edge_row, edge_col, edge_vals, eps, W1, b1, g1, be1, W2, b2, g2, be2):
        import jax, jax.numpy as jnp
        import numpy as np
        N = 100000
        E = 50000
        DI = 256
        DO = 256
        BN_EPS = 1e-05

        def _bn_relu(h, gamma, beta):
            mean = jnp.mean(h, axis=0)
            var = jnp.var(h, axis=0)
            hn = (h - mean) * jax.lax.rsqrt(var + BN_EPS)
            return jax.nn.relu(hn * gamma + beta)
        n = x.shape[0]
        msgs = edge_vals[:, None] * x[edge_col]
        agg = jax.ops.segment_sum(msgs, edge_row, num_segments=n)
        h = (1.0 + eps[0]) * x + agg
        h = _bn_relu(h @ W1 + b1, g1, be1)
        h = _bn_relu(h @ W2 + b2, g2, be2)
        return h

    def _L1_gnn_ref(x, edge_index, W, a):
        import jax, jax.numpy as jnp
        import numpy as np
        ALPHA = 0.2
        N_NODES = 100000
        N_EDGES = 25000
        NFEAT = 256
        HID = 64
        NHEADS = 4

        def _gat_head(x, src, dst, Wh, ah, n_nodes):
            hid = Wh.shape[1]
            h = x @ Wh
            h = jnp.where(jnp.isnan(h), 0.0, h)
            a1, a2 = (ah[0, :hid], ah[0, hid:])
            alpha_src = h @ a1
            alpha_dst = h @ a2
            s = alpha_src[src] + alpha_dst[dst]
            e = jnp.exp(-jax.nn.leaky_relu(s, ALPHA))
            e = jnp.where(jnp.isnan(e), 0.0, e)
            rowsum = jax.ops.segment_sum(e, src, num_segments=n_nodes)
            hp = jax.ops.segment_sum(e[:, None] * h[dst], src, num_segments=n_nodes)
            hp = jnp.where(jnp.isnan(hp), 0.0, hp)
            hp = hp / rowsum[:, None]
            hp = jnp.where(jnp.isnan(hp), 0.0, hp)
            return jax.nn.elu(hp)
        n_nodes = x.shape[0]
        src, dst = (edge_index[0], edge_index[1])
        outs = [_gat_head(x, src, dst, W[h], a[h], n_nodes) for h in range(W.shape[0])]
        out = jnp.concatenate(outs, axis=1)
        return jax.nn.elu(out)

    def _L2_gnn_ref(nfeat, attn_bias, Wq, Wk, Wv, Wo, src, dst):
        import jax, jax.numpy as jnp
        import numpy as np
        N = 100000
        E = 12500
        FEAT = 256
        HEADS = 8
        HEAD_DIM = FEAT // HEADS
        SCALING = HEAD_DIM ** (-0.5)
        n = nfeat.shape[0]
        q = (nfeat @ Wq.T).reshape(n, HEADS, HEAD_DIM) / SCALING
        k = (nfeat @ Wk.T).reshape(n, HEADS, HEAD_DIM)
        v = (nfeat @ Wv.T).reshape(n, HEADS, HEAD_DIM)
        attn = jnp.einsum('ehd,ehd->eh', k[src], q[dst])
        attn = attn + attn_bias
        m = jax.ops.segment_max(attn, dst, num_segments=n)
        a = jnp.exp(attn - m[dst])
        s = jax.ops.segment_sum(a, dst, num_segments=n)
        a = a / s[dst]
        out = jax.ops.segment_sum(v[src] * a[:, :, None], dst, num_segments=n)
        return out.reshape(n, FEAT) @ Wo.T

    def _L3_gnn_ref(x, edge_index, W, att_src, att_dst, bias):
        import jax, jax.numpy as jnp
        import numpy as np
        N = 100000
        E = 25000
        IN = 256
        H = 4
        C = 64
        n = x.shape[0]
        loops = jnp.arange(n, dtype=edge_index.dtype)
        src = jnp.concatenate([edge_index[0], loops])
        dst = jnp.concatenate([edge_index[1], loops])
        xp = (x @ W).reshape(n, H, C)
        a_src = jnp.einsum('nhc,hc->nh', xp, att_src)
        a_dst = jnp.einsum('nhc,hc->nh', xp, att_dst)
        alpha = jax.nn.leaky_relu(a_src[src] + a_dst[dst], negative_slope=0.2)
        amax = jax.ops.segment_max(alpha, dst, num_segments=n)
        amax = jnp.where(jnp.isfinite(amax), amax, 0.0)
        ex = jnp.exp(alpha - amax[dst])
        denom = jax.ops.segment_sum(ex, dst, num_segments=n)
        w = ex / denom[dst]
        msg = xp[src] * w[..., None]
        agg = jax.ops.segment_sum(msg, dst, num_segments=n)
        out = agg.reshape(n, H * C) + bias
        return jax.nn.elu(out)
    edge_index = jnp.stack([src, dst])
    x = _layernorm(x + _L0_gnn_ref(x, src, dst, edge_weight, L0_gnn_eps, L0_gnn_W1, L0_gnn_b1, L0_gnn_g1, L0_gnn_be1, L0_gnn_W2, L0_gnn_b2, L0_gnn_g2, L0_gnn_be2), axis=-1)
    x = _layernorm(x + _L1_gnn_ref(x, edge_index, L1_gnn_W, L1_gnn_a), axis=-1)
    x = _layernorm(x + _L2_gnn_ref(x, edge_attr_8, L2_gnn_Wq, L2_gnn_Wk, L2_gnn_Wv, L2_gnn_Wo, src, dst), axis=-1)
    x = _layernorm(x + _L3_gnn_ref(x, edge_index, L3_gnn_W, L3_gnn_att_src, L3_gnn_att_dst, L3_gnn_bias), axis=-1)
    return x

_drawn_inputs = setup_inputs


def setup_inputs(seed=0):
    import zlib

    import numpy as np

    out = dict(_drawn_inputs(seed))
    spreads = {'L0_gnn_b1': (0.0, 0.8),
     'L0_gnn_g1': (1.0, 0.2),
     'L0_gnn_be1': (0.0, 0.1),
     'L0_gnn_b2': (0.0, 0.8),
     'L0_gnn_g2': (1.0, 0.2),
     'L0_gnn_be2': (0.0, 0.1)}
    factors = {'edge_attr_8': 7.841, 'L3_gnn_bias': 8.0}
    for name, (base, spread) in spreads.items():
        noise = np.random.default_rng([zlib.crc32(name.encode()), seed]).standard_normal(out[name].shape)
        drawn = base * np.exp(spread * noise) if base else spread * noise
        out[name] = jnp.asarray(drawn.astype(out[name].dtype))
    for name, factor in factors.items():
        out[name] = (out[name] * factor).astype(out[name].dtype)
    return out
```

```python
from contextlib import ExitStack

import concourse.bass as bass
import concourse.mybir as mybir
import numpy as np

F32 = mybir.dt.float32
I32 = mybir.dt.int32
BF16 = mybir.dt.bfloat16
ALU = mybir.AluOpType
ACT = mybir.ActivationFunctionType
X = mybir.AxisListType.X

N, F, E = 50000, 256, 12500
P = 125
T = E // P
CH = 4 * P
NCH = N // CH
KH = F // 128
EPS = 1e-5
ALPHA = 0.2
H1, C1 = 4, 64
H2, C2 = 8, 32
BIG = 3.0e38
TINY = 1.0e-37
DROP = 1 << 20
RC = 12
CUTS = ((0, 112), (112, 13))


class Use:

    def __init__(self, eng, u):
        self.eng, self.u, self.known = eng, u, {}

    def value(self, scale, offset=0):
        if isinstance(self.u, int):
            return self.u * scale + offset
        return self.u * scale + offset if offset else self.u * scale

    free = property(lambda self: self.value(1))
    ready = property(lambda self: self.value(1, 1))
    free16 = property(lambda self: self.value(16))
    ready16 = property(lambda self: self.value(16, 16))
    free32 = property(lambda self: self.value(32))
    ready32 = property(lambda self: self.value(32, 32))

    def base(self, k):
        return self.value(k)


class Chain:

    def __init__(self, eng, sem, base=0):
        self.eng, self.sem, self.base, self.n = eng, sem, base, 0

    def step(self, ins):
        ins.then_inc(self.sem, 1)
        self.n += 1
        self.eng.wait_ge(self.sem, self.base + self.n)


def stages(eng, steps, tiles=100, total=None):
    total = tiles if total is None else total
    lag = len(steps) - 1
    head = 2 * ((lag + 1) // 2)

    def alone(t):
        for k, step in enumerate(steps):
            if 0 <= t - k < total:
                step(t - k, (t - k) % 2, Use(eng, (t - k) // 2))
    for t in range(head):
        alone(t)
    with eng.Fori(head // 2, tiles // 2) as j:
        uses = {}
        for a in range(2):
            for k, step in enumerate(steps):
                back = (a - k) // 2
                if back not in uses:
                    uses[back] = Use(eng, j + back if back else j)
                step(2 * j + (a - k) if a != k else 2 * j, (a - k) % 2, uses[back])
    for t in range(tiles, total + lag):
        alone(t)


def each_tile(eng, body, tiles=100, total=None):
    stages(eng, [body], tiles, total)


def two_stages(eng, first, second, tiles=100, total=None):
    stages(eng, [first, second], tiles, total)


def col(t):
    return t if isinstance(t, slice) else bass.ds(t, 1)


class Phase:

    def __init__(self, nc, name):
        self.nc, self.name = nc, name
        self.ctx = ExitStack()
        self.sems = []

    def sb(self, name, shape, dt=F32):
        return self.ctx.enter_context(self.nc.sbuf_tensor(f"{self.name}_{name}", shape, dt))

    def ps(self, name, shape, dt=F32):
        return self.ctx.enter_context(self.nc.psum_tensor(f"{self.name}_{name}", shape, dt))

    def sem(self, name):
        s = self.nc.alloc_semaphore(f"{self.name}_{name}")
        self.sems.append(s)
        return s

    def pair(self, name):
        return [self.sem(f"{name}0"), self.sem(f"{name}1")]

    def end(self):
        self.nc.clear_and_free_semaphores(self.sems)
        self.nc.all_engine_barrier()
        self.ctx.close()


def load_rows(eng, dst, src, sem):
    for a, n in CUTS:
        eng.dma_start(dst[a:a + n], src[a:a + n]).then_inc(sem, 16)


class Rows:

    def __init__(self, ph, pool, rows):
        self.pool, self.bound, self.started = pool, pool.to_reg(rows - 1), ph.sem("started")

    def after_wait(self):
        self.pool.sem_inc(self.started, 1)

    def gather(self, out, table, index, sem):
        self.after_wait()
        self.pool.indirect_dma_start(out, None, table, bass.IndirectOffsetOnAxis(index, 0)).then_inc(sem, 16)

    def scatter(self, table, index, rows, sem):
        self.after_wait()
        self.pool.indirect_dma_start(table, bass.IndirectOffsetOnAxis(index, 0), rows, None,
                                     bounds_check=self.bound, oob_is_err=False).then_inc(sem, 16)


def setup(nc, env, d):
    ph = Phase(nc, "setup")
    s_dma, s_g, s_g2, s_v = ph.sem("dma"), ph.sem("masks"), ph.sem("iota"), ph.sem("steps")
    s_w = ph.sem("wrow")
    iota_i = ph.sb("iota_i", [128, 256], I32)
    keys = ph.sb("keys", [P, 2, T], I32)
    keyp = ph.sb("keyp", [P, 2, T], I32)
    wts = ph.sb("wts", [P, T])
    attr = ph.sb("attr", [P, T, H2])
    arow = ph.sb("arow", [128, 4, F])
    prod = ph.sb("prod", [128, KH, F])
    w_gat, w_self = env["w_gat"], env["w_self"]
    loads = [
        (keys[:, 0, :], d["src"].rearrange("(p t) -> p t", p=P)),
        (keys[:, 1, :], d["dst"].rearrange("(p t) -> p t", p=P)),
        (wts[:, :], d["edge_weight"].rearrange("(p t) -> p t", p=P)),
        (attr[:, :, :], d["edge_attr_8"].rearrange("(p t) h -> p t h", p=P)),
        (env["onep"][:, :], d["L0_gnn_eps"].rearrange("(o n) -> o n", o=1).broadcast_to([128, 1])),
        (env["bias_row"][0:1, :], d["L3_gnn_bias"].rearrange("(o n) -> o n", o=1)),
        (env["bias_all"][:, :], d["L3_gnn_bias"].rearrange("(o n) -> o n", o=1).broadcast_to([128, F])),
        (w_gat[:, :, 0:F], d["W_gat"].rearrange("(k p) n -> p k n", p=128)),
        (w_self[:, :, 0:F], d["L3_gnn_W"].rearrange("(k p) n -> p k n", p=128)),
        (env["w_kv"][:, :, 0:F], d["WkT"].rearrange("(k p) n -> p k n", p=128)),
        (env["w_kv"][:, :, F:2 * F], d["WvT"].rearrange("(k p) n -> p k n", p=128)),
    ]
    for name, src in (("w1", "L0_gnn_W1"), ("w2", "L0_gnn_W2"), ("w_q", "WqT"), ("w_o", "WoT")):
        loads.append((env[name][:, :, :], d[src].rearrange("(k p) n -> p k n", p=128)))
    for n, src in enumerate(("L0_gnn_b1", "L0_gnn_g1", "L0_gnn_be1", "L0_gnn_b2", "L0_gnn_g2", "L0_gnn_be2")):
        for k in range(KH):
            loads.append((env["bn"][:, n, k:k + 1], d[src].rearrange("(k p o) -> k p o", p=128, o=1)[k]))
    for n, src in enumerate(("a_src", "a_dst", "att_src", "att_dst")):
        loads.append((arow[:, n, :], d[src].rearrange("(o n) -> o n", o=1).broadcast_to([128, F])))

    with nc.Block() as block:
        @block.sync
        def _(sp):
            for dst, src in loads:
                sp.dma_start(dst, src).then_inc(s_dma, 16)

        @block.gpsimd
        def _(pool):
            pool.iota(iota_i[:, :], [[1, 256]], base=0, channel_multiplier=0).then_inc(s_g2, 1)
            pool.memset(env["ident"][:, :], 0.0).then_inc(s_g, 1)
            pool.memset(env["before"][:, :], 1.0).then_inc(s_g, 1)
            pool.memset(env["after"][:, :], 1.0).then_inc(s_g, 1)
            pool.memset(env["ones"][:, :], 1.0).then_inc(s_g, 1)
            pool.memset(env["zrow"][:, :], 0.0).then_inc(s_g, 1)
            pool.memset(env["zcol"][:, :], 0.0).then_inc(s_g, 1)
            pool.memset(env["zwide"][:, :], 0.0).then_inc(s_g, 1)
            pool.memset(env["minus1"][:, :], -1.0).then_inc(s_g, 1)
            pool.wait_ge(s_g, 8)
            pool.affine_select(out=env["ident"][:, :], in_=env["ident"][:, :], compare_op=ALU.not_equal, fill=1.0,
                               base=0, pattern=[[-1, 128]], channel_multiplier=1).then_inc(s_g, 1)
            pool.affine_select(out=env["before"][:, :], in_=env["before"][:, :], compare_op=ALU.is_gt, fill=0.0,
                               base=0, pattern=[[-1, 128]], channel_multiplier=1).then_inc(s_g, 1)
            pool.affine_select(out=env["after"][:, :], in_=env["after"][:, :], compare_op=ALU.is_gt, fill=0.0,
                               base=0, pattern=[[1, 128]], channel_multiplier=-1).then_inc(s_g, 1)

        @block.vector
        def _(dve):
            ch = Chain(dve, s_v)
            dve.wait_ge(s_g2, 1)
            dve.wait_ge(s_g, 11)
            ch.step(dve.tensor_copy(env["iota_row"][:, :], iota_i[:, :]))
            ch.step(dve.tensor_copy(env["ident_bf"][:, :], env["ident"][:, :]))
            dve.wait_ge(s_dma, 16 * len(loads))
            rec = env["rec"]
            for k in range(2):
                ch.step(dve.tensor_copy(rec[:, :, k], keys[:, k, :]))
                ch.step(dve.tensor_copy(env["keyf"][:, k, :], keys[:, k, :]))
            ch.step(dve.tensor_copy(rec[:, :, 2], wts[:, :]))
            ch.step(dve.memset(rec[:, :, 3], 0.0))
            ch.step(dve.tensor_copy(rec[:, :, 4:12], attr[:, :, :]))
            ch.step(dve.tensor_scalar(keyp[:, :, :], keys[:, :, :], 8, None, ALU.logical_shift_right))
            ch.step(dve.tensor_copy(env["digit"][:, 0, :, :], keyp[:, :, :]))
            ch.step(dve.tensor_scalar(keyp[:, :, :], keys[:, :, :], 255, None, ALU.bitwise_and))
            ch.step(dve.tensor_copy(env["digit"][:, 1, :, :], keyp[:, :, :]))
            ch.step(dve.tensor_scalar(env["onep"][:, :], env["onep"][:, :], 1.0, None, ALU.add))
            ch.step(dve.tensor_scalar(env["bias_row"][0:1, :], env["bias_row"][0:1, :], 1.0, None, ALU.add))
            ch.step(dve.tensor_scalar(env["bias_all"][:, :], env["bias_all"][:, :], 1.0, None, ALU.add))
            for w, n, out in ((w_gat, 1, w_gat[:, :, F:F + 4]), (w_gat, 0, env["w_gat_s"][:, :, :]),
                              (w_self, 2, w_self[:, :, F:F + 4]), (w_self, 3, w_self[:, :, F + 4:F + 8])):
                for k in range(KH):
                    ch.step(dve.tensor_tensor(prod[:, k, :], w[:, k, 0:F], arow[:, n, :], ALU.mult))
                    ch.step(dve.tensor_reduce(out[:, k, :], prod[:, k, :].rearrange("p (h c) -> p h c", h=4), X, ALU.add))
    ph.end()


def histogram(nc, env):
    ph = Phase(nc, "hist")
    hot = ph.sb("hot", [P, 2, 2, 2, 256], BF16)
    count = ph.sb("count", [128, 2, 2, 256])
    incl = ph.sb("incl", [128, 2, 2, 256])
    tot = ph.sb("tot", [128, 4])
    ones = ph.sb("ones", [128, 256])
    full = ph.sb("full", [128, 128])
    offs = ph.sb("offs", [128, 4])
    acc = ph.ps("acc", [128, 2, 512])
    off = ph.ps("off", [128, 512])
    s_hot, s_used = ph.pair("hot"), ph.pair("used")
    s_v, s_all, s_tot, s_off, s_one = ph.sem("steps"), ph.sem("counted"), ph.sem("totals"), ph.sem("offsets"), ph.sem("ones")
    base = env["base"]

    with nc.Block() as block:
        @block.vector
        def _(dve):
            dve.memset(ones[:, :], 1.0).then_inc(s_one, 1)
            dve.memset(full[:, :], 1.0).then_inc(s_one, 1)

            def tile(t, s, use):
                dve.wait_ge(s_used[s], use.free)
                for digit in range(2):
                    for key in range(2):
                        dve.tensor_scalar(hot[:, s, digit, key, :], env["iota_row"][0:P, :],
                                          env["digit"][:, digit, key, col(t)], None, ALU.is_equal).then_inc(s_hot[s], 1)
            with dve.Fori(0, T // 2) as j:
                use = Use(dve, j)
                for s in range(2):
                    tile(2 * j + s, s, use)
            ch = Chain(dve, s_v)
            dve.wait_ge(s_one, 2)
            dve.wait_ge(s_all, 1)
            ch.step(dve.tensor_copy(count[:, :, :, :], acc[:, :, :].rearrange("p k (h n) -> p k h n", h=2)))
            for key in range(2):
                for half in range(2):
                    ch.step(dve.tensor_tensor_scan(incl[:, key, half, :], ones[:, :], count[:, key, half, :],
                                                   0.0, ALU.mult, ALU.add))
            ch.step(dve.tensor_copy(tot[:, :].rearrange("p (k h) -> p k h", k=2), incl[:, :, :, 255]))
            dve.tensor_tensor(base[:, :, :, :], incl[:, :, :, :], count[:, :, :, :], ALU.subtract).then_inc(s_tot, 1)
            dve.wait_ge(s_off, 1)
            ch.step(dve.tensor_copy(offs[:, :], off[:, 0:4]))
            dve.wait_ge(s_tot, 1)
            for key in range(2):
                for half in range(2):
                    ch.step(dve.tensor_scalar(base[:, key, half, :], base[:, key, half, :],
                                              offs[:, 2 * key + half:2 * key + half + 1], None, ALU.add))

        @block.tensor
        def _(pe):
            for key in range(2):
                pe.matmul(acc[:, key, :], env["ident_bf"][:, :], env["zrow"][:, :], start=True, stop=True)
            with pe.Fori(0, T // 2) as j:
                ready = pe.snap(4 * j + 4)
                for s in range(2):
                    pe.wait_ge(s_hot[s], ready)
                    for key in range(2):
                        for half in range(2):
                            mm = pe.matmul(acc[:, key, 256 * half:256 * half + 256],
                                           hot[:, s, 0, key, 128 * half:128 * half + 128], hot[:, s, 1, key, :],
                                           start=False, stop=True, skip_group_check=True)
                    mm.then_inc(s_used[s], 1)
            mm = pe.matmul(acc[:, 1, :], env["ident_bf"][:, :], env["zrow"][:, :], start=False, stop=True,
                           skip_group_check=True)
            mm.then_inc(s_all, 1)
            pe.wait_ge(s_one, 2)
            pe.wait_ge(s_tot, 1)
            for key in range(2):
                pe.matmul(off[:, 2 * key:2 * key + 1], env["after"][:, :], tot[:, 2 * key:2 * key + 1], start=True, stop=True)
                pe.matmul(off[:, 2 * key + 1:2 * key + 2], env["after"][:, :], tot[:, 2 * key + 1:2 * key + 2],
                          start=True, stop=False)
                mm = pe.matmul(off[:, 2 * key + 1:2 * key + 2], full[:, :], tot[:, 2 * key:2 * key + 1],
                               start=False, stop=True)
            mm.then_inc(s_off, 1)
    ph.end()


def rank(nc, env, d):
    ph = Phase(nc, "rank")
    hot = ph.sb("hot", [P, 2, 2, 2, 256], BF16)
    keyb = ph.sb("keyb", [P, 2, 2, 128])
    hotT = ph.sb("hotT", [128, 2, 2, 2, P])
    table = ph.sb("table", [128, 2, 2, 2, 256])
    junk = ph.sb("junk", [P, 2, 2, 256])
    parts = ph.sb("parts", [P, 2, 2, 2])
    place = ph.sb("place", [P, 2, 2], I32)
    recs = ph.sb("recs", [P, 2, RC])
    keyf = env["keyf"]
    xin = ph.sb("xin", [P, 2, 4, F])
    xc = ph.sb("xc", [P, 2, 4, F + 4])
    tab = ph.ps("tab", [128, 2, 512])
    look = ph.ps("look", [P, 2, 256])
    rows = ph.ps("rows", [128, 2, 128])
    hT = ph.ps("hT", [128, 2, 2, 128], BF16)
    gram = env["gram"]
    s_hot, s_keyb, s_tab, s_tabT = ph.pair("hot"), ph.pair("keyb"), ph.pair("table"), ph.pair("hotT")
    s_hist, s_pT, s_look, s_parts = ph.pair("hist"), ph.pair("transposed"), ph.pair("looked"), ph.pair("parts")
    s_place, s_scat, s_scat2 = ph.pair("place"), ph.pair("scattered"), ph.pair("scattered_b")
    s_x, s_xc, s_gr, s_h = ph.pair("x"), ph.pair("xc"), ph.pair("gram"), ph.pair("h_stored")
    s_seed, s_one = ph.sem("seed"), ph.sem("ones")
    x_v = d["x"].rearrange("(c p j) f -> c p j f", p=P, j=4)
    h_v = env["H"].rearrange("(c p j) f -> c p j f", p=P, j=4)

    with nc.Block() as block:
        @block.sync
        def _(sp):
            def load(t, s, use):
                sp.wait_ge(s_xc[s], use.free)
                for a, n in CUTS:
                    sp.dma_start(xin[a:a + n, s, :, :], x_v[bass.ds(t, 1), a:a + n, :, :].rearrange("o p j f -> (o p) j f")).then_inc(s_x[s], 16)

            def store(t, s, use):
                sp.wait_ge(s_xc[s], use.ready)
                for a, n in CUTS:
                    sp.dma_start(h_v[bass.ds(t, 1), a:a + n, :, :].rearrange("o p j f -> (o p) j f"), xc[a:a + n, s, :, 0:F]).then_inc(s_h[s], 16)
            two_stages(sp, load, store, NCH)
            for s in range(2):
                sp.wait_ge(s_h[s], 32 * (NCH // 2))

        @block.scalar
        def _(act):
            act.preload_act_table_set("natural_log_exp_and_others")
            act.wait_ge(s_one, 2)

            def tile(t, s, use):
                if isinstance(t, int) and t == 0:
                    act.wait_ge(s_seed, 1)
                elif s == 0:
                    act.wait_ge(s_hist[1], use.free)
                else:
                    act.wait_ge(s_hist[0], use.ready)
                act.wait_ge(s_look[s], use.free)
                act.copy(table[:, s, :, :, :].rearrange("p k h n -> p k (h n)"), tab[:, :, :]).then_inc(s_tab[s], 1)
                act.wait_ge(s_pT[s], use.ready)
                act.copy(hotT[:, s, :, :, :].rearrange("p k h n -> p (k h) n"), hT[:, :, :, 0:P].rearrange("p k h n -> p (k h) n")).then_inc(s_tabT[s], 1)
                act.wait_ge(s_x[s], use.ready32)
                act.wait_ge(s_h[s], use.free32)
                act.wait_ge(s_gr[s], use.free)
                act.activation(xc[:, s, :, 0:F], xin[:, s, :, :], ACT.Copy, scale=env["onep"][0:P, :]).then_inc(s_xc[s], 1)
            act.wait_ge(s_seed, 1)
            each_tile(act, tile)

        @block.vector
        def _(dve):
            for s in range(2):
                dve.memset(xc[:, s, :, F:F + 4], 1.0).then_inc(s_one, 1)
            dve.wait_ge(s_one, 2)

            def tile(t, s, use):
                for digit in range(2):
                    for key in range(2):
                        if digit == 0 and key == 0:
                            dve.wait_ge(s_hist[s], use.free)
                        dve.tensor_scalar(hot[:, s, digit, key, :], env["iota_row"][0:P, :],
                                          env["digit"][:, digit, key, col(t)], None, ALU.is_equal).then_inc(s_hot[s], 1)
                for key in range(2):
                    dve.tensor_copy(keyb[:, s, key, :], keyf[:, key, col(t)].broadcast_to([P, 128])).then_inc(s_keyb[s], 1)
                dve.wait_ge(s_pT[s], use.ready)
                b = use.base(6)
                ch = Chain(dve, s_parts[s], b)
                for key in range(2):
                    ch.step(dve.scalar_tensor_tensor(out=junk[:, s, 0, 0:P], in0=rows[0:P, key, 0:P], scalar=keyf[:, key, col(t)],
                                                     in1=env["before"][0:P, 0:P], op0=ALU.is_equal, op1=ALU.mult,
                                                     accum_out=parts[:, s, key, 0:1]))
                dve.wait_ge(s_look[s], use.ready)
                for key in range(2):
                    ch.step(dve.scalar_tensor_tensor(out=junk[:, s, 1, :], in0=look[:, key, :], scalar=1.0, in1=hot[:, s, 1, key, :],
                                                     op0=ALU.mult, op1=ALU.mult, accum_out=parts[:, s, key, 1:2]))
                dve.wait_ge(s_scat[s], use.free16)
                dve.wait_ge(s_scat2[s], use.free16)
                ch.step(dve.tensor_tensor(place[:, s, :], parts[:, s, :, 0], parts[:, s, :, 1], ALU.add))
                ch.step(dve.tensor_copy(recs[:, s, :], env["rec"][:, col(t), :].rearrange("p o r -> p (o r)")))
                dve.sem_inc(s_place[s], 1)
            each_tile(dve, tile)

        @block.tensor
        def _(pe):
            for key in range(2):
                mm = pe.matmul(tab[:, key, :], env["ident"][:, :], env["base"][:, key, :, :].rearrange("p h n -> p (h n)"),
                               start=True, stop=True)
            mm.then_inc(s_seed, 1)
            for m in range(KH):
                pe.matmul(gram[:, m, 0:F + 1], env["zcol"][:, :], env["zwide"][:, 0:F + 1], start=True, stop=True)

            def tile(t, s, use):
                pe.wait_ge(s_hot[s], use.base(4) + 4)
                pe.wait_ge(s_keyb[s], use.base(2) + 2)
                if isinstance(t, int) or s == 0:
                    pe.wait_ge(s_parts[1], use.base(6))
                    pe.wait_ge(s_tabT[1], use.free)
                else:
                    pe.wait_ge(s_parts[0], use.base(6) + 6)
                    pe.wait_ge(s_tabT[0], use.ready)
                for key in range(2):
                    for half in range(2):
                        pe.transpose(hT[:, key, half, 0:P], hot[:, s, 0, key, 128 * half:128 * half + 128], env["ident_bf"][0:P, 0:P])
                    mm = pe.transpose(rows[:, key, 0:P], keyb[:, s, key, :], env["ident"][0:P, 0:P])
                mm.then_inc(s_pT[s], 1)
                pe.wait_ge(s_tab[s], use.ready)
                for key in range(2):
                    for half in range(2):
                        mm = pe.matmul(tab[:, key, 256 * half:256 * half + 256],
                                       hot[:, s, 0, key, 128 * half:128 * half + 128], hot[:, s, 1, key, :],
                                       start=False, stop=True, skip_group_check=True)
                mm.then_inc(s_hist[s], 1)
                pe.wait_ge(s_xc[s], use.ready)
                for j in range(4):
                    for m in range(KH):
                        mm = pe.matmul(gram[:, m, 0:F + 1], xc[:, s, j, 128 * m:128 * m + 128], xc[:, s, j, 0:F + 1],
                                       start=False, stop=True, skip_group_check=True)
                mm.then_inc(s_gr[s], 1)
                pe.wait_ge(s_tabT[s], use.ready)
                for key in range(2):
                    for half in range(2):
                        mm = pe.matmul(look[:, key, :], hotT[:, s, key, half, :], table[:, s, key, half, :],
                                       start=(half == 0), stop=(half == 1))
                mm.then_inc(s_look[s], 1)
            each_tile(pe, tile)

        @block.gpsimd
        def _(pool):
            rows_of_edges = Rows(ph, pool, E)

            def tile(t, s, use):
                pool.wait_ge(s_place[s], use.ready)
                for key, done in ((0, s_scat), (1, s_scat2)):
                    rows_of_edges.scatter(env["sorted"][key], place[:, s, key:key + 1], recs[:, s, :], done[s])
            each_tile(pool, tile)
            for s in range(2):
                pool.wait_ge(s_scat[s], 16 * (T // 2))
                pool.wait_ge(s_scat2[s], 16 * (T // 2))
    ph.end()


def segments(nc, env):
    ph = Phase(nc, "seg")
    nxt = ph.sb("next", [P, 2, 2])
    lead = ph.sb("lead", [P, T + 1])
    ends = ph.sb("ends", [P, T])
    emit = ph.sb("emit", [P, T + 1])
    tmp = ph.sb("tmp", [P, T + 1])
    first = ph.sb("first", [P, 2, 128])
    rows = ph.ps("rows", [128, 2, 128])
    s_dma, s_v, s_m, s_t, s_n = ph.sem("loads"), ph.sem("steps"), ph.sem("minus"), ph.sem("rows"), ph.sem("first")
    with nc.Block() as block:
        @block.sync
        def _(sp):
            sp.wait_ge(s_m, 1)
            for key in range(2):
                sp.dma_start(env["srec"][key][:, :, :], env["sorted"][key].rearrange("(p t) r -> p t r", p=P)).then_inc(s_dma, 16)
                sp.dma_start(nxt[0:P - 1, key, :], env["sorted"][key].rearrange("(p t) r -> p t r", p=P)[1:P, 0, 0:2]).then_inc(s_dma, 16)

        @block.vector
        def _(dve):
            ch = Chain(dve, s_v)
            dve.memset(nxt[:, :, :], -1.0).then_inc(s_m, 1)
            dve.wait_ge(s_dma, 64)
            for key in range(2):
                r, meta = env["srec"][key], env["meta"][key]
                k = r[:, :, key]
                ch.step(dve.memset(meta["same"][:, 0:1], 0.0))
                ch.step(dve.tensor_tensor(meta["same"][:, 1:T], k[:, 1:T], k[:, 0:T - 1], ALU.is_equal))
                ch.step(dve.tensor_scalar(lead[:, 0:T], k, k[:, 0:1], None, ALU.is_equal))
                ch.step(dve.memset(lead[:, T:T + 1], 0.0))
                ch.step(dve.tensor_tensor(meta["lead_end"][:, :], lead[:, 0:T], lead[:, 1:T + 1], ALU.subtract))
                ch.step(dve.tensor_tensor(ends[:, 0:T - 1], k[:, 0:T - 1], k[:, 1:T], ALU.not_equal))
                ch.step(dve.tensor_tensor(ends[:, T - 1:T], k[:, T - 1:T], nxt[:, key, key:key + 1], ALU.not_equal))
                ch.step(dve.tensor_tensor(tmp[:, 0:T], ends[:, :], lead[:, 0:T], ALU.mult))
                ch.step(dve.tensor_tensor(emit[:, 0:T], ends[:, :], tmp[:, 0:T], ALU.subtract))
                ch.step(dve.tensor_scalar(emit[:, T:T + 1], ends[:, T - 1:T], 1.0, None, ALU.subtract))
                ch.step(dve.tensor_tensor(emit[:, T:T + 1], emit[:, T:T + 1], lead[:, T - 1:T], ALU.mult))
                ch.step(dve.tensor_scalar(emit[:, T:T + 1], emit[:, T:T + 1], 1.0, None, ALU.add))
                ch.step(dve.tensor_copy(meta["emit"][:, :], emit[:, :]))
                ch.step(dve.tensor_copy(meta["node"][:, 0:T], k))
                ch.step(dve.tensor_copy(meta["node"][:, T:T + 1], k[:, 0:1]))
                ch.step(dve.tensor_copy(meta["other"][:, 0:T], r[:, :, 1 - key]))
                ch.step(dve.tensor_scalar(tmp[:, :], emit[:, :], -float(DROP), float(DROP), ALU.mult, ALU.add))
                ch.step(dve.tensor_tensor(tmp[:, 0:T], tmp[:, 0:T], k, ALU.add))
                ch.step(dve.tensor_tensor(tmp[:, T:T + 1], tmp[:, T:T + 1], k[:, 0:1], ALU.add))
                ch.step(dve.tensor_copy(meta["write"][:, :], tmp[:, :]))
                dve.tensor_copy(first[:, key, :], k[:, 0:1].broadcast_to([P, 128])).then_inc(s_n, 1)
            dve.wait_ge(s_t, 1)
            for key in range(2):
                k = env["srec"][key][:, :, key]
                ch.step(dve.scalar_tensor_tensor(out=env["meta"][key]["carry"][:, :], in0=rows[0:P, key, 0:P], scalar=k[:, T - 1:T],
                                                 in1=env["after"][0:P, 0:P], op0=ALU.is_equal, op1=ALU.mult))

        @block.tensor
        def _(pe):
            pe.wait_ge(s_n, 2)
            for key in range(2):
                mm = pe.transpose(rows[:, key, 0:P], first[:, key, :], env["ident"][0:P, 0:P])
            mm.then_inc(s_t, 1)
    ph.end()


def gin_edges(nc, env, d):
    ph = Phase(nc, "gin")
    meta, rec, gram, carry = env["meta"][0], env["srec"][0], env["gram"], env["meta"][0]["carry"]
    gix = ph.sb("gix", [P, 2, 2], I32)
    wix = ph.sb("wix", [P, 2], I32)
    xd, xs = ph.sb("xd", [P, 2, F]), ph.sb("xs", [P, 2, F])
    msg, hs = ph.sb("msg", [P, 2, F]), ph.sb("hs", [P, 2, F])
    acc, lead = ph.sb("acc", [P, 2, F]), ph.sb("lead", [P, F])
    am, both, hrow = ph.sb("am", [P, 2, F]), ph.sb("both", [P, 2, F + 4]), ph.sb("hrow", [P, 2, F])
    cps = ph.ps("carried", [P, 512])
    s_ix, s_wx, s_d, s_s = ph.pair("index"), ph.pair("write_index"), ph.pair("dst_rows"), ph.pair("src_rows")
    s_msg, s_hs, s_v, s_out = ph.pair("message"), ph.pair("scaled"), ph.pair("steps"), ph.pair("rows_ready")
    s_gr, s_sc = ph.pair("gram"), ph.pair("scattered")
    s_init, s_c = ph.sem("init"), ph.sem("carried")
    K = 5

    with nc.Block() as block:
        @block.gpsimd
        def _(pool):
            dram = Rows(ph, pool, N)

            def fetch(t, s, use):
                pool.wait_ge(s_msg[s], use.free)
                pool.wait_ge(s_hs[s], use.free)
                pool.tensor_copy(gix[:, s, 0:1], meta["other"][:, col(t)]).then_inc(s_ix[s], 1)
                pool.tensor_copy(gix[:, s, 1:2], meta["node"][:, col(t)]).then_inc(s_ix[s], 1)
                pool.wait_ge(s_ix[s], use.base(2) + 2)
                dram.gather(xd[:, s, :], d["x"], gix[:, s, 0:1], s_d[s])
                dram.gather(xs[:, s, :], d["x"], gix[:, s, 1:2], s_s[s])

            def write(t, s, use):
                pool.wait_ge(s_out[s], use.ready)
                pool.wait_ge(s_sc[s], use.free16)
                pool.tensor_copy(wix[:, s:s + 1], meta["write"][:, col(t)]).then_inc(s_wx[s], 1)
                pool.wait_ge(s_wx[s], use.ready)
                dram.scatter(env["H"], wix[:, s:s + 1], hrow[:, s, :], s_sc[s])
            two_stages(pool, fetch, write)
            last = Use(pool, T // 2)
            pool.wait_ge(s_hs[0], last.free)
            pool.tensor_copy(gix[:, 0, 1:2], meta["node"][:, T:T + 1]).then_inc(s_ix[0], 1)
            pool.wait_ge(s_ix[0], 2 * last.u + 1)
            dram.gather(xs[:, 0, :], d["x"], gix[:, 0, 1:2], s_s[0])
            write(T, 0, last)
            pool.wait_ge(s_sc[0], 16 * (T // 2 + 1))
            pool.wait_ge(s_sc[1], 16 * (T // 2))

        @block.scalar
        def _(act):
            def scaled(t, s, use):
                act.wait_ge(s_s[s], use.ready16)
                act.wait_ge(s_out[s], use.free)
                act.activation(hs[:, s, :], xs[:, s, :], ACT.Copy, scale=env["onep"][0:P, :]).then_inc(s_hs[s], 1)

            def tile(t, s, use):
                act.wait_ge(s_d[s], use.ready16)
                act.wait_ge(s_v[s], use.base(K))
                act.activation(msg[:, s, :], xd[:, s, :], ACT.Copy, scale=rec[:, col(t), 2]).then_inc(s_msg[s], 1)
                scaled(t, s, use)
            each_tile(act, tile)
            scaled(T, 0, Use(act, T // 2))

        @block.vector
        def _(dve):
            dve.memset(acc[:, 1, :], 0.0).then_inc(s_init, 1)
            dve.memset(lead[:, :], 0.0).then_inc(s_init, 1)
            for s in range(2):
                dve.memset(both[:, s, F:F + 4], 1.0).then_inc(s_init, 1)
            dve.wait_ge(s_init, 4)

            def rows_of(ch, total, t, s, use):
                dve.wait_ge(s_gr[s], use.free)
                ch.step(dve.tensor_scalar(am[:, s, :], total, meta["emit"][:, col(t)], None, ALU.mult))
                dve.wait_ge(s_hs[s], use.ready)
                dve.wait_ge(s_sc[s], use.free16)
                ch.step(dve.tensor_tensor(hrow[:, s, :], total, hs[:, s, :], ALU.add))
                ch.step(dve.tensor_tensor(both[:, s, 0:F], hrow[:, s, :], hs[:, s, :], ALU.add))
                dve.sem_inc(s_out[s], 1)

            def tile(t, s, use):
                ch = Chain(dve, s_v[s], use.base(K))
                dve.wait_ge(s_msg[s], use.ready)
                ch.step(dve.scalar_tensor_tensor(out=acc[:, s, :], in0=acc[:, 1 - s, :], scalar=meta["same"][:, col(t)],
                                                 in1=msg[:, s, :], op0=ALU.mult, op1=ALU.add))
                ch.step(dve.scalar_tensor_tensor(out=lead[:, :], in0=acc[:, s, :], scalar=meta["lead_end"][:, col(t)],
                                                 in1=lead[:, :], op0=ALU.mult, op1=ALU.add))
                rows_of(ch, acc[:, s, :], t, s, use)
            each_tile(dve, tile)
            last = Use(dve, T // 2)
            dve.wait_ge(s_c, 1)
            ch = Chain(dve, s_v[0], K * (T // 2))
            ch.step(dve.tensor_tensor(acc[:, 0, :], cps[:, 0:F], lead[:, :], ALU.add))
            rows_of(ch, acc[:, 0, :], T, 0, last)

        @block.tensor
        def _(pe):
            def tile(t, s, use):
                pe.wait_ge(s_out[s], use.ready)
                for m in range(KH):
                    mm = pe.matmul(gram[:, m, 0:F + 1], am[:, s, 128 * m:128 * m + 128], both[:, s, 0:F + 1],
                                   start=False, stop=True, skip_group_check=True)
                mm.then_inc(s_gr[s], 1)
            each_tile(pe, tile)
            pe.matmul(cps[:, 0:F], carry[:, :], acc[:, 1, :], start=True, stop=True).then_inc(s_c, 1)
            tile(T, 0, Use(pe, T // 2))
    ph.end()


def rsqrt(act, ch, out, tmp, in_):
    ch.step(act.activation(tmp, in_, ACT.Ln))
    ch.step(act.activation(out, tmp, ACT.Exp, scale=-0.5))


def moments(nc, env):
    ph = Phase(nc, "mom")
    g = ph.sb("g", [128, KH, F + 4])
    z = ph.sb("z", [128, KH, F])
    cols = ph.sb("cols", [128, 12, KH])
    zp, cp = ph.ps("zp", [128, KH, 512]), ph.ps("cp", [128, 512])
    s_v, s_z, s_q, s_a, s_w = ph.sem("steps"), ph.sem("z"), ph.sem("sums"), ph.sem("rsqrt"), ph.sem("var")
    s_g = ph.sem("gram")
    w1 = env["w1"]
    with nc.Block() as block:
        @block.vector
        def _(dve):
            ch = Chain(dve, s_v)
            ch.step(dve.tensor_copy(g[:, :, 0:F + 1], env["gram"][:, :, 0:F + 1]))
            dve.sem_inc(s_g, 1)
            dve.wait_ge(s_z, 1)
            ch.step(dve.tensor_tensor(z[:, :, :], zp[:, :, 0:F], w1[:, :, :], ALU.mult))
            dve.sem_inc(s_g, 1)
            dve.wait_ge(s_q, 1)
            ch.step(dve.tensor_scalar(cols[:, 0:2, :], cp[:, 0:4].rearrange("p (a m) -> p a m", a=2), 1.0 / N, None, ALU.mult))
            ch.step(dve.tensor_tensor(cols[:, 2, :], cols[:, 0, :], cols[:, 0, :], ALU.mult))
            ch.step(dve.tensor_tensor(cols[:, 3, :], cols[:, 1, :], cols[:, 2, :], ALU.subtract))
            ch.step(dve.tensor_scalar(cols[:, 3, :], cols[:, 3, :], EPS, None, ALU.add))
            dve.sem_inc(s_w, 1)
            dve.wait_ge(s_a, 2)
            scale_shift(dve, ch, env, cols, 0)

        @block.scalar
        def _(act):
            ch = Chain(act, s_a)
            act.wait_ge(s_w, 1)
            rsqrt(act, ch, cols[:, 5, :], cols[:, 4, :], cols[:, 3, :])

        @block.tensor
        def _(pe):
            pe.wait_ge(s_g, 1)
            for m in range(KH):
                for k in range(KH):
                    mm = pe.matmul(zp[:, m, 0:F], g[:, k, 128 * m:128 * m + 128], w1[:, k, :], start=(k == 0), stop=(k == 1))
            mm.then_inc(s_z, 1)
            pe.wait_ge(s_g, 2)
            for m in range(KH):
                for k in range(KH):
                    pe.matmul(cp[:, m:m + 1], w1[:, k, 128 * m:128 * m + 128], g[:, k, F:F + 1], start=(k == 0), stop=(k == 1))
                for k in range(KH):
                    mm = pe.matmul(cp[:, 2 + m:3 + m], z[:, k, 128 * m:128 * m + 128], env["ones"][:, 0:1],
                                   start=(k == 0), stop=(k == 1))
            mm.then_inc(s_q, 1)
    ph.end()


def scale_shift(dve, ch, env, cols, layer):
    bn, out = env["bn"], env["affine"]
    b, gamma, beta = bn[:, 3 * layer, :], bn[:, 3 * layer + 1, :], bn[:, 3 * layer + 2, :]
    ch.step(dve.tensor_tensor(out[:, 2 * layer, :], cols[:, 5, :], gamma, ALU.mult))
    ch.step(dve.tensor_tensor(cols[:, 6, :], cols[:, 0, :], b, ALU.add))
    ch.step(dve.tensor_tensor(cols[:, 7, :], b, cols[:, 6, :], ALU.subtract))
    ch.step(dve.tensor_tensor(cols[:, 8, :], cols[:, 7, :], out[:, 2 * layer, :], ALU.mult))
    ch.step(dve.tensor_tensor(out[:, 2 * layer + 1, :], cols[:, 8, :], beta, ALU.add))


def mlp(nc, env):
    ph = Phase(nc, "mlp")
    h = ph.sb("h", [P, 2, 4, F])
    hT = ph.sb("hT", [128, 2, KH, CH])
    r = ph.sb("r", [128, 2, KH, CH])
    y = ph.sb("y", [128, 2, KH, CH])
    stats = ph.sb("stats", [128, KH, NCH, 6])
    mv = ph.sb("mv", [128, KH, 2])
    cols = ph.sb("cols", [128, 12, KH])
    tp, y1, y2 = ph.ps("tp", [128, 2, KH, 512]), ph.ps("y1", [128, KH, 512]), ph.ps("y2", [128, KH, 512])
    s_h, s_t, s_hT, s_1, s_r, s_2 = (ph.pair(n) for n in ("h", "transposed", "hT", "y1", "r", "y2"))
    s_y, s_st, s_o = ph.pair("y2_copied"), ph.pair("stats"), ph.pair("y2_stored")
    s_v, s_a, s_w = ph.sem("steps"), ph.sem("rsqrt"), ph.sem("var")
    w1, w2, aff = env["w1"], env["w2"], env["affine"]
    h_v = env["H"].rearrange("(c p j) f -> c p j f", p=P, j=4)

    with nc.Block() as block:
        @block.sync
        def _(sp):
            def load(t, s, use):
                sp.wait_ge(s_t[s], use.free)
                for a, n in CUTS:
                    sp.dma_start(h[a:a + n, s, :, :], h_v[bass.ds(t, 1), a:a + n, :, :].rearrange("o p j f -> (o p) j f")).then_inc(s_h[s], 16)

            def store(t, s, use):
                sp.wait_ge(s_y[s], use.base(2) + 2)
                sp.dma_start(env["Y2"][bass.ds(t, 1), :, :].rearrange("o p n -> (o p) n"),
                             y[:, s, :, :].rearrange("p k n -> p (k n)")).then_inc(s_o[s], 16)
            two_stages(sp, load, store, NCH)
            for s in range(2):
                sp.wait_ge(s_o[s], 16 * (NCH // 2))

        @block.tensor
        def _(pe):
            def front(t, s, use):
                pe.wait_ge(s_h[s], use.ready32)
                pe.wait_ge(s_hT[s], use.base(2))
                for k in range(KH):
                    for j in range(4):
                        mm = pe.transpose(tp[:, s, k, P * j:P * j + P], h[:, s, j, 128 * k:128 * k + 128], env["ident"][0:P, 0:P])
                mm.then_inc(s_t[s], 1)

            def back(t, s, use):
                pe.wait_ge(s_hT[s], use.base(2) + 2)
                if s == 0:
                    pe.wait_ge(s_r[1], use.base(2))
                else:
                    pe.wait_ge(s_r[0], use.base(2) + 2)
                for m in range(KH):
                    for k in range(KH):
                        mm = pe.matmul(y1[:, m, 0:CH], w1[:, k, 128 * m:128 * m + 128], hT[:, s, k, :],
                                       start=(k == 0), stop=(k == 1))
                    mm.then_inc(s_1[s], 1)
                if s == 0:
                    pe.wait_ge(s_y[1], use.base(2))
                else:
                    pe.wait_ge(s_y[0], use.base(2) + 2)
                for k in range(KH):
                    pe.wait_ge(s_r[s], use.base(2) + k + 1)
                    for m in range(KH):
                        mm = pe.matmul(y2[:, m, 0:CH], w2[:, k, 128 * m:128 * m + 128], r[:, s, k, :],
                                       start=(k == 0), stop=(k == 1), skip_group_check=True)
                mm.then_inc(s_2[s], 1)
            two_stages(pe, front, back, NCH)

        @block.scalar
        def _(act):
            def tile(t, s, use):
                for m in range(KH):
                    act.wait_ge(s_1[s], use.base(2) + m + 1)
                    act.wait_ge(s_2[s], use.free)
                    act.activation(r[:, s, m, :], y1[:, m, 0:CH], ACT.Relu, bias=aff[:, 1, m:m + 1],
                                   scale=aff[:, 0, m:m + 1]).then_inc(s_r[s], 1)
                act.wait_ge(s_2[s], use.ready)
                act.wait_ge(s_o[s], use.free16)
                act.wait_ge(s_st[s], use.base(2))
                for m in range(KH):
                    act.copy(y[:, s, m, :], y2[:, m, 0:CH]).then_inc(s_y[s], 1)
            each_tile(act, tile, NCH)
            ch = Chain(act, s_a)
            act.wait_ge(s_w, 1)
            rsqrt(act, ch, cols[:, 5, :], cols[:, 4, :], cols[:, 3, :])

        @block.vector
        def _(dve):
            def copies(t, s, use):
                dve.wait_ge(s_t[s], use.ready)
                dve.wait_ge(s_2[s], use.free)
                for k in range(KH):
                    dve.tensor_copy(hT[:, s, k, :], tp[:, s, k, 0:CH]).then_inc(s_hT[s], 1)

            def stat(t, s, use):
                for m in range(KH):
                    dve.wait_ge(s_y[s], use.base(2) + m + 1)
                    dve.bn_stats(stats[:, m, col(t), :].rearrange("p o n -> p (o n)"), y[:, s, m, :]).then_inc(s_st[s], 1)
            two_stages(dve, copies, stat, NCH)
            ch = Chain(dve, s_v)
            for s in range(2):
                dve.wait_ge(s_st[s], NCH)
            for m in range(KH):
                ch.step(dve.bn_aggr(mv[:, m, :], stats[:, m, :, :].rearrange("p c n -> p (c n)")))
            ch.step(dve.tensor_copy(cols[:, 0, :], mv[:, :, 0]))
            ch.step(dve.tensor_scalar(cols[:, 3, :], mv[:, :, 1], EPS, None, ALU.add))
            dve.sem_inc(s_w, 1)
            dve.wait_ge(s_a, 2)
            scale_shift(dve, ch, env, cols, 1)
    ph.end()


def nodes(nc, env, d):
    ph = Phase(nc, "nodes")
    y, z = ph.sb("y", [128, 2, KH, CH]), ph.sb("z", [128, 2, KH, CH])
    x, u = ph.sb("x", [P, 2, 4, F]), ph.sb("u", [P, 2, 4, F])
    x1, x2, x3 = (ph.sb(n, [P, 2, 4, F]) for n in ("x1", "x2", "x3"))
    x3T, ex = ph.sb("x3T", [128, 2, KH, CH]), ph.sb("exp", [P, 2, 4, F])
    el, v, out = ph.sb("elu", [P, 2, 4, F]), ph.sb("v", [P, 2, 4, F]), ph.sb("out", [P, 2, 4, F])
    st, mv = ph.sb("stats", [P, 2, 4, 6]), ph.sb("mv", [P, 2, 4, 2])
    q, r, nm = ph.sb("q", [P, 2, 3, 4]), ph.sb("r", [P, 2, 3, 4]), ph.sb("nm", [P, 2, 3, 4])
    lnq = ph.sb("lnq", [P, 2, 3, 4])
    st2, mv2 = ph.sb("stats2", [P, 2, 4, 6]), ph.sb("mv2", [P, 2, 4, 2])
    q2, r2, lnq2 = ph.sb("q2", [P, 2, 4]), ph.sb("r2", [P, 2, 4]), ph.sb("lnq2", [P, 2, 4])
    zp, tp, xp = ph.ps("zp", [P, 4, F]), ph.ps("tp", [128, KH, 512]), ph.ps("xp", [P, 4, F])
    names = ("y", "x", "z", "zp", "u", "q", "r", "nm", "x1", "x2", "x3", "x3T", "x3T_copied", "xp", "exp", "elu", "v", "q2", "r2", "out")
    s_y, s_x, s_z, s_zp, s_u, s_q, s_r, s_nm, s_x1, s_x2, s_x3, s_t3, s_c3, s_xp, s_ex, s_el, s_v, s_q2, s_r2, s_out = (
        ph.pair(n) for n in names)
    o_1, o_2, o_o = ph.pair("x1_stored"), ph.pair("x2_stored"), ph.pair("out_stored")
    c_a, c_b, c_ra, c_rb = ph.pair("steps_a"), ph.pair("steps_b"), ph.pair("rsqrt_a"), ph.pair("rsqrt_b")
    s_hold, s_hold_p = ph.sem("hold"), ph.sem("hold_pool")
    aff, w_self = env["affine"], env["w_self"]
    x_v, x1_v, x2_v, out_v = (a.rearrange("(c p j) f -> c p j f", p=P, j=4) for a in (d["x"], env["X1"], env["X2"], d["out"]))

    with nc.Block() as block:
        @block.sync
        def _(sp):
            def put(dst, t, src, s, sem):
                for a, n in CUTS:
                    sp.dma_start(dst[bass.ds(t, 1), a:a + n, :, :].rearrange("o p j f -> (o p) j f"), src[a:a + n, s, :, :]).then_inc(sem[s], 16)

            def load(t, s, use):
                sp.wait_ge(s_z[s], use.base(2))
                sp.dma_start(y[:, s, :, :].rearrange("p k n -> p (k n)"),
                             env["Y2"][bass.ds(t, 1), :, :].rearrange("o p n -> (o p) n")).then_inc(s_y[s], 16)
                sp.wait_ge(s_u[s], use.free)
                for a, n in CUTS:
                    sp.dma_start(x[a:a + n, s, :, :], x_v[bass.ds(t, 1), a:a + n, :, :].rearrange("o p j f -> (o p) j f")).then_inc(s_x[s], 16)

            def store(t, s, use):
                sp.wait_ge(s_x1[s], use.base(4) + 4)
                put(x1_v, t, x1, s, o_1)
                sp.wait_ge(s_x2[s], use.base(4) + 4)
                put(x2_v, t, x2, s, o_2)

            def store_out(t, s, use):
                sp.wait_ge(s_out[s], use.base(4) + 4)
                put(out_v, t, out, s, o_o)
            stages(sp, [load, store, store_out], NCH)
            for sem in (o_1, o_2, o_o):
                for s in range(2):
                    sp.wait_ge(sem[s], 32 * (NCH // 2))

        @block.scalar
        def _(act):
            def first(t, s, use):
                act.wait_ge(s_y[s], use.ready16)
                act.wait_ge(s_zp[s], use.free)
                for m in range(KH):
                    act.activation(z[:, s, m, :], y[:, s, m, :], ACT.Relu, bias=aff[:, 3, m:m + 1],
                                   scale=aff[:, 2, m:m + 1]).then_inc(s_z[s], 1)
                act.wait_ge(s_q[s], use.ready)
                act.wait_ge(s_x1[s], use.base(4))
                act.wait_ge(s_x2[s], use.base(4))
                act.wait_ge(s_nm[s], use.free)
                ch = Chain(act, c_ra[s], use.base(2))
                rsqrt(act, ch, r[:, s, :, :], lnq[:, s, :, :], q[:, s, :, :])
                act.sem_inc(s_r[s], 1)
                act.wait_ge(s_nm[s], use.ready)
                act.wait_ge(s_t3[s], use.free)
                act.wait_ge(s_v[s], use.free)
                for j in range(4):
                    act.activation(x3[:, s, j, :], u[:, s, j, :], ACT.Identity, bias=nm[:, s, 2, j:j + 1],
                                   scale=r[:, s, 2, j:j + 1]).then_inc(s_x3[s], 1)

            def second(t, s, use):
                act.wait_ge(s_t3[s], use.ready)
                act.wait_ge(s_xp[s], use.free)
                for k in range(KH):
                    act.copy(x3T[:, s, k, :], tp[:, k, 0:CH]).then_inc(s_c3[s], 1)
                act.wait_ge(s_xp[s], use.ready)
                act.wait_ge(s_el[s], use.free)
                act.activation(ex[:, s, :, :], xp[:, :, :], ACT.Exp, bias=env["minus1"][0:P, :]).then_inc(s_ex[s], 1)
                act.wait_ge(s_q2[s], use.ready)
                act.wait_ge(s_out[s], use.base(4))
                ch = Chain(act, c_rb[s], use.base(2))
                rsqrt(act, ch, r2[:, s, :], lnq2[:, s, :], q2[:, s, :])
                act.sem_inc(s_r2[s], 1)
            two_stages(act, first, second, NCH)

        @block.vector
        def _(dve):
            def first(t, s, use):
                ch = Chain(dve, c_a[s], use.base(13))
                dve.wait_ge(s_zp[s], use.ready)
                dve.wait_ge(s_x[s], use.ready32)
                dve.wait_ge(s_x1[s], use.base(4))
                dve.wait_ge(s_x2[s], use.base(4))
                dve.wait_ge(s_x3[s], use.base(4))
                ch.step(dve.tensor_tensor(u[:, s, :, :], zp[:, :, :], x[:, s, :, :], ALU.add))
                dve.sem_inc(s_u[s], 1)
                for j in range(4):
                    ch.step(dve.bn_stats(st[:, s, j, :], u[:, s, j, :]))
                for j in range(4):
                    dve.sem_inc(s_hold, 1)
                    ch.step(dve.bn_aggr(mv[:, s, j, :], st[:, s, j, :]))
                dve.wait_ge(s_r[s], use.free)
                for k, (a, b) in enumerate(((1.0, EPS), (1.0 + EPS, EPS * EPS), (1.0 + EPS + EPS * EPS, EPS ** 3))):
                    ch.step(dve.tensor_scalar(q[:, s, k, :], mv[:, s, :, 1], a, b, ALU.mult, ALU.add))
                dve.sem_inc(s_q[s], 1)
                dve.wait_ge(s_r[s], use.ready)
                ch.step(dve.scalar_tensor_tensor(out=nm[:, s, :, :], in0=r[:, s, :, :], scalar=-1.0,
                                                 in1=mv[:, s, :, 0].unsqueeze(1).broadcast_to([P, 3, 4]), op0=ALU.mult, op1=ALU.mult))
                dve.sem_inc(s_nm[s], 1)

            def second(t, s, use):
                ch = Chain(dve, c_b[s], use.base(10))
                dve.wait_ge(s_ex[s], use.ready)
                dve.wait_ge(s_v[s], use.free)
                ch.step(dve.scalar_tensor_tensor(out=el[:, s, :, :].rearrange("p j f -> p (j f)"), in0=ex[:, s, :, :].rearrange("p j f -> p (j f)"), scalar=1.0,
                                                 in1=xp[:, :, :].rearrange("p j f -> p (j f)"), op0=ALU.min, op1=ALU.max))
                dve.sem_inc(s_el[s], 1)
                dve.wait_ge(s_v[s], use.ready)
                for j in range(4):
                    ch.step(dve.bn_stats(st2[:, s, j, :], v[:, s, j, :]))
                for j in range(4):
                    dve.sem_inc(s_hold, 1)
                    ch.step(dve.bn_aggr(mv2[:, s, j, :], st2[:, s, j, :]))
                dve.wait_ge(s_r2[s], use.free)
                ch.step(dve.tensor_scalar(q2[:, s, :], mv2[:, s, :, 1], EPS, None, ALU.add))
                dve.sem_inc(s_q2[s], 1)
                dve.wait_ge(s_r2[s], use.ready)
                dve.wait_ge(o_o[s], use.free32)
                for j in range(4):
                    dve.tensor_scalar(out[:, s, j, :], v[:, s, j, :], mv2[:, s, j, 0:1], r2[:, s, j:j + 1],
                                      ALU.subtract, ALU.mult).then_inc(s_out[s], 1)
            two_stages(dve, first, second, NCH)

        @block.gpsimd
        def _(pool):
            def first(t, s, use):
                pool.wait_ge(s_nm[s], use.ready)
                for k, (dst, done, stored) in enumerate(((x1, s_x1, o_1), (x2, s_x2, o_2))):
                    pool.wait_ge(stored[s], use.free32)
                    pool.sem_inc(s_hold_p, 1)
                    for j in range(4):
                        pool.tensor_scalar(dst[:, s, j, :], u[:, s, j, :], r[:, s, k, j:j + 1], nm[:, s, k, j:j + 1],
                                           ALU.mult, ALU.add).then_inc(done[s], 1)

            def second(t, s, use):
                pool.wait_ge(s_el[s], use.ready)
                pool.wait_ge(s_x3[s], use.base(4) + 4)
                pool.wait_ge(s_out[s], use.base(4))
                pool.tensor_tensor(v[:, s, :, :], el[:, s, :, :], x3[:, s, :, :], ALU.add).then_inc(s_v[s], 1)
            two_stages(pool, first, second, NCH)

        @block.tensor
        def _(pe):
            def first(t, s, use):
                pe.wait_ge(s_z[s], use.base(2) + 2)
                pe.wait_ge(s_u[1 - s], use.free if s == 0 else use.ready)
                for j in range(4):
                    for k in range(KH):
                        mm = pe.transpose(zp[:, j, 128 * k:128 * k + 128], z[:, s, k, P * j:P * j + P], env["ident"][:, :])
                mm.then_inc(s_zp[s], 1)

            def second(t, s, use):
                pe.wait_ge(s_x3[s], use.base(4) + 4)
                pe.wait_ge(s_c3[1 - s], use.base(2) if s == 0 else use.base(2) + 2)
                for k in range(KH):
                    for j in range(4):
                        mm = pe.transpose(tp[:, k, P * j:P * j + P], x3[:, s, j, 128 * k:128 * k + 128], env["ident"][0:P, 0:P])
                mm.then_inc(s_t3[s], 1)
                pe.wait_ge(s_c3[s], use.base(2) + 2)
                pe.wait_ge(s_el[1 - s], use.free if s == 0 else use.ready)
                for j in range(4):
                    for k in range(KH):
                        pe.matmul(xp[:, j, :], x3T[:, s, k, P * j:P * j + P], w_self[:, k, 0:F], start=(k == 0), stop=False)
                    mm = pe.matmul(xp[:, j, :], env["ones"][0:1, 0:P], env["bias_row"][0:1, :], start=False, stop=True)
                mm.then_inc(s_xp[s], 1)
            two_stages(pe, first, second, NCH)
    ph.end()


class At:

    def __init__(self, turn, unroll, a):
        self.turn, self.unroll, self.a = turn, unroll, a

    def count(self, per=1, plus=0):
        if isinstance(self.turn, int):
            return per * (self.turn * self.unroll + self.a) + plus
        return self.turn * (per * self.unroll) + (per * self.a + plus)

    def slot(self, ring):
        return self.a % ring

    def uses(self, ring, per=1, plus=0):
        if isinstance(self.turn, int):
            return per * ((self.turn * self.unroll + self.a) // ring) + plus
        return self.turn * (per * self.unroll // ring) + (per * (self.a // ring) + plus)

    @property
    def col(self):
        return bass.ds(self.count(), 1)

    @property
    def is_lead(self):
        return isinstance(self.turn, int) and self.turn * self.unroll + self.a == T


def wait(eng, sem, value):
    if not (isinstance(value, int) and value <= 0):
        eng.wait_ge(sem, value)


RING = 4


def run_stages(eng, steps, total, tiles=100, unroll=RING, behind=4):
    most = max(lag for lag, _ in steps)
    head = unroll * -(-(most + behind) // unroll)
    for t in range(head):
        for lag, step in steps:
            if 0 <= t - lag < total:
                step(At(0, unroll, t - lag))
    with eng.Fori(head // unroll, tiles // unroll) as turn:
        for a in range(unroll):
            for lag, step in steps:
                step(At(turn, unroll, a - lag))
    for t in range(tiles, total + most):
        for lag, step in steps:
            if 0 <= t - lag < total:
                step(At(0, unroll, t - lag))


def gat_edges(nc, env, d):
    ph = Phase(nc, "gat")
    meta, carry = env["meta"][0], env["meta"][0]["carry"]
    w, ws, w_self = env["w_gat"], env["w_gat_s"], env["w_self"]
    HW = F + 2 * H1
    gix, wix = ph.sb("gix", [P, RING, 2], I32), ph.sb("wix", [P, RING], I32)
    xd, xs = ph.sb("xd", [P, RING, F]), ph.sb("xs", [P, RING, F])
    xT = ph.sb("xT", [128, RING, 4, P])
    low, hg, msg = ph.sb("low", [P, RING, HW]), ph.sb("hg", [P, RING, HW]), ph.sb("msg", [P, RING, F + H1])
    sc = ph.sb("scores", [P, RING, 4, H1])
    acc, lead = ph.sb("acc", [P, RING, F + H1]), ph.sb("lead", [P, F + H1])
    den, rr = ph.sb("den", [P, RING, H1]), ph.sb("rr", [P, RING, H1])
    hn, g, e1, e2 = (ph.sb(n, [P, RING, F]) for n in ("hn", "g", "e1", "e2"))
    elu, u, x2, x3 = (ph.sb(n, [P, RING, F]) for n in ("elu", "u", "x2", "x3"))
    st, mv, q, lnq, r, nm = (ph.sb(n, [P, RING, k]) for n, k in (("st", 6), ("mv", 2), ("q", 2), ("lnq", 2), ("r", 2), ("nm", 2)))
    x3T = ph.sb("x3T", [128, RING, KH, P])
    t1, ex, el, v, out = (ph.sb(n, [P, RING, F]) for n in ("t1", "ex", "el", "v", "out"))
    neg = ph.sb("neg", [P, RING, 1])
    st3, mv3, q3, lnq3, r3, nm3 = (ph.sb(n, [P, RING, k]) for n, k in (("st3", 6), ("mv3", 2), ("q3", 1), ("lnq3", 1), ("r3", 1), ("nm3", 1)))
    tp, hp = ph.ps("tp", [128, 2, 4, 128]), ph.ps("hp", [P, 2, 512])
    tp3, xp, cps = ph.ps("tp3", [128, 4, 128]), ph.ps("xp", [P, 2, 512]), ph.ps("cps", [P, 512])
    s_d, s_s = [ph.sem(f"dst_rows{k}") for k in range(RING)], [ph.sem(f"src_rows{k}") for k in range(RING)]
    s_w2, s_w3, s_wo = ([ph.sem(f"{n}{k}") for k in range(RING)] for n in ("x2_stored", "x3_stored", "out_stored"))
    names = ("index", "windex", "transposed", "xT", "projected", "scored", "weights", "msgs", "normed", "exp1", "exp2",
             "u", "q", "r", "x3", "x2", "x3_transposed", "x3T", "xp", "exp3", "t1", "v", "q3", "out")
    (s_ix, s_wx, s_t, s_xT, s_hp, s_sc, s_e4, s_msg, s_g, s_e1, s_e2, s_u, s_q, s_r, s_x3, s_x2, s_t3, s_x3T, s_xp,
     s_ex, s_t1, s_v, s_q3, s_out) = (ph.sem(n) for n in names)
    c1, c2, c3, c4, c5, ca, cb = (ph.sem(f"steps{k}") for k in range(7))
    s_init, s_c, s_hold = ph.sem("init"), ph.sem("carried"), ph.sem("hold")

    with nc.Block() as block:
        @block.gpsimd
        def _(pool):
            dram = Rows(ph, pool, N)

            def fetch(at):
                s = at.slot(RING)
                wait(pool, s_t, at.count(1, 1 - RING))
                wait(pool, s_u, at.count(1, 1 - RING))
                pool.tensor_copy(gix[:, s, 1:2], meta["node"][:, at.col]).then_inc(s_ix, 1)
                if at.is_lead:
                    pool.wait_ge(s_ix, 2 * T + 1)
                    dram.gather(xs[:, s, :], env["X1"], gix[:, s, 1:2], s_s[s])
                    return
                pool.tensor_copy(gix[:, s, 0:1], meta["other"][:, at.col]).then_inc(s_ix, 1)
                pool.wait_ge(s_ix, at.count(2, 2))
                dram.gather(xd[:, s, :], env["X1"], gix[:, s, 0:1], s_d[s])
                dram.gather(xs[:, s, :], env["X1"], gix[:, s, 1:2], s_s[s])

            def put_x(at):
                s = at.slot(RING)
                wait(pool, s_wo[s], at.uses(RING, 16))
                pool.tensor_copy(wix[:, s:s + 1], meta["write"][:, at.col]).then_inc(s_wx, 1)
                pool.wait_ge(s_wx, at.count(1, 1))
                pool.wait_ge(s_x2, at.count(1, 1))
                dram.scatter(env["X2"], wix[:, s:s + 1], x2[:, s, :], s_w2[s])
                pool.wait_ge(s_x3, at.count(1, 1))
                dram.scatter(env["X3"], wix[:, s:s + 1], x3[:, s, :], s_w3[s])

            def put_out(at):
                s = at.slot(RING)
                pool.wait_ge(s_out, at.count(1, 1))
                dram.scatter(d["out"], wix[:, s:s + 1], out[:, s, :], s_wo[s])
            run_stages(pool, [(8, put_out), (5, put_x), (0, fetch)], T + 1)
            for s in range(RING):
                for sem in (s_w2, s_w3, s_wo):
                    pool.wait_ge(sem[s], 16 * (T // RING + (s == 0)))

        @block.tensor
        def _(pe):
            def turn_rows(at):
                if at.is_lead:
                    return
                s, b = at.slot(RING), at.slot(2)
                pe.wait_ge(s_d[s], at.uses(RING, 16, 16))
                pe.wait_ge(s_s[s], at.uses(RING, 16, 16))
                wait(pe, s_xT, at.count(1, -1))
                for k in range(KH):
                    pe.transpose(tp[:, b, k, 0:P], xd[:, s, 128 * k:128 * k + 128], env["ident"][0:P, 0:P])
                for k in range(KH):
                    mm = pe.transpose(tp[:, b, 2 + k, 0:P], xs[:, s, 128 * k:128 * k + 128], env["ident"][0:P, 0:P])
                mm.then_inc(s_t, 1)

            def project(at):
                s, b = at.slot(RING), at.slot(2)
                if at.is_lead:
                    pe.wait_ge(s_msg, T)
                    pe.matmul(cps[:, 0:F + H1], carry[:, :], acc[:, (T - 1) % RING, :], start=True, stop=True).then_inc(s_c, 1)
                    return
                pe.wait_ge(s_xT, at.count(1, 1))
                wait(pe, s_sc, at.count(1, -1))
                for k in range(KH):
                    pe.matmul(hp[:, b, 0:F + H1], xT[:, s, k, :], w[:, k, :], start=(k == 0), stop=(k == 1))
                for k in range(KH):
                    mm = pe.matmul(hp[:, b, F + H1:HW], xT[:, s, 2 + k, :], ws[:, k, :], start=(k == 0), stop=(k == 1),
                                   skip_group_check=True)
                mm.then_inc(s_hp, 1)

            def turn_x3(at):
                s, b = at.slot(RING), at.slot(2)
                pe.wait_ge(s_x3, at.count(1, 1))
                wait(pe, s_x3T, at.count(1, 0))
                for k in range(KH):
                    mm = pe.transpose(tp3[:, k, 0:P], x3[:, s, 128 * k:128 * k + 128], env["ident"][0:P, 0:P])
                mm.then_inc(s_t3, 1)

            def product(at):
                s, b = at.slot(RING), at.slot(2)
                pe.wait_ge(s_x3T, at.count(1, 1))
                wait(pe, s_t1, at.count(1, -1))
                for k in range(KH):
                    mm = pe.matmul(xp[:, b, 0:F], x3T[:, s, k, :], w_self[:, k, 0:F], start=(k == 0), stop=(k == 1))
                mm.then_inc(s_xp, 1)
            run_stages(pe, [(7, product), (6, turn_x3), (1, project), (0, turn_rows)], T + 1)

        @block.scalar
        def _(act):
            def copy_rows(at):
                if at.is_lead:
                    return
                s, b = at.slot(RING), at.slot(2)
                act.wait_ge(s_t, at.count(1, 1))
                wait(act, s_hp, at.count(1, 1 - RING))
                act.copy(xT[:, s, :, :], tp[:, b, :, 0:P]).then_inc(s_xT, 1)

            def weights(at):
                if at.is_lead:
                    return
                s = at.slot(RING)
                act.wait_ge(s_sc, at.count(1, 1))
                wait(act, s_msg, at.count(1, 1 - RING))
                act.activation(sc[:, s, 2, :], sc[:, s, 1, :], ACT.Exp, scale=-1.0).then_inc(s_e4, 1)

            def elus(at):
                s = at.slot(RING)
                act.wait_ge(s_g, at.count(1, 1))
                wait(act, s_u, at.count(1, 1 - RING))
                act.activation(e1[:, s, :], g[:, s, :], ACT.Exp).then_inc(s_e1, 1)
                act.wait_ge(s_e1, at.count(1, 1))
                act.activation(e2[:, s, :], e1[:, s, :], ACT.Exp, bias=env["minus1"][0:P, :]).then_inc(s_e2, 1)

            def norm2(at):
                s = at.slot(RING)
                act.wait_ge(s_q, at.count(1, 1))
                wait(act, s_x2, at.count(1, 1 - RING))
                wait(act, s_x3, at.count(1, 1 - RING))
                ch = Chain(act, ca, at.count(2))
                rsqrt(act, ch, r[:, s, :], lnq[:, s, :], q[:, s, :])
                act.sem_inc(s_r, 1)

            def copy_x3(at):
                s = at.slot(RING)
                act.wait_ge(s_t3, at.count(1, 1))
                wait(act, s_xp, at.count(1, 1 - RING))
                act.copy(x3T[:, s, :, :], tp3[:, 0:KH, 0:P]).then_inc(s_x3T, 1)

            def exps(at):
                s, b = at.slot(RING), at.slot(2)
                act.wait_ge(s_t1, at.count(1, 1))
                wait(act, s_v, at.count(1, 1 - RING))
                act.activation(ex[:, s, :], t1[:, s, :], ACT.Exp, bias=env["minus1"][0:P, :]).then_inc(s_ex, 1)

            def norm_out(at):
                s = at.slot(RING)
                act.wait_ge(s_q3, at.count(1, 1))
                ch = Chain(act, cb, at.count(3))
                rsqrt(act, ch, r3[:, s, :], lnq3[:, s, :], q3[:, s, :])
                ch.step(act.activation(nm3[:, s, :], neg[:, s, :], ACT.Copy, scale=r3[:, s, :]))
                wait(act, s_wo[s], at.uses(RING, 16))
                act.activation(out[:, s, :], v[:, s, :], ACT.Identity, bias=nm3[:, s, :], scale=r3[:, s, :]).then_inc(s_out, 1)
            run_stages(act, [(8, norm_out), (7, exps), (6, copy_x3), (4, norm2), (3, elus), (1, weights), (0, copy_rows)], T + 1)

        @block.vector
        def _(dve):
            dve.memset(acc[:, RING - 1, :], 0.0).then_inc(s_init, 1)
            dve.memset(lead[:, :], 0.0).then_inc(s_init, 1)
            dve.wait_ge(s_init, 2)

            def score(at):
                if at.is_lead:
                    return
                s, b = at.slot(RING), at.slot(2)
                ch = Chain(dve, c1, at.count(4))
                dve.wait_ge(s_hp, at.count(1, 1))
                ch.step(dve.tensor_scalar(low[:, s, :], hp[:, b, 0:HW], 0.0, None, ALU.min))
                ch.step(dve.scalar_tensor_tensor(out=hg[:, s, :], in0=hp[:, b, 0:HW], scalar=0.0, in1=low[:, s, :],
                                                 op0=ALU.max, op1=ALU.add))
                ch.step(dve.tensor_tensor(sc[:, s, 0, :], hg[:, s, F:F + H1], hg[:, s, F + H1:HW], ALU.add))
                ch.step(dve.scalar_tensor_tensor(out=sc[:, s, 1, :], in0=sc[:, s, 0, :], scalar=ALPHA, in1=sc[:, s, 0, :],
                                                 op0=ALU.mult, op1=ALU.max))
                dve.sem_inc(s_sc, 1)

            def sums(at):
                s = at.slot(RING)
                ch = Chain(dve, c2, at.count(4))
                if at.is_lead:
                    dve.wait_ge(s_c, 1)
                    ch.step(dve.tensor_tensor(acc[:, s, :], cps[:, 0:F + H1], lead[:, :], ALU.add))
                else:
                    dve.wait_ge(s_e4, at.count(1, 1))
                    ch.step(dve.tensor_scalar(msg[:, s, F:F + H1], sc[:, s, 2, :], 0.0, None, ALU.max))
                    ch.step(dve.tensor_tensor(msg[:, s, 0:F].rearrange("p (h c) -> p h c", h=H1),
                                              hg[:, s, 0:F].rearrange("p (h c) -> p h c", h=H1),
                                              msg[:, s, F:F + H1].unsqueeze(2).broadcast_to([P, H1, C1]), ALU.mult))
                    ch.step(dve.scalar_tensor_tensor(out=acc[:, s, :], in0=acc[:, (s - 1) % RING, :], scalar=meta["same"][:, at.col],
                                                     in1=msg[:, s, :], op0=ALU.mult, op1=ALU.add))
                    ch.step(dve.scalar_tensor_tensor(out=lead[:, :], in0=acc[:, s, :], scalar=meta["lead_end"][:, at.col],
                                                     in1=lead[:, :], op0=ALU.mult, op1=ALU.add))
                dve.sem_inc(s_msg, 1)
                ch = Chain(dve, c3, at.count(4))
                wait(dve, s_e1, at.count(1, 1 - RING))
                ch.step(dve.tensor_scalar(den[:, s, :], acc[:, s, F:F + H1], TINY, None, ALU.max))
                ch.step(dve.reciprocal(rr[:, s, :], den[:, s, :]))
                ch.step(dve.tensor_tensor(hn[:, s, :].rearrange("p (h c) -> p h c", h=H1),
                                          acc[:, s, 0:F].rearrange("p (h c) -> p h c", h=H1),
                                          rr[:, s, :].unsqueeze(2).broadcast_to([P, H1, C1]), ALU.mult))
                ch.step(dve.tensor_scalar(g[:, s, :], hn[:, s, :], 0.0, None, ALU.min))
                dve.sem_inc(s_g, 1)

            def residual(at):
                s = at.slot(RING)
                ch = Chain(dve, c4, at.count(6))
                dve.wait_ge(s_e2, at.count(1, 1))
                dve.wait_ge(s_s[s], at.uses(RING, 16, 16))
                ch.step(dve.scalar_tensor_tensor(out=elu[:, s, :], in0=hn[:, s, :], scalar=0.0, in1=e2[:, s, :],
                                                 op0=ALU.max, op1=ALU.add))
                wait(dve, s_x2, at.count(1, 1 - RING))
                wait(dve, s_x3, at.count(1, 1 - RING))
                ch.step(dve.scalar_tensor_tensor(out=u[:, s, :], in0=elu[:, s, :], scalar=-1.0, in1=xs[:, s, :],
                                                 op0=ALU.add, op1=ALU.add))
                dve.sem_inc(s_u, 1)
                ch.step(dve.bn_stats(st[:, s, :], u[:, s, :]))
                dve.sem_inc(s_hold, 1)
                ch.step(dve.bn_aggr(mv[:, s, :], st[:, s, :]))
                wait(dve, s_r, at.count(1, 1 - RING))
                ch.step(dve.tensor_scalar(q[:, s, 0:1], mv[:, s, 1:2], EPS, None, ALU.add))
                ch.step(dve.tensor_scalar(q[:, s, 1:2], mv[:, s, 1:2], 1.0 + EPS, EPS * EPS, ALU.mult, ALU.add))
                dve.sem_inc(s_q, 1)

            def norms(at):
                s = at.slot(RING)
                dve.wait_ge(s_r, at.count(1, 1))
                wait(dve, s_w2[s], at.uses(RING, 16))
                dve.tensor_scalar(x2[:, s, :], u[:, s, :], mv[:, s, 0:1], r[:, s, 0:1], ALU.subtract, ALU.mult).then_inc(s_x2, 1)
                wait(dve, s_w3[s], at.uses(RING, 16))
                wait(dve, s_v, at.count(1, 1 - RING))
                wait(dve, s_t3, at.count(1, 1 - RING))
                dve.tensor_scalar(x3[:, s, :], u[:, s, :], mv[:, s, 0:1], r[:, s, 1:2], ALU.subtract, ALU.mult).then_inc(s_x3, 1)

            def biased(at):
                s, b = at.slot(RING), at.slot(2)
                dve.wait_ge(s_xp, at.count(1, 1))
                wait(dve, s_ex, at.count(1, 1 - RING))
                dve.tensor_tensor(t1[:, s, :], xp[:, b, 0:F], env["bias_all"][0:P, :], ALU.add).then_inc(s_t1, 1)

            def last(at):
                s = at.slot(RING)
                ch = Chain(dve, c5, at.count(6))
                dve.wait_ge(s_ex, at.count(1, 1))
                dve.wait_ge(s_t1, at.count(1, 1))
                ch.step(dve.scalar_tensor_tensor(out=el[:, s, :], in0=ex[:, s, :], scalar=1.0, in1=t1[:, s, :], op0=ALU.min, op1=ALU.max))
                wait(dve, s_out, at.count(1, 1 - RING))
                ch.step(dve.tensor_tensor(v[:, s, :], el[:, s, :], x3[:, s, :], ALU.add))
                dve.sem_inc(s_v, 1)
                ch.step(dve.bn_stats(st3[:, s, :], v[:, s, :]))
                dve.sem_inc(s_hold, 1)
                ch.step(dve.bn_aggr(mv3[:, s, :], st3[:, s, :]))
                wait(dve, s_out, at.count(1, 1 - RING))
                ch.step(dve.tensor_scalar(neg[:, s, :], mv3[:, s, 0:1], -1.0, None, ALU.mult))
                ch.step(dve.tensor_scalar(q3[:, s, :], mv3[:, s, 1:2], EPS, None, ALU.add))
                dve.sem_inc(s_q3, 1)
            run_stages(dve, [(8, last), (7, biased), (5, norms), (4, residual), (2, sums), (1, score)], T + 1)
    ph.end()


def segment_max(nc, env, name, value, most, heads):
    ph = Phase(nc, name)
    meta, key = env["meta"][1], env["srec"][1][:, :, 1]
    low = 1.0e38
    cut, cut_back = ph.sb("cut", [P, T]), ph.sb("cut_back", [P, T])
    run = ph.sb("run", [P, T, heads])
    ends = ph.sb("ends", [P, 2 * heads + 2, 128])
    penalty = ph.sb("penalty", [P, 2, 2, P])
    cand = ph.sb("cand", [P, 2 * heads, P])
    both, full = ph.sb("both", [P, 2, 2 * heads]), ph.sb("full", [P, 2, heads])
    rows = ph.ps("rows", [P, 2 * heads + 4, 128])
    s_v, s_ends, s_rows = ph.sem("steps"), ph.sem("ends"), ph.sem("rows")

    with nc.Block() as block:
        @block.vector
        def _(dve):
            ch = Chain(dve, s_v)

            def spread(src):
                for h in range(heads):
                    ch.step(dve.tensor_tensor_scan(run[:, :, h], cut[:, :], src[:, :, h], -low, ALU.add, ALU.max))
                for h in range(heads):
                    ch.step(dve.tensor_tensor_scan(most[:, ::-1, h], cut_back[:, ::-1], run[:, ::-1, h], -low, ALU.add, ALU.max))
            ch.step(dve.tensor_scalar(cut[:, :], meta["same"][:, :], low, -low, ALU.mult, ALU.add))
            ch.step(dve.tensor_copy(cut_back[:, 0:T - 1], cut[:, 1:T]))
            ch.step(dve.memset(cut_back[:, T - 1:T], 0.0))
            spread(value)
            for h in range(heads):
                ch.step(dve.tensor_copy(ends[:, 2 * h, :], most[:, 0, h:h + 1].broadcast_to([P, 128])))
                ch.step(dve.tensor_copy(ends[:, 2 * h + 1, :], most[:, T - 1, h:h + 1].broadcast_to([P, 128])))
            ch.step(dve.tensor_copy(ends[:, 2 * heads, :], key[:, 0:1].broadcast_to([P, 128])))
            ch.step(dve.tensor_copy(ends[:, 2 * heads + 1, :], key[:, T - 1:T].broadcast_to([P, 128])))
            dve.sem_inc(s_ends, 1)
            dve.wait_ge(s_rows, 1)
            for mine, t in enumerate((0, T - 1)):
                for theirs in range(2):
                    ch.step(dve.tensor_scalar(penalty[:, mine, theirs, :], rows[:, 2 * heads + theirs, 0:P], key[:, t:t + 1], -low,
                                              ALU.not_equal, ALU.mult))
                for h in range(heads):
                    ch.step(dve.tensor_tensor(cand[:, 2 * h:2 * h + 2, :], rows[:, 2 * h:2 * h + 2, 0:P], penalty[:, mine, :, :], ALU.add))
                ch.step(dve.tensor_reduce(both[:, mine, :], cand[:, :, :], X, ALU.max))
                ch.step(dve.tensor_reduce(full[:, mine, :], both[:, mine, :].rearrange("p (h e) -> p h e", e=2), X, ALU.max))
                ch.step(dve.tensor_tensor(most[:, t, :], most[:, t, :], full[:, mine, :], ALU.max))
            spread(most)

        @block.tensor
        def _(pe):
            pe.wait_ge(s_ends, 1)
            for n in range(2 * heads + 2):
                mm = pe.transpose(rows[:, n, 0:P], ends[:, n, 0:P], env["ident"][0:P, 0:P])
            mm.then_inc(s_rows, 1)
    ph.end()


def running_sums(dve, ch, meta, acc, lead, msg, at, s):
    ch.step(dve.scalar_tensor_tensor(out=acc[:, s, :], in0=acc[:, (s - 1) % RING, :], scalar=meta["same"][:, at.col],
                                     in1=msg[:, s, :], op0=ALU.mult, op1=ALU.add))
    ch.step(dve.scalar_tensor_tensor(out=lead[:, :], in0=acc[:, s, :], scalar=meta["lead_end"][:, at.col],
                                     in1=lead[:, :], op0=ALU.mult, op1=ALU.add))


def attention_scores(nc, env, V, score):
    ph = Phase(nc, "att1")
    meta, rec = env["meta"][1], env["srec"][1]
    gix = ph.sb("gix", [P, RING, 2], I32)
    xd, xs = ph.sb("xd", [P, RING, F]), ph.sb("xs", [P, RING, F])
    xT = ph.sb("xT", [128, RING, 4, P])
    qs, prod, dot = ph.sb("qs", [P, RING, F]), ph.sb("prod", [P, RING, F]), ph.sb("dot", [P, RING, H2])
    tp, kq, vp = ph.ps("tp", [128, 2, 4, 128]), ph.ps("kq", [P, 2, 512]), ph.ps("vp", [P, 2, 512])
    s_d, s_s, s_o = ([ph.sem(f"{n}{k}") for k in range(RING)] for n in ("dst_rows", "src_rows", "kept"))
    s_ix, s_t, s_xT, s_p, s_qs, s_V, s_dot, c1 = (ph.sem(n) for n in ("index", "transposed", "xT", "projected", "q", "v", "scored", "steps"))
    w_kv, w_q = env["w_kv"], env["w_q"]

    with nc.Block() as block:
        @block.gpsimd
        def _(pool):
            dram = Rows(ph, pool, N)

            def fetch(at):
                s = at.slot(RING)
                wait(pool, s_t, at.count(1, 1 - RING))
                wait(pool, s_o[s], at.uses(RING, 32))
                pool.tensor_copy(gix[:, s, 0:1], meta["node"][:, at.col]).then_inc(s_ix, 1)
                pool.tensor_copy(gix[:, s, 1:2], meta["other"][:, at.col]).then_inc(s_ix, 1)
                pool.wait_ge(s_ix, at.count(2, 2))
                dram.gather(xd[:, s, :], env["X2"], gix[:, s, 0:1], s_d[s])
                dram.gather(xs[:, s, :], env["X2"], gix[:, s, 1:2], s_s[s])
            run_stages(pool, [(0, fetch)], T)

        @block.sync
        def _(sp):
            def keep(at):
                s = at.slot(RING)
                sp.wait_ge(s_d[s], at.uses(RING, 16, 16))
                for a, n in CUTS:
                    sp.dma_start(env["D2"][at.col, a:a + n, :].rearrange("o p f -> (o p) f"), xd[a:a + n, s, :]).then_inc(s_o[s], 16)
            run_stages(sp, [(0, keep)], T)
            for s in range(RING):
                sp.wait_ge(s_o[s], 32 * (T // RING))

        @block.tensor
        def _(pe):
            def turn_rows(at):
                s, b = at.slot(RING), at.slot(2)
                pe.wait_ge(s_d[s], at.uses(RING, 16, 16))
                pe.wait_ge(s_s[s], at.uses(RING, 16, 16))
                wait(pe, s_xT, at.count(1, -1))
                for n, rows in enumerate((xs, xd)):
                    for k in range(KH):
                        mm = pe.transpose(tp[:, b, 2 * n + k, 0:P], rows[:, s, 128 * k:128 * k + 128], env["ident"][0:P, 0:P])
                mm.then_inc(s_t, 1)

            def project(at):
                s, b = at.slot(RING), at.slot(2)
                pe.wait_ge(s_xT, at.count(1, 1))
                wait(pe, s_dot, at.count(1, -1))
                wait(pe, s_V, at.count(1, -1))
                for out, x0, w in ((kq[:, b, F:2 * F], 2, w_q[:, :, :]), (kq[:, b, 0:F], 0, w_kv[:, :, 0:F]), (vp[:, b, 0:F], 0, w_kv[:, :, F:2 * F])):
                    for k in range(KH):
                        mm = pe.matmul(out, xT[:, s, x0 + k, :], w[:, k, :], start=(k == 0), stop=(k == 1), skip_group_check=True)
                mm.then_inc(s_p, 1)
            run_stages(pe, [(1, project), (0, turn_rows)], T)

        @block.scalar
        def _(act):
            def copy_rows(at):
                s, b = at.slot(RING), at.slot(2)
                act.wait_ge(s_t, at.count(1, 1))
                wait(act, s_p, at.count(1, 1 - RING))
                act.copy(xT[:, s, :, :], tp[:, b, :, 0:P]).then_inc(s_xT, 1)

            def copy_out(at):
                s, b = at.slot(RING), at.slot(2)
                act.wait_ge(s_p, at.count(1, 1))
                wait(act, s_dot, at.count(1, 1 - RING))
                act.mul(qs[:, s, :], kq[:, b, F:2 * F], float(C2) ** 0.5).then_inc(s_qs, 1)
                act.copy(V[:, at.col, :].rearrange("p o f -> p (o f)"), vp[:, b, 0:F]).then_inc(s_V, 1)
            run_stages(act, [(1, copy_out), (0, copy_rows)], T)

        @block.vector
        def _(dve):
            def dots(at):
                s, b = at.slot(RING), at.slot(2)
                ch = Chain(dve, c1, at.count(3))
                dve.wait_ge(s_qs, at.count(1, 1))
                ch.step(dve.tensor_tensor(prod[:, s, :], kq[:, b, 0:F], qs[:, s, :], ALU.mult))
                ch.step(dve.tensor_reduce(dot[:, s, :], prod[:, s, :].rearrange("p (h c) -> p h c", h=H2), X, ALU.add))
                ch.step(dve.tensor_tensor(score[:, at.col, :].rearrange("p o h -> p (o h)"), dot[:, s, :],
                                          rec[:, at.col, 4:4 + H2].rearrange("p o h -> p (o h)"), ALU.add))
                dve.sem_inc(s_dot, 1)
            run_stages(dve, [(1, dots)], T)
    ph.end()


def attention_sums(nc, env, V, score, most):
    ph = Phase(nc, "att2")
    meta, carry, w_o = env["meta"][1], env["meta"][1]["carry"], env["w_o"]
    W = F + H2
    wix = ph.sb("wix", [P, RING], I32)
    xd, msg, acc, lead = ph.sb("xd", [P, RING, F]), ph.sb("msg", [P, RING, W]), ph.sb("acc", [P, RING, W]), ph.sb("lead", [P, W])
    den = ph.sb("den", [P, RING, H2])
    rr, on, onT = ph.sb("rr", [P, RING, H2]), ph.sb("on", [P, RING, F]), ph.sb("onT", [128, RING, KH, P])
    u, x3 = ph.sb("u", [P, RING, F]), ph.sb("x3", [P, RING, F])
    st, mv, q, lnq, r = (ph.sb(n, [P, RING, k]) for n, k in (("st", 6), ("mv", 2), ("q", 1), ("lnq", 1), ("r", 1)))
    tp, op, cps = ph.ps("tp", [128, 2, 4, 128]), ph.ps("op", [P, 2, 512]), ph.ps("cps", [P, 512])
    s_l, s_w = ([ph.sem(f"{n}{k}") for k in range(RING)] for n in ("kept_rows", "stored"))
    (s_wx, s_a, s_msg, s_on, s_t, s_onT, s_o, s_u, s_q, s_r, s_x3, s_init, s_c, s_hold, c0, c1, c2, c3, ca) = (
        ph.sem(n) for n in ("windex", "weights", "msgs", "normed", "transposed", "copied", "product", "u", "q", "r", "x3",
                            "init", "carried", "hold", "steps0", "steps1", "steps2", "steps3", "rsqrt"))

    with nc.Block() as block:
        @block.sync
        def _(sp):
            def load(at):
                s = at.slot(RING)
                wait(sp, s_u, at.count(1, 1 - RING))
                src = env["D2"][slice(0, 1) if at.is_lead else at.col, :, :].rearrange("o p f -> (o p) f")
                load_rows(sp, xd[:, s, :], src, s_l[s])
            run_stages(sp, [(0, load)], T + 1)

        @block.gpsimd
        def _(pool):
            dram = Rows(ph, pool, N)

            def put(at):
                s = at.slot(RING)
                wait(pool, s_w[s], at.uses(RING, 16))
                pool.tensor_copy(wix[:, s:s + 1], meta["write"][:, at.col]).then_inc(s_wx, 1)
                pool.wait_ge(s_wx, at.count(1, 1))
                pool.wait_ge(s_x3, at.count(1, 1))
                dram.scatter(env["X3"], wix[:, s:s + 1], x3[:, s, :], s_w[s])
            run_stages(pool, [(0, put)], T + 1)
            for s in range(RING):
                pool.wait_ge(s_w[s], 16 * (T // RING + (s == 0)))

        @block.tensor
        def _(pe):
            def turn(at):
                s, b = at.slot(RING), at.slot(2)
                if at.is_lead:
                    pe.wait_ge(s_msg, T)
                    pe.matmul(cps[:, 0:W], carry[:, :], acc[:, (T - 1) % RING, :], start=True, stop=True).then_inc(s_c, 1)
                pe.wait_ge(s_on, at.count(1, 1))
                wait(pe, s_onT, at.count(1, -1))
                for k in range(KH):
                    mm = pe.transpose(tp[:, b, k, 0:P], on[:, s, 128 * k:128 * k + 128], env["ident"][0:P, 0:P])
                mm.then_inc(s_t, 1)

            def product(at):
                s, b = at.slot(RING), at.slot(2)
                pe.wait_ge(s_onT, at.count(1, 1))
                wait(pe, s_u, at.count(1, -1))
                for k in range(KH):
                    mm = pe.matmul(op[:, b, 0:F], onT[:, s, k, :], w_o[:, k, :], start=(k == 0), stop=(k == 1))
                mm.then_inc(s_o, 1)
            run_stages(pe, [(1, product), (0, turn)], T + 1)

        @block.scalar
        def _(act):
            act.wait_ge(s_a, 1)
            act.activation(score[:, :, :], score[:, :, :], ACT.Exp).then_inc(s_a, 1)

            def copy(at):
                s, b = at.slot(RING), at.slot(2)
                act.wait_ge(s_t, at.count(1, 1))
                wait(act, s_o, at.count(1, 1 - RING))
                act.copy(onT[:, s, :, :], tp[:, b, 0:KH, 0:P]).then_inc(s_onT, 1)

            def norm(at):
                s = at.slot(RING)
                act.wait_ge(s_q, at.count(1, 1))
                wait(act, s_x3, at.count(1, 1 - RING))
                ch = Chain(act, ca, at.count(2))
                rsqrt(act, ch, r[:, s, :], lnq[:, s, :], q[:, s, :])
                act.sem_inc(s_r, 1)
            run_stages(act, [(2, norm), (0, copy)], T + 1)

        @block.vector
        def _(dve):
            dve.memset(acc[:, RING - 1, :], 0.0).then_inc(s_init, 1)
            dve.memset(lead[:, :], 0.0).then_inc(s_init, 1)
            ch = Chain(dve, c0)
            ch.step(dve.tensor_tensor(score[:, :, :], score[:, :, :], most[:, :, :], ALU.subtract))
            dve.sem_inc(s_a, 1)
            dve.wait_ge(s_a, 2)
            dve.wait_ge(s_init, 2)

            def sums(at):
                s = at.slot(RING)
                ch = Chain(dve, c1, at.count(4))
                if at.is_lead:
                    dve.wait_ge(s_c, 1)
                    ch.step(dve.tensor_tensor(acc[:, s, :], cps[:, 0:W], lead[:, :], ALU.add))
                else:
                    a = score[:, at.col, :].rearrange("p o h -> p (o h)")
                    ch.step(dve.tensor_copy(msg[:, s, F:W], a))
                    ch.step(dve.tensor_tensor(msg[:, s, 0:F].rearrange("p (h c) -> p h c", h=H2),
                                              V[:, at.col, :].rearrange("p o (h c) -> p (o h) c", h=H2),
                                              a.unsqueeze(2).broadcast_to([P, H2, C2]), ALU.mult))
                    running_sums(dve, ch, meta, acc, lead, msg, at, s)
                dve.sem_inc(s_msg, 1)
                ch = Chain(dve, c2, at.count(3))
                ch.step(dve.tensor_scalar(den[:, s, :], acc[:, s, F:W], TINY, None, ALU.max))
                ch.step(dve.reciprocal(rr[:, s, :], den[:, s, :]))
                wait(dve, s_t, at.count(1, 1 - RING))
                ch.step(dve.tensor_tensor(on[:, s, :].rearrange("p (h c) -> p h c", h=H2),
                                          acc[:, s, 0:F].rearrange("p (h c) -> p h c", h=H2),
                                          rr[:, s, :].unsqueeze(2).broadcast_to([P, H2, C2]), ALU.mult))
                dve.sem_inc(s_on, 1)

            def residual(at):
                s, b = at.slot(RING), at.slot(2)
                ch = Chain(dve, c3, at.count(4))
                dve.wait_ge(s_o, at.count(1, 1))
                dve.wait_ge(s_l[s], at.uses(RING, 32, 32))
                wait(dve, s_x3, at.count(1, 1 - RING))
                ch.step(dve.tensor_tensor(u[:, s, :], op[:, b, 0:F], xd[:, s, :], ALU.add))
                dve.sem_inc(s_u, 1)
                ch.step(dve.bn_stats(st[:, s, :], u[:, s, :]))
                dve.sem_inc(s_hold, 1)
                ch.step(dve.bn_aggr(mv[:, s, :], st[:, s, :]))
                wait(dve, s_r, at.count(1, 1 - RING))
                ch.step(dve.tensor_scalar(q[:, s, :], mv[:, s, 1:2], EPS, None, ALU.add))
                dve.sem_inc(s_q, 1)

            def norms(at):
                s = at.slot(RING)
                dve.wait_ge(s_r, at.count(1, 1))
                wait(dve, s_w[s], at.uses(RING, 16))
                dve.tensor_scalar(x3[:, s, :], u[:, s, :], mv[:, s, 0:1], r[:, s, :], ALU.subtract, ALU.mult).then_inc(s_x3, 1)
            run_stages(dve, [(3, norms), (2, residual), (0, sums)], T + 1)
    ph.end()


def attention(nc, env, d):
    with ExitStack() as ctx:
        V = ctx.enter_context(nc.sbuf_tensor("att_v", [P, T, F], F32))
        score = ctx.enter_context(nc.sbuf_tensor("att_score", [P, T, H2], F32))
        most = ctx.enter_context(nc.sbuf_tensor("att_most", [P, T, H2], F32))
        attention_scores(nc, env, V, score)
        segment_max(nc, env, "attm", score, most, H2)
        attention_sums(nc, env, V, score, most)


def self_scores(nc, env, V, edge, loop):
    ph = Phase(nc, "self1")
    meta, w = env["meta"][1], env["w_self"]
    gix = ph.sb("gix", [P, RING, 2], I32)
    xd, xs = ph.sb("xd", [P, RING, F]), ph.sb("xs", [P, RING, F])
    xT = ph.sb("xT", [128, RING, 4, P])
    a_s, hd, sc = ph.sb("a_s", [P, RING, H1]), ph.sb("hd", [P, RING, F + 8]), ph.sb("sc", [P, RING, 2, H1])
    tp, sp_, dp = ph.ps("tp", [128, 2, 4, 128]), ph.ps("src", [P, 2, 512]), ph.ps("dst", [P, 2, 512])
    s_d, s_s, s_o, s_o2 = ([ph.sem(f"{n}{k}") for k in range(RING)] for n in ("dst_rows", "src_rows", "kept", "kept_h"))
    s_ix, s_t, s_xT, s_p, s_V, s_hd, s_sc, c1 = (ph.sem(n) for n in ("index", "transposed", "xT", "projected", "v", "hd", "scored", "steps"))

    with nc.Block() as block:
        @block.gpsimd
        def _(pool):
            dram = Rows(ph, pool, N)

            def fetch(at):
                s = at.slot(RING)
                wait(pool, s_t, at.count(1, 1 - RING))
                wait(pool, s_o[s], at.uses(RING, 32))
                pool.tensor_copy(gix[:, s, 0:1], meta["node"][:, at.col]).then_inc(s_ix, 1)
                pool.tensor_copy(gix[:, s, 1:2], meta["other"][:, at.col]).then_inc(s_ix, 1)
                pool.wait_ge(s_ix, at.count(2, 2))
                dram.gather(xd[:, s, :], env["X3"], gix[:, s, 0:1], s_d[s])
                dram.gather(xs[:, s, :], env["X3"], gix[:, s, 1:2], s_s[s])
            run_stages(pool, [(0, fetch)], T)

        @block.sync
        def _(sp):
            def keep(at):
                s = at.slot(RING)
                sp.wait_ge(s_d[s], at.uses(RING, 16, 16))
                for a, n in CUTS:
                    sp.dma_start(env["D3"][at.col, a:a + n, 0:F].rearrange("o p f -> (o p) f"), xd[a:a + n, s, :]).then_inc(s_o[s], 16)

            def keep_h(at):
                s = at.slot(RING)
                sp.wait_ge(s_hd, at.count(1, 1))
                for a, n in CUTS:
                    sp.dma_start(env["D3"][at.col, a:a + n, F:2 * F].rearrange("o p f -> (o p) f"), hd[a:a + n, s, 0:F]).then_inc(s_o2[s], 16)
            run_stages(sp, [(2, keep_h), (0, keep)], T)
            for s in range(RING):
                sp.wait_ge(s_o[s], 32 * (T // RING))
                sp.wait_ge(s_o2[s], 32 * (T // RING))

        @block.tensor
        def _(pe):
            def turn_rows(at):
                s, b = at.slot(RING), at.slot(2)
                pe.wait_ge(s_d[s], at.uses(RING, 16, 16))
                pe.wait_ge(s_s[s], at.uses(RING, 16, 16))
                wait(pe, s_xT, at.count(1, -1))
                for n, rows in enumerate((xs, xd)):
                    for k in range(KH):
                        mm = pe.transpose(tp[:, b, 2 * n + k, 0:P], rows[:, s, 128 * k:128 * k + 128], env["ident"][0:P, 0:P])
                mm.then_inc(s_t, 1)

            def project(at):
                s, b = at.slot(RING), at.slot(2)
                pe.wait_ge(s_xT, at.count(1, 1))
                wait(pe, s_V, at.count(2, -2))
                wait(pe, s_hd, at.count(1, -1))
                for out, x0, n in ((sp_[:, b, 0:F + 4], 0, F + 4), (dp[:, b, 0:F + 8], 2, F + 8)):
                    for k in range(KH):
                        mm = pe.matmul(out, xT[:, s, x0 + k, :], w[:, k, 0:n], start=(k == 0), stop=(k == 1))
                mm.then_inc(s_p, 1)
            run_stages(pe, [(1, project), (0, turn_rows)], T)

        @block.scalar
        def _(act):
            def copy_rows(at):
                s, b = at.slot(RING), at.slot(2)
                act.wait_ge(s_t, at.count(1, 1))
                wait(act, s_p, at.count(1, 1 - RING))
                act.copy(xT[:, s, :, :], tp[:, b, :, 0:P]).then_inc(s_xT, 1)

            def copy_out(at):
                s, b = at.slot(RING), at.slot(2)
                act.wait_ge(s_p, at.count(1, 1))
                wait(act, s_sc, at.count(1, 1 - RING))
                act.copy(V[:, at.col, :].rearrange("p o f -> p (o f)"), sp_[:, b, 0:F]).then_inc(s_V, 1)
                act.copy(a_s[:, s, :], sp_[:, b, F:F + H1]).then_inc(s_V, 1)
                wait(act, s_o2[s], at.uses(RING, 32))
                act.copy(hd[:, s, :], dp[:, b, 0:F + 8]).then_inc(s_hd, 1)
            run_stages(act, [(1, copy_out), (0, copy_rows)], T)

        @block.vector
        def _(dve):
            def scores(at):
                s = at.slot(RING)
                ch = Chain(dve, c1, at.count(4))
                dve.wait_ge(s_V, at.count(2, 2))
                dve.wait_ge(s_hd, at.count(1, 1))
                ch.step(dve.tensor_tensor(sc[:, s, 0, :], a_s[:, s, :], hd[:, s, F + 4:F + 8], ALU.add))
                ch.step(dve.tensor_tensor(sc[:, s, 1, :], hd[:, s, F:F + 4], hd[:, s, F + 4:F + 8], ALU.add))
                for n, out in enumerate((edge, loop)):
                    ch.step(dve.scalar_tensor_tensor(out=out[:, at.col, :].rearrange("p o h -> p (o h)"), in0=sc[:, s, n, :], scalar=ALPHA,
                                                     in1=sc[:, s, n, :], op0=ALU.mult, op1=ALU.max))
                dve.sem_inc(s_sc, 1)
            run_stages(dve, [(1, scores)], T)
    ph.end()


def self_sums(nc, env, d, V, edge, loop, most):
    ph = Phase(nc, "self2")
    meta, carry = env["meta"][1], env["meta"][1]["carry"]
    W = F + H1
    finite = ph.sb("finite", [P, T, H1])
    wix = ph.sb("wix", [P, RING], I32)
    xd, msg, acc, lead = ph.sb("xd", [P, RING, 2 * F]), ph.sb("msg", [P, RING, W]), ph.sb("acc", [P, RING, W]), ph.sb("lead", [P, W])
    own, tot = ph.sb("own", [P, RING, F]), ph.sb("tot", [P, RING, F])
    den, rr = ph.sb("den", [P, RING, H1]), ph.sb("rr", [P, RING, H1])
    agg, t1, ex, el, v, out = (ph.sb(n, [P, RING, F]) for n in ("agg", "t1", "ex", "el", "v", "out"))
    st, mv, q, lnq, r = (ph.sb(n, [P, RING, k]) for n, k in (("st", 6), ("mv", 2), ("q", 1), ("lnq", 1), ("r", 1)))
    cps = ph.ps("cps", [P, 512])
    s_l, s_w = ([ph.sem(f"{n}{k}") for k in range(RING)] for n in ("kept_rows", "stored"))
    (s_wx, s_a, s_msg, s_t1, s_ex, s_v, s_q, s_r, s_out, s_init, s_c, s_hold, c0, c1, c2, c3, ca) = (
        ph.sem(n) for n in ("windex", "weights", "msgs", "t1", "exp", "v", "q", "r", "out",
                            "init", "carried", "hold", "steps0", "steps1", "steps2", "steps3", "rsqrt"))

    with nc.Block() as block:
        @block.sync
        def _(sp):
            def load(at):
                s = at.slot(RING)
                wait(sp, s_v, at.count(1, 1 - RING))
                src = env["D3"][slice(0, 1) if at.is_lead else at.col, :, :].rearrange("o p f -> (o p) f")
                load_rows(sp, xd[:, s, :], src, s_l[s])
            run_stages(sp, [(0, load)], T + 1)

        @block.gpsimd
        def _(pool):
            dram = Rows(ph, pool, N)

            def put(at):
                s = at.slot(RING)
                wait(pool, s_w[s], at.uses(RING, 16))
                pool.tensor_copy(wix[:, s:s + 1], meta["write"][:, at.col]).then_inc(s_wx, 1)
                pool.wait_ge(s_wx, at.count(1, 1))
                pool.wait_ge(s_out, at.count(1, 1))
                dram.scatter(d["out"], wix[:, s:s + 1], out[:, s, :], s_w[s])
            run_stages(pool, [(0, put)], T + 1)
            for s in range(RING):
                pool.wait_ge(s_w[s], 16 * (T // RING + (s == 0)))

        @block.tensor
        def _(pe):
            pe.wait_ge(s_msg, T)
            pe.matmul(cps[:, 0:W], carry[:, :], acc[:, (T - 1) % RING, :], start=True, stop=True).then_inc(s_c, 1)

        @block.scalar
        def _(act):
            act.wait_ge(s_a, 1)
            act.activation(edge[:, :, :], edge[:, :, :], ACT.Exp).then_inc(s_a, 1)
            act.activation(loop[:, :, :], loop[:, :, :], ACT.Exp).then_inc(s_a, 1)

            def exps(at):
                s = at.slot(RING)
                act.wait_ge(s_t1, at.count(1, 1))
                wait(act, s_v, at.count(1, 1 - RING))
                act.activation(ex[:, s, :], t1[:, s, :], ACT.Exp, bias=env["minus1"][0:P, :]).then_inc(s_ex, 1)

            def norm(at):
                s = at.slot(RING)
                act.wait_ge(s_q, at.count(1, 1))
                wait(act, s_out, at.count(1, 1 - RING))
                ch = Chain(act, ca, at.count(2))
                rsqrt(act, ch, r[:, s, :], lnq[:, s, :], q[:, s, :])
                act.sem_inc(s_r, 1)
            run_stages(act, [(1, norm), (0, exps)], T + 1)

        @block.vector
        def _(dve):
            dve.memset(acc[:, RING - 1, :], 0.0).then_inc(s_init, 1)
            dve.memset(lead[:, :], 0.0).then_inc(s_init, 1)
            ch = Chain(dve, c0)
            ch.step(dve.tensor_tensor(finite[:, :, :], most[:, :, :], most[:, :, :], ALU.subtract))
            ch.step(dve.tensor_scalar(finite[:, :, :], finite[:, :, :], 0.0, None, ALU.is_equal))
            ch.step(dve.tensor_scalar(most[:, :, :], most[:, :, :], -BIG, BIG, ALU.max, ALU.min))
            ch.step(dve.tensor_tensor(most[:, :, :], most[:, :, :], finite[:, :, :], ALU.mult))
            ch.step(dve.tensor_tensor(edge[:, :, :], edge[:, :, :], most[:, :, :], ALU.subtract))
            ch.step(dve.tensor_tensor(loop[:, :, :], loop[:, :, :], most[:, :, :], ALU.subtract))
            dve.sem_inc(s_a, 1)
            dve.wait_ge(s_a, 3)
            dve.wait_ge(s_init, 2)

            def heads(ap):
                return ap.rearrange("p (h c) -> p h c", h=H1)

            def each_head(ap):
                return ap.unsqueeze(2).broadcast_to([P, H1, C1])

            def sums(at):
                s = at.slot(RING)
                ch = Chain(dve, c1, at.count(4))
                if at.is_lead:
                    dve.wait_ge(s_c, 1)
                    ch.step(dve.tensor_tensor(acc[:, s, :], cps[:, 0:W], lead[:, :], ALU.add))
                else:
                    a = edge[:, at.col, :].rearrange("p o h -> p (o h)")
                    ch.step(dve.tensor_copy(msg[:, s, F:W], a))
                    ch.step(dve.tensor_tensor(heads(msg[:, s, 0:F]), V[:, at.col, :].rearrange("p o (h c) -> p (o h) c", h=H1),
                                              each_head(a), ALU.mult))
                    running_sums(dve, ch, meta, acc, lead, msg, at, s)
                dve.sem_inc(s_msg, 1)
                mine = loop[:, 0, :] if at.is_lead else loop[:, at.col, :].rearrange("p o h -> p (o h)")
                ch = Chain(dve, c2, at.count(7))
                dve.wait_ge(s_l[s], at.uses(RING, 32, 32))
                ch.step(dve.tensor_tensor(heads(own[:, s, :]), heads(xd[:, s, F:2 * F]), each_head(mine), ALU.mult))
                ch.step(dve.tensor_tensor(tot[:, s, :], own[:, s, :], acc[:, s, 0:F], ALU.add))
                ch.step(dve.tensor_tensor(den[:, s, :], acc[:, s, F:W], mine, ALU.add))
                ch.step(dve.tensor_scalar(den[:, s, :], den[:, s, :], TINY, None, ALU.max))
                ch.step(dve.reciprocal(rr[:, s, :], den[:, s, :]))
                ch.step(dve.tensor_tensor(heads(agg[:, s, :]), heads(tot[:, s, :]), each_head(rr[:, s, :]), ALU.mult))
                wait(dve, s_ex, at.count(1, 1 - RING))
                ch.step(dve.tensor_tensor(t1[:, s, :], agg[:, s, :], env["bias_all"][0:P, :], ALU.add))
                dve.sem_inc(s_t1, 1)

            def residual(at):
                s = at.slot(RING)
                ch = Chain(dve, c3, at.count(5))
                dve.wait_ge(s_ex, at.count(1, 1))
                ch.step(dve.scalar_tensor_tensor(out=el[:, s, :], in0=ex[:, s, :], scalar=1.0, in1=t1[:, s, :], op0=ALU.min, op1=ALU.max))
                wait(dve, s_out, at.count(1, 1 - RING))
                ch.step(dve.tensor_tensor(v[:, s, :], el[:, s, :], xd[:, s, 0:F], ALU.add))
                dve.sem_inc(s_v, 1)
                ch.step(dve.bn_stats(st[:, s, :], v[:, s, :]))
                dve.sem_inc(s_hold, 1)
                ch.step(dve.bn_aggr(mv[:, s, :], st[:, s, :]))
                wait(dve, s_r, at.count(1, 1 - RING))
                ch.step(dve.tensor_scalar(q[:, s, :], mv[:, s, 1:2], EPS, None, ALU.add))
                dve.sem_inc(s_q, 1)

            def norms(at):
                s = at.slot(RING)
                dve.wait_ge(s_r, at.count(1, 1))
                wait(dve, s_w[s], at.uses(RING, 16))
                dve.tensor_scalar(out[:, s, :], v[:, s, :], mv[:, s, 0:1], r[:, s, :], ALU.subtract, ALU.mult).then_inc(s_out, 1)
            run_stages(dve, [(2, norms), (1, residual), (0, sums)], T + 1)
    ph.end()


def self_loops(nc, env, d):
    with ExitStack() as ctx:
        V = ctx.enter_context(nc.sbuf_tensor("self_v", [P, T, F], F32))
        edge, loop, top, most = (ctx.enter_context(nc.sbuf_tensor(f"self_{n}", [P, T, H1], F32)) for n in ("edge", "loop", "top", "most"))
        self_scores(nc, env, V, edge, loop)
        larger(nc, edge, loop, top)
        segment_max(nc, env, "selfm", top, most, H1)
        self_sums(nc, env, d, V, edge, loop, most)


def larger(nc, edge, loop, top):
    ph = Phase(nc, "larger")
    done = ph.sem("done")
    with nc.Block() as block:
        @block.vector
        def _(dve):
            dve.tensor_tensor(top[:, :, :], edge[:, :, :], loop[:, :, :], ALU.max).then_inc(done, 1)
            dve.wait_ge(done, 1)
    ph.end()


def graph_net(nc, d, upto="all", debug=None):
    with ExitStack() as ctx:
        def sb(name, shape, dt=F32):
            return ctx.enter_context(nc.sbuf_tensor(name, shape, dt))
        scratch = (lambda n, s: (debug or {}).get(n) if (debug or {}).get(n) is not None else nc.dram_tensor(n, s, F32, kind="Internal").ap())
        env = {
            "ident": sb("ident", [128, 128]), "ident_bf": sb("ident_bf", [128, 128], BF16),
            "before": sb("before", [128, 128]), "after": sb("after", [128, 128]), "ones": sb("ones", [128, 128]),
            "iota_row": sb("iota_row", [128, 256], BF16), 
            "zrow": sb("zrow", [128, 512], BF16), "zcol": sb("zcol", [128, 128]), "zwide": sb("zwide", [128, F + 4]),
            "onep": sb("onep", [128, 1]), "minus1": sb("minus1", [128, 1]),
            "bias_row": sb("bias_row", [128, F]), "bias_all": sb("bias_all", [128, F]),
            "bn": sb("bn", [128, 6, KH]), "affine": sb("affine", [128, 4, KH]),
            "w1": sb("w1", [128, KH, F]), "w2": sb("w2", [128, KH, F]),
            "w_gat": sb("w_gat", [128, KH, F + 4]), "w_gat_s": sb("w_gat_s", [128, KH, 4]),
            "w_self": sb("w_self", [128, KH, F + 8]), "w_kv": sb("w_kv", [128, KH, 2 * F]),
            "w_q": sb("w_q", [128, KH, F]), "w_o": sb("w_o", [128, KH, F]),
            "H": scratch("H", [N, F]), "X1": scratch("X1", [N, F]), "X2": scratch("X2", [N, F]),
            "Y2": scratch("Y2", [NCH, 128, KH * CH]), "D2": scratch("D2", [T, P, F]), "D3": scratch("D3", [T, P, 2 * F]),
            "sorted": [scratch("by_src", [E, RC]), scratch("by_dst", [E, RC])],
        }
        env["X3"] = env["H"]
        meta = [{
            "same": sb(f"same{k}", [P, T]), "lead_end": sb(f"lead_end{k}", [P, T]), "emit": sb(f"emit{k}", [P, T + 1]),
            "node": sb(f"node{k}", [P, T + 1], I32), "other": sb(f"other{k}", [P, T], I32),
            "write": sb(f"write{k}", [P, T + 1], I32), "carry": sb(f"carry{k}", [P, P]),
        } for k in range(2)]
        env["meta"] = meta
        env["srec"] = [sb(f"srec{k}", [P, T, RC]) for k in range(2)]
        order = ["setup", "hist", "rank", "seg", "gin", "mom", "mlp", "nodes", "gat", "att", "self"]
        last = len(order) if upto == "all" else order.index(upto) + 1
        with ExitStack() as early:
            env["gram"] = early.enter_context(nc.psum_tensor("gram", [128, KH, 512], F32))
            with ExitStack() as sort:
                env["rec"] = sort.enter_context(nc.sbuf_tensor("rec", [P, T, RC], F32))
                env["digit"] = sort.enter_context(nc.sbuf_tensor("digit", [P, 2, 2, T], F32))
                env["base"] = sort.enter_context(nc.sbuf_tensor("base", [128, 2, 2, 256], F32))
                env["keyf"] = sort.enter_context(nc.sbuf_tensor("keyf", [P, 2, T], F32))
                setup(nc, env, d)
                if last > 1:
                    histogram(nc, env)
                if last > 2:
                    rank(nc, env, d)
            if last > 3:
                segments(nc, env)
            if last > 4:
                gin_edges(nc, env, d)
            if last > 5:
                moments(nc, env)
        if last > 6:
            mlp(nc, env)
        if last > 7:
            nodes(nc, env, d)
        if last > 8:
            gat_edges(nc, env, d)
        if last > 9:
            attention(nc, env, d)
        if last > 10:
            self_loops(nc, env, d)


_IN = ("x", "src", "dst", "edge_attr_8", "edge_weight", "L0_gnn_eps", "L0_gnn_W1", "L0_gnn_b1", "L0_gnn_g1", "L0_gnn_be1",
       "L0_gnn_W2", "L0_gnn_b2", "L0_gnn_g2", "L0_gnn_be2", "L3_gnn_W", "L3_gnn_bias")


def lay_out(inputs):
    a = {n: np.ascontiguousarray(np.asarray(inputs[n])) for n in _IN}
    a["W_gat"] = np.ascontiguousarray(np.asarray(inputs["L1_gnn_W"]).transpose(1, 0, 2).reshape(F, F))
    att = np.asarray(inputs["L1_gnn_a"])
    a["a_src"] = np.ascontiguousarray(att[:, 0, :C1].reshape(F))
    a["a_dst"] = np.ascontiguousarray(att[:, 0, C1:].reshape(F))
    a["att_src"] = np.ascontiguousarray(np.asarray(inputs["L3_gnn_att_src"]).reshape(F))
    a["att_dst"] = np.ascontiguousarray(np.asarray(inputs["L3_gnn_att_dst"]).reshape(F))
    for n in "qkvo":
        a[f"W{n}T"] = np.ascontiguousarray(np.asarray(inputs[f"L2_gnn_W{n}"]).T)
    return a


def kernel(**inputs):
    import concourse.bacc as bacc
    from concourse.bass_utils import run_bass_kernel_spmd

    nc = bacc.Bacc("TRN2", target_bir_lowering=False, num_devices=1)
    arrays = lay_out(inputs)
    d = {n: nc.dram_tensor(n, a.shape, mybir.dt.from_np(a.dtype), kind="ExternalInput").ap() for n, a in arrays.items()}
    d["out"] = nc.dram_tensor("out", (N, F), F32, kind="ExternalOutput").ap()
    graph_net(nc, d)
    return run_bass_kernel_spmd(nc, [arrays], core_ids=[0]).results[0]["out"]
```

```python
from contextlib import ExitStack

import concourse.bass as bass
import concourse.mybir as mybir
import numpy as np

F32 = mybir.dt.float32
I32 = mybir.dt.int32
BF16 = mybir.dt.bfloat16
ALU = mybir.AluOpType
ACT = mybir.ActivationFunctionType
X = mybir.AxisListType.X

N, F, E = 50000, 256, 12500
P = 125
T = E // P
CH = 4 * P
NCH = N // CH
KH = F // 128
EPS = 1e-5
ALPHA = 0.2
H1, C1 = 4, 64
H2, C2 = 8, 32
BIG = 3.0e38
TINY = 1.0e-37
DROP = 1 << 20
RC = 12
CUTS = ((0, 112), (112, 13))


class Use:

    def __init__(self, eng, u):
        self.eng, self.u, self.known = eng, u, {}

    def value(self, scale, offset=0):
        if isinstance(self.u, int):
            return self.u * scale + offset
        return self.u * scale + offset if offset else self.u * scale

    free = property(lambda self: self.value(1))
    ready = property(lambda self: self.value(1, 1))
    free16 = property(lambda self: self.value(16))
    ready16 = property(lambda self: self.value(16, 16))
    free32 = property(lambda self: self.value(32))
    ready32 = property(lambda self: self.value(32, 32))

    def base(self, k):
        return self.value(k)


class Chain:

    def __init__(self, eng, sem, base=0):
        self.eng, self.sem, self.base, self.n = eng, sem, base, 0

    def step(self, ins):
        self.go(ins)
        self.done()

    def go(self, ins):
        ins.then_inc(self.sem, 1)
        self.n += 1

    def done(self):
        self.eng.wait_ge(self.sem, self.base + self.n)


def stages(eng, steps, tiles=100, total=None):
    total = tiles if total is None else total
    lag = len(steps) - 1
    head = 2 * ((lag + 1) // 2)

    def alone(t):
        for k, step in enumerate(steps):
            if 0 <= t - k < total:
                step(t - k, (t - k) % 2, Use(eng, (t - k) // 2))
    for t in range(head):
        alone(t)
    with eng.Fori(head // 2, tiles // 2) as j:
        uses = {}
        for a in range(2):
            for k, step in enumerate(steps):
                back = (a - k) // 2
                if back not in uses:
                    uses[back] = Use(eng, j + back if back else j)
                step(2 * j + (a - k) if a != k else 2 * j, (a - k) % 2, uses[back])
    for t in range(tiles, total + lag):
        alone(t)


def each_tile(eng, body, tiles=100, total=None):
    stages(eng, [body], tiles, total)


def two_stages(eng, first, second, tiles=100, total=None):
    stages(eng, [first, second], tiles, total)


def col(t):
    return t if isinstance(t, slice) else bass.ds(t, 1)


class Phase:

    def __init__(self, nc, name):
        self.nc, self.name = nc, name
        self.ctx = ExitStack()
        self.sems = []

    def sb(self, name, shape, dt=F32):
        return self.ctx.enter_context(self.nc.sbuf_tensor(f"{self.name}_{name}", shape, dt))

    def ps(self, name, shape, dt=F32):
        return self.ctx.enter_context(self.nc.psum_tensor(f"{self.name}_{name}", shape, dt))

    def sem(self, name):
        s = self.nc.alloc_semaphore(f"{self.name}_{name}")
        self.sems.append(s)
        return s

    def pair(self, name):
        return [self.sem(f"{name}0"), self.sem(f"{name}1")]

    def end(self):
        self.nc.clear_and_free_semaphores(self.sems)
        self.nc.all_engine_barrier()
        self.ctx.close()


def load_rows(eng, dst, src, sem):
    for a, n in CUTS:
        eng.dma_start(dst[a:a + n], src[a:a + n]).then_inc(sem, 16)


class Rows:

    def __init__(self, ph, pool, rows):
        self.pool, self.bound, self.started = pool, pool.to_reg(rows - 1), ph.sem("started")

    def after_wait(self):
        self.pool.sem_inc(self.started, 1)

    def gather(self, out, table, index, sem):
        self.after_wait()
        self.pool.indirect_dma_start(out, None, table, bass.IndirectOffsetOnAxis(index, 0)).then_inc(sem, 16)

    def scatter(self, table, index, rows, sem):
        self.after_wait()
        self.pool.indirect_dma_start(table, bass.IndirectOffsetOnAxis(index, 0), rows, None,
                                     bounds_check=self.bound, oob_is_err=False).then_inc(sem, 16)


def setup(nc, env, d):
    ph = Phase(nc, "setup")
    s_dma, s_g, s_g2, s_v = ph.sem("dma"), ph.sem("masks"), ph.sem("iota"), ph.sem("steps")
    s_w = ph.sem("wrow")
    iota_i = ph.sb("iota_i", [128, 256], I32)
    keys = ph.sb("keys", [P, 2, T], I32)
    keyp = ph.sb("keyp", [P, 2, T], I32)
    wts = ph.sb("wts", [P, T])
    attr = ph.sb("attr", [P, T, H2])
    arow = ph.sb("arow", [128, 4, F])
    prod = ph.sb("prod", [128, KH, F])
    rest, part = ph.sb("rest", [3, F]), ph.sb("part", [3, F], BF16)
    w_gat, w_self = env["w_gat"], env["w_self"]
    loads = [
        (keys[:, 0, :], d["src"].rearrange("(p t) -> p t", p=P)),
        (keys[:, 1, :], d["dst"].rearrange("(p t) -> p t", p=P)),
        (wts[:, :], d["edge_weight"].rearrange("(p t) -> p t", p=P)),
        (attr[:, :, :], d["edge_attr_8"].rearrange("(p t) h -> p t h", p=P)),
        (env["onep"][:, :], d["L0_gnn_eps"].rearrange("(o n) -> o n", o=1).broadcast_to([128, 1])),
        (env["bias_all"][:, :], d["L3_gnn_bias"].rearrange("(o n) -> o n", o=1).broadcast_to([128, F])),
        (w_gat[:, :, 0:F], d["W_gat"].rearrange("(k p) n -> p k n", p=128)),
        (w_self[:, :, 0:F], d["L3_gnn_W"].rearrange("(k p) n -> p k n", p=128)),
        (env["w_kv"][:, :, 0:F], d["WkT"].rearrange("(k p) n -> p k n", p=128)),
        (env["w_kv"][:, :, F:2 * F], d["WvT"].rearrange("(k p) n -> p k n", p=128)),
    ]
    for name, src in (("w1", "L0_gnn_W1"), ("w2", "L0_gnn_W2"), ("w_q", "WqT"), ("w_o", "WoT")):
        loads.append((env[name][:, :, :], d[src].rearrange("(k p) n -> p k n", p=128)))
    for n, src in enumerate(("L0_gnn_b1", "L0_gnn_g1", "L0_gnn_be1", "L0_gnn_b2", "L0_gnn_g2", "L0_gnn_be2")):
        for k in range(KH):
            loads.append((env["bn"][:, n, k:k + 1], d[src].rearrange("(k p o) -> k p o", p=128, o=1)[k]))
    for n, src in enumerate(("a_src", "a_dst", "att_src", "att_dst")):
        loads.append((arow[:, n, :], d[src].rearrange("(o n) -> o n", o=1).broadcast_to([128, F])))

    with nc.Block() as block:
        @block.sync
        def _(sp):
            for dst, src in loads:
                sp.dma_start(dst, src).then_inc(s_dma, 16)

        @block.gpsimd
        def _(pool):
            pool.iota(iota_i[:, :], [[1, 256]], base=0, channel_multiplier=0).then_inc(s_g2, 1)
            pool.memset(env["ident"][:, :], 0.0).then_inc(s_g, 1)
            pool.memset(env["before"][:, :], 1.0).then_inc(s_g, 1)
            pool.memset(env["after"][:, :], 1.0).then_inc(s_g, 1)
            pool.memset(env["ones"][:, :], 1.0).then_inc(s_g, 1)
            pool.memset(env["zrow"][:, :], 0.0).then_inc(s_g, 1)
            pool.memset(env["zcol"][:, :], 0.0).then_inc(s_g, 1)
            pool.memset(env["zwide"][:, :], 0.0).then_inc(s_g, 1)
            pool.memset(env["minus1"][:, :], -1.0).then_inc(s_g, 1)
            pool.wait_ge(s_g, 8)
            pool.affine_select(out=env["ident"][:, :], in_=env["ident"][:, :], compare_op=ALU.not_equal, fill=1.0,
                               base=0, pattern=[[-1, 128]], channel_multiplier=1).then_inc(s_g, 1)
            pool.affine_select(out=env["before"][:, :], in_=env["before"][:, :], compare_op=ALU.is_gt, fill=0.0,
                               base=0, pattern=[[-1, 128]], channel_multiplier=1).then_inc(s_g, 1)
            pool.affine_select(out=env["after"][:, :], in_=env["after"][:, :], compare_op=ALU.is_gt, fill=0.0,
                               base=0, pattern=[[1, 128]], channel_multiplier=-1).then_inc(s_g, 1)

        @block.vector
        def _(dve):
            ch = Chain(dve, s_v)
            dve.wait_ge(s_g2, 1)
            dve.wait_ge(s_g, 11)
            ch.step(dve.tensor_copy(env["iota_row"][:, :], iota_i[:, :]))
            ch.step(dve.tensor_copy(env["ident_bf"][:, :], env["ident"][:, :]))
            dve.wait_ge(s_dma, 16 * len(loads))
            rec = env["rec"]
            for k in range(2):
                ch.step(dve.tensor_copy(rec[:, :, k], keys[:, k, :]))
                ch.step(dve.tensor_copy(env["keyf"][:, k, :], keys[:, k, :]))
            ch.step(dve.tensor_copy(rec[:, :, 2], wts[:, :]))
            ch.step(dve.memset(rec[:, :, 3], 0.0))
            ch.step(dve.tensor_copy(rec[:, :, 4:12], attr[:, :, :]))
            ch.step(dve.tensor_scalar(keyp[:, :, :], keys[:, :, :], 8, None, ALU.logical_shift_right))
            ch.step(dve.tensor_copy(env["digit"][:, 0, :, :], keyp[:, :, :]))
            ch.step(dve.tensor_scalar(keyp[:, :, :], keys[:, :, :], 255, None, ALU.bitwise_and))
            ch.step(dve.tensor_copy(env["digit"][:, 1, :, :], keyp[:, :, :]))
            ch.step(dve.tensor_scalar(env["onep"][:, :], env["onep"][:, :], 1.0, None, ALU.add))
            ch.step(dve.tensor_scalar(env["bias_all"][:, :], env["bias_all"][:, :], 1.0, None, ALU.add))
            ch.step(dve.memset(env["one3"][:, :], 1.0))
            ch.step(dve.tensor_copy(rest[:, :], env["bias_all"][0:3, :]))
            for n in range(3):
                ch.step(dve.tensor_copy(part[:, :], rest[:, :]))
                ch.step(dve.tensor_tensor(rest[:, :], rest[:, :], part[:, :], ALU.subtract))
                ch.step(dve.tensor_scalar(part[:, :], part[:, :], env["ident"][0:3, n:n + 1], None, ALU.mult))
                ch.step(dve.tensor_copy(env["bias3"][:, :], part[:, :]) if n == 0 else
                        dve.tensor_tensor(env["bias3"][:, :], env["bias3"][:, :], part[:, :], ALU.add))
            for w, n, out in ((w_gat, 1, w_gat[:, :, F:F + 4]), (w_gat, 0, env["w_gat_s"][:, :, :]),
                              (w_self, 2, w_self[:, :, F:F + 4]), (w_self, 3, w_self[:, :, F + 4:F + 8])):
                for k in range(KH):
                    ch.step(dve.tensor_tensor(prod[:, k, :], w[:, k, 0:F], arow[:, n, :], ALU.mult))
                    ch.step(dve.tensor_reduce(out[:, k, :], prod[:, k, :].rearrange("p (h c) -> p h c", h=4), X, ALU.add))
    ph.end()


def histogram(nc, env):
    ph = Phase(nc, "hist")
    hot = ph.sb("hot", [P, 2, 2, 2, 256], BF16)
    count = ph.sb("count", [128, 2, 2, 256])
    incl = ph.sb("incl", [128, 2, 2, 256])
    tot = ph.sb("tot", [128, 4])
    ones = ph.sb("ones", [128, 256])
    full = ph.sb("full", [128, 128])
    offs = ph.sb("offs", [128, 4])
    acc = ph.ps("acc", [128, 2, 512])
    off = ph.ps("off", [128, 512])
    s_hot, s_used = ph.pair("hot"), ph.pair("used")
    s_v, s_all, s_tot, s_off, s_one = ph.sem("steps"), ph.sem("counted"), ph.sem("totals"), ph.sem("offsets"), ph.sem("ones")
    base = env["base"]

    with nc.Block() as block:
        @block.vector
        def _(dve):
            dve.memset(ones[:, :], 1.0).then_inc(s_one, 1)
            dve.memset(full[:, :], 1.0).then_inc(s_one, 1)

            def tile(t, s, use):
                dve.wait_ge(s_used[s], use.free)
                for digit in range(2):
                    for key in range(2):
                        dve.tensor_scalar(hot[:, s, digit, key, :], env["iota_row"][0:P, :],
                                          env["digit"][:, digit, key, col(t)], None, ALU.is_equal).then_inc(s_hot[s], 1)
            with dve.Fori(0, T // 2) as j:
                use = Use(dve, j)
                for s in range(2):
                    tile(2 * j + s, s, use)
            ch = Chain(dve, s_v)
            dve.wait_ge(s_one, 2)
            dve.wait_ge(s_all, 1)
            ch.step(dve.tensor_copy(count[:, :, :, :], acc[:, :, :].rearrange("p k (h n) -> p k h n", h=2)))
            for key in range(2):
                for half in range(2):
                    ch.step(dve.tensor_tensor_scan(incl[:, key, half, :], ones[:, :], count[:, key, half, :],
                                                   0.0, ALU.mult, ALU.add))
            ch.step(dve.tensor_copy(tot[:, :].rearrange("p (k h) -> p k h", k=2), incl[:, :, :, 255]))
            dve.tensor_tensor(base[:, :, :, :], incl[:, :, :, :], count[:, :, :, :], ALU.subtract).then_inc(s_tot, 1)
            dve.wait_ge(s_off, 1)
            ch.step(dve.tensor_copy(offs[:, :], off[:, 0:4]))
            dve.wait_ge(s_tot, 1)
            for key in range(2):
                for half in range(2):
                    ch.step(dve.tensor_scalar(base[:, key, half, :], base[:, key, half, :],
                                              offs[:, 2 * key + half:2 * key + half + 1], None, ALU.add))

        @block.tensor
        def _(pe):
            for key in range(2):
                pe.matmul(acc[:, key, :], env["ident_bf"][:, :], env["zrow"][:, :], start=True, stop=True)
            with pe.Fori(0, T // 2) as j:
                ready = pe.snap(4 * j + 4)
                for s in range(2):
                    pe.wait_ge(s_hot[s], ready)
                    for key in range(2):
                        for half in range(2):
                            mm = pe.matmul(acc[:, key, 256 * half:256 * half + 256],
                                           hot[:, s, 0, key, 128 * half:128 * half + 128], hot[:, s, 1, key, :],
                                           start=False, stop=True, skip_group_check=True)
                    mm.then_inc(s_used[s], 1)
            mm = pe.matmul(acc[:, 1, :], env["ident_bf"][:, :], env["zrow"][:, :], start=False, stop=True,
                           skip_group_check=True)
            mm.then_inc(s_all, 1)
            pe.wait_ge(s_one, 2)
            pe.wait_ge(s_tot, 1)
            for key in range(2):
                pe.matmul(off[:, 2 * key:2 * key + 1], env["after"][:, :], tot[:, 2 * key:2 * key + 1], start=True, stop=True)
                pe.matmul(off[:, 2 * key + 1:2 * key + 2], env["after"][:, :], tot[:, 2 * key + 1:2 * key + 2],
                          start=True, stop=False)
                mm = pe.matmul(off[:, 2 * key + 1:2 * key + 2], full[:, :], tot[:, 2 * key:2 * key + 1],
                               start=False, stop=True)
            mm.then_inc(s_off, 1)
    ph.end()


def rank(nc, env, d):
    ph = Phase(nc, "rank")
    hot = ph.sb("hot", [P, RING, 2, 2, 256], BF16)
    keyb = ph.sb("keyb", [P, RING, 2, 128])
    hotT = ph.sb("hotT", [128, RING, 2, 2, P])
    table = ph.sb("table", [128, RING, 2, 2, 256])
    junk = ph.sb("junk", [P, 4, 256])
    parts = ph.sb("parts", [P, RING, 2, 2])
    place = ph.sb("place", [P, RING, 2], I32)
    recs = ph.sb("recs", [P, RING, RC])
    keyf = env["keyf"]
    xin = ph.sb("xin", [P, 2, 4, F])
    xc = ph.sb("xc", [P, 2, 4, F + 4])
    tab = ph.ps("tab", [128, 2, 512])
    look = ph.ps("look", [P, 2, 2, 256])
    rows = ph.ps("rows", [128, 4, 128])
    hT = ph.ps("hT", [128, 4, 2, 128], BF16)
    gram = env["gram"]
    s_x, s_h = ph.pair("x"), ph.pair("h_stored")
    s_scat, s_scat2 = ([ph.sem(f"{n}{k}") for k in range(RING)] for n in ("scattered_a", "scattered_b"))
    (s_hot, s_keyb, s_tab, s_hotT, s_count, s_turn, s_look, s_same, s_found, s_place, s_xc, s_gr, s_seed, s_one) = (
        ph.sem(n) for n in ("hot", "keyb", "table", "hotT", "counted", "transposed", "looked", "same_before", "found",
                            "place", "xc", "gram", "seed", "ones"))
    x_v = d["x"].rearrange("(c p j) f -> c p j f", p=P, j=4)
    h_v = env["H"].rearrange("(c p j) f -> c p j f", p=P, j=4)

    with nc.Block() as block:
        @block.sync
        def _(sp):
            def load(at):
                s = at.slot(2)
                wait(sp, s_xc, at.count(1, -1))
                for a, n in CUTS:
                    sp.dma_start(xin[a:a + n, s, :, :], x_v[at.col, a:a + n, :, :].rearrange("o p j f -> (o p) j f")).then_inc(s_x[s], 16)

            def store(at):
                s = at.slot(2)
                sp.wait_ge(s_xc, at.count(1, 1))
                for a, n in CUTS:
                    sp.dma_start(h_v[at.col, a:a + n, :, :].rearrange("o p j f -> (o p) j f"), xc[a:a + n, s, :, 0:F]).then_inc(s_h[s], 16)
            run_stages(sp, [(2, store), (0, load)], NCH)
            for s in range(2):
                sp.wait_ge(s_h[s], 32 * (NCH // 2))

        @block.scalar
        def _(act):
            act.preload_act_table_set("natural_log_exp_and_others")
            act.wait_ge(s_seed, 1)
            act.wait_ge(s_one, 2)

            def copy_table(at):
                s = at.slot(RING)
                wait(act, s_count, at.count(1))
                wait(act, s_look, at.count(1, 1 - RING))
                act.copy(table[:, s, :, :, :].rearrange("p k h n -> p k (h n)"), tab[:, :, :]).then_inc(s_tab, 1)

            def copy_hot(at):
                s = at.slot(RING)
                act.wait_ge(s_turn, at.count(1, 1))
                wait(act, s_look, at.count(1, 1 - RING))
                act.copy(hotT[:, s, :, :, :].rearrange("p k h n -> p (k h) n"), hT[:, :, 0, 0:P]).then_inc(s_hotT, 1)

            def scale(at):
                s = at.slot(2)
                act.wait_ge(s_x[s], at.uses(2, 32, 32))
                wait(act, s_h[s], at.uses(2, 32))
                wait(act, s_gr, at.count(1, -1))
                act.activation(xc[:, s, :, 0:F], xin[:, s, :, :], ACT.Copy, scale=env["onep"][0:P, :]).then_inc(s_xc, 1)
            run_stages(act, [(1, copy_table), (1, copy_hot), (0, scale)], T)

        @block.vector
        def _(dve):
            for s in range(2):
                dve.memset(xc[:, s, :, F:F + 4], 1.0).then_inc(s_one, 1)

            def one_hot(at):
                s = at.slot(RING)
                wait(dve, s_count, at.count(1, 1 - RING))
                wait(dve, s_turn, at.count(1, 1 - RING))
                wait(dve, s_found, at.count(2, 2 - 2 * RING))
                for digit in range(2):
                    for key in range(2):
                        dve.tensor_scalar(hot[:, s, digit, key, :], env["iota_row"][0:P, :],
                                          env["digit"][:, digit, key, at.col], None, ALU.is_equal).then_inc(s_hot, 1)
                for key in range(2):
                    dve.tensor_copy(keyb[:, s, key, :], keyf[:, key, at.col].broadcast_to([P, 128])).then_inc(s_keyb, 1)

            def same_before(at):
                s = at.slot(RING)
                dve.wait_ge(s_turn, at.count(1, 1))
                wait(dve, s_same, at.count(2))
                wait(dve, s_place, at.count(2, 2 - 2 * RING))
                for key in range(2):
                    dve.scalar_tensor_tensor(out=junk[:, key, 0:P], in0=rows[0:P, key, 0:P], scalar=keyf[:, key, at.col],
                                             in1=env["before"][0:P, 0:P], op0=ALU.is_equal, op1=ALU.mult,
                                             accum_out=parts[:, s, key, 0:1]).then_inc(s_same, 1)

            def find(at):
                s, b = at.slot(RING), at.slot(2)
                dve.wait_ge(s_look, at.count(1, 1))
                wait(dve, s_found, at.count(2))
                for key in range(2):
                    dve.scalar_tensor_tensor(out=junk[:, 2 + key, :], in0=look[:, b, key, :], scalar=1.0, in1=hot[:, s, 1, key, :],
                                             op0=ALU.mult, op1=ALU.mult, accum_out=parts[:, s, key, 1:2]).then_inc(s_found, 1)

            def places(at):
                s = at.slot(RING)
                dve.wait_ge(s_found, at.count(2, 2))
                dve.wait_ge(s_same, at.count(2, 2))
                wait(dve, s_scat[s], at.uses(RING, 16))
                wait(dve, s_scat2[s], at.uses(RING, 16))
                dve.tensor_tensor(place[:, s, :], parts[:, s, :, 0], parts[:, s, :, 1], ALU.add).then_inc(s_place, 1)
                dve.tensor_copy(recs[:, s, :], env["rec"][:, at.col, :].rearrange("p o r -> p (o r)")).then_inc(s_place, 1)
            run_stages(dve, [(3, find), (0, one_hot), (3, places), (1, same_before)], T)

        @block.tensor
        def _(pe):
            for key in range(2):
                mm = pe.matmul(tab[:, key, :], env["ident"][:, :], env["base"][:, key, :, :].rearrange("p h n -> p (h n)"),
                               start=True, stop=True)
            mm.then_inc(s_seed, 1)
            for m in range(KH):
                pe.matmul(gram[:, m, 0:F + 1], env["zcol"][:, :], env["zwide"][:, 0:F + 1], start=True, stop=True)

            def turn(at):
                s = at.slot(RING)
                pe.wait_ge(s_hot, at.count(4, 4))
                pe.wait_ge(s_keyb, at.count(2, 2))
                wait(pe, s_same, at.count(2))
                wait(pe, s_hotT, at.count(1))
                for key in range(2):
                    for half in range(2):
                        pe.transpose(hT[:, 2 * key + half, 0, 0:P], hot[:, s, 0, key, 128 * half:128 * half + 128], env["ident_bf"][0:P, 0:P])
                    mm = pe.transpose(rows[:, key, 0:P], keyb[:, s, key, :], env["ident"][0:P, 0:P])
                mm.then_inc(s_turn, 1)

            def find(at):
                s, b = at.slot(RING), at.slot(2)
                pe.wait_ge(s_hotT, at.count(1, 1))
                wait(pe, s_found, at.count(2, -2))
                for key in range(2):
                    for half in range(2):
                        mm = pe.matmul(look[:, b, key, :], hotT[:, s, key, half, :], table[:, s, key, half, :],
                                       start=(half == 0), stop=(half == 1))
                mm.then_inc(s_look, 1)

            def count_in(at):
                s = at.slot(RING)
                pe.wait_ge(s_tab, at.count(1, 1))
                for key in range(2):
                    for half in range(2):
                        mm = pe.matmul(tab[:, key, 256 * half:256 * half + 256],
                                       hot[:, s, 0, key, 128 * half:128 * half + 128], hot[:, s, 1, key, :],
                                       start=False, stop=True, skip_group_check=True)
                mm.then_inc(s_count, 1)

            def moments(at):
                s = at.slot(2)
                pe.wait_ge(s_xc, at.count(1, 1))
                for j in range(4):
                    for m in range(KH):
                        mm = pe.matmul(gram[:, m, 0:F + 1], xc[:, s, j, 128 * m:128 * m + 128], xc[:, s, j, 0:F + 1],
                                       start=False, stop=True, skip_group_check=True)
                mm.then_inc(s_gr, 1)
            run_stages(pe, [(1, turn), (2, find), (1, count_in), (1, moments)], T)

        @block.gpsimd
        def _(pool):
            rows_of_edges = Rows(ph, pool, E)

            def put(at):
                s = at.slot(RING)
                pool.wait_ge(s_place, at.count(2, 2))
                for key, done in ((0, s_scat), (1, s_scat2)):
                    rows_of_edges.scatter(env["sorted"][key], place[:, s, key:key + 1], recs[:, s, :], done[s])
            run_stages(pool, [(0, put)], T)
            for s in range(RING):
                pool.wait_ge(s_scat[s], 16 * (T // RING))
                pool.wait_ge(s_scat2[s], 16 * (T // RING))
    ph.end()


def segments(nc, env):
    ph = Phase(nc, "seg")
    nxt = ph.sb("next", [P, 2, 2])
    lead = ph.sb("lead", [P, T + 1])
    ends = ph.sb("ends", [P, T])
    emit = ph.sb("emit", [P, T + 1])
    tmp = ph.sb("tmp", [P, T + 1])
    first = ph.sb("first", [P, 2, 128])
    rows = ph.ps("rows", [128, 2, 128])
    s_dma, s_v, s_m, s_t, s_n = ph.sem("loads"), ph.sem("steps"), ph.sem("minus"), ph.sem("rows"), ph.sem("first")
    with nc.Block() as block:
        @block.sync
        def _(sp):
            sp.wait_ge(s_m, 1)
            for key in range(2):
                sp.dma_start(env["srec"][key][:, :, :], env["sorted"][key].rearrange("(p t) r -> p t r", p=P)).then_inc(s_dma, 16)
                sp.dma_start(nxt[0:P - 1, key, :], env["sorted"][key].rearrange("(p t) r -> p t r", p=P)[1:P, 0, 0:2]).then_inc(s_dma, 16)

        @block.vector
        def _(dve):
            ch = Chain(dve, s_v)
            dve.memset(nxt[:, :, :], -1.0).then_inc(s_m, 1)
            dve.wait_ge(s_dma, 64)
            for key in range(2):
                r, meta = env["srec"][key], env["meta"][key]
                k = r[:, :, key]
                ch.step(dve.memset(meta["same"][:, 0:1], 0.0))
                ch.step(dve.tensor_tensor(meta["same"][:, 1:T], k[:, 1:T], k[:, 0:T - 1], ALU.is_equal))
                ch.step(dve.tensor_scalar(lead[:, 0:T], k, k[:, 0:1], None, ALU.is_equal))
                ch.step(dve.memset(lead[:, T:T + 1], 0.0))
                ch.step(dve.tensor_tensor(meta["lead_end"][:, :], lead[:, 0:T], lead[:, 1:T + 1], ALU.subtract))
                ch.step(dve.tensor_tensor(ends[:, 0:T - 1], k[:, 0:T - 1], k[:, 1:T], ALU.not_equal))
                ch.step(dve.tensor_tensor(ends[:, T - 1:T], k[:, T - 1:T], nxt[:, key, key:key + 1], ALU.not_equal))
                ch.step(dve.tensor_tensor(tmp[:, 0:T], ends[:, :], lead[:, 0:T], ALU.mult))
                ch.step(dve.tensor_tensor(emit[:, 0:T], ends[:, :], tmp[:, 0:T], ALU.subtract))
                ch.step(dve.tensor_scalar(emit[:, T:T + 1], ends[:, T - 1:T], 1.0, None, ALU.subtract))
                ch.step(dve.tensor_tensor(emit[:, T:T + 1], emit[:, T:T + 1], lead[:, T - 1:T], ALU.mult))
                ch.step(dve.tensor_scalar(emit[:, T:T + 1], emit[:, T:T + 1], 1.0, None, ALU.add))
                ch.step(dve.tensor_copy(meta["emit"][:, :], emit[:, :]))
                ch.step(dve.tensor_copy(meta["node"][:, 0:T], k))
                ch.step(dve.tensor_copy(meta["node"][:, T:T + 1], k[:, 0:1]))
                ch.step(dve.tensor_copy(meta["other"][:, 0:T], r[:, :, 1 - key]))
                ch.step(dve.tensor_scalar(tmp[:, :], emit[:, :], -float(DROP), float(DROP), ALU.mult, ALU.add))
                ch.step(dve.tensor_tensor(tmp[:, 0:T], tmp[:, 0:T], k, ALU.add))
                ch.step(dve.tensor_tensor(tmp[:, T:T + 1], tmp[:, T:T + 1], k[:, 0:1], ALU.add))
                ch.step(dve.tensor_copy(meta["write"][:, :], tmp[:, :]))
                dve.tensor_copy(first[:, key, :], k[:, 0:1].broadcast_to([P, 128])).then_inc(s_n, 1)
            dve.wait_ge(s_t, 1)
            for key in range(2):
                k = env["srec"][key][:, :, key]
                ch.step(dve.scalar_tensor_tensor(out=env["meta"][key]["carry"][:, :], in0=rows[0:P, key, 0:P], scalar=k[:, T - 1:T],
                                                 in1=env["after"][0:P, 0:P], op0=ALU.is_equal, op1=ALU.mult))

        @block.tensor
        def _(pe):
            pe.wait_ge(s_n, 2)
            for key in range(2):
                mm = pe.transpose(rows[:, key, 0:P], first[:, key, :], env["ident"][0:P, 0:P])
            mm.then_inc(s_t, 1)
    ph.end()


def gin_edges(nc, env, d):
    ph = Phase(nc, "gin")
    meta, rec, gram, carry = env["meta"][0], env["srec"][0], env["gram"], env["meta"][0]["carry"]
    gix = ph.sb("gix", [P, 2, 2], I32)
    wix = ph.sb("wix", [P, 2], I32)
    xd, xs = ph.sb("xd", [P, 2, F]), ph.sb("xs", [P, 2, F])
    msg, hs = ph.sb("msg", [P, 2, F]), ph.sb("hs", [P, 2, F])
    acc, lead = ph.sb("acc", [P, 2, F]), ph.sb("lead", [P, F])
    am, both, hrow = ph.sb("am", [P, 2, F]), ph.sb("both", [P, 2, F + 4]), ph.sb("hrow", [P, 2, F])
    cps = ph.ps("carried", [P, 512])
    s_ix, s_wx, s_d, s_s = ph.pair("index"), ph.pair("write_index"), ph.pair("dst_rows"), ph.pair("src_rows")
    s_msg, s_hs, s_v, s_out = ph.pair("message"), ph.pair("scaled"), ph.pair("steps"), ph.pair("rows_ready")
    s_gr, s_sc = ph.pair("gram"), ph.pair("scattered")
    s_init, s_c = ph.sem("init"), ph.sem("carried")
    K = 5

    with nc.Block() as block:
        @block.gpsimd
        def _(pool):
            dram = Rows(ph, pool, N)

            def fetch(t, s, use):
                pool.wait_ge(s_msg[s], use.free)
                pool.wait_ge(s_hs[s], use.free)
                pool.tensor_copy(gix[:, s, 0:1], meta["other"][:, col(t)]).then_inc(s_ix[s], 1)
                pool.tensor_copy(gix[:, s, 1:2], meta["node"][:, col(t)]).then_inc(s_ix[s], 1)
                pool.wait_ge(s_ix[s], use.base(2) + 2)
                dram.gather(xd[:, s, :], d["x"], gix[:, s, 0:1], s_d[s])
                dram.gather(xs[:, s, :], d["x"], gix[:, s, 1:2], s_s[s])

            def write(t, s, use):
                pool.wait_ge(s_out[s], use.ready)
                pool.wait_ge(s_sc[s], use.free16)
                pool.tensor_copy(wix[:, s:s + 1], meta["write"][:, col(t)]).then_inc(s_wx[s], 1)
                pool.wait_ge(s_wx[s], use.ready)
                dram.scatter(env["H"], wix[:, s:s + 1], hrow[:, s, :], s_sc[s])
            two_stages(pool, fetch, write)
            last = Use(pool, T // 2)
            pool.wait_ge(s_hs[0], last.free)
            pool.tensor_copy(gix[:, 0, 1:2], meta["node"][:, T:T + 1]).then_inc(s_ix[0], 1)
            pool.wait_ge(s_ix[0], 2 * last.u + 1)
            dram.gather(xs[:, 0, :], d["x"], gix[:, 0, 1:2], s_s[0])
            write(T, 0, last)
            pool.wait_ge(s_sc[0], 16 * (T // 2 + 1))
            pool.wait_ge(s_sc[1], 16 * (T // 2))

        @block.scalar
        def _(act):
            def scaled(t, s, use):
                act.wait_ge(s_s[s], use.ready16)
                act.wait_ge(s_out[s], use.free)
                act.activation(hs[:, s, :], xs[:, s, :], ACT.Copy, scale=env["onep"][0:P, :]).then_inc(s_hs[s], 1)

            def tile(t, s, use):
                act.wait_ge(s_d[s], use.ready16)
                act.wait_ge(s_v[s], use.base(K))
                act.activation(msg[:, s, :], xd[:, s, :], ACT.Copy, scale=rec[:, col(t), 2]).then_inc(s_msg[s], 1)
                scaled(t, s, use)
            each_tile(act, tile)
            scaled(T, 0, Use(act, T // 2))

        @block.vector
        def _(dve):
            dve.memset(acc[:, 1, :], 0.0).then_inc(s_init, 1)
            dve.memset(lead[:, :], 0.0).then_inc(s_init, 1)
            for s in range(2):
                dve.memset(both[:, s, F:F + 4], 1.0).then_inc(s_init, 1)
            dve.wait_ge(s_init, 4)

            def rows_of(ch, total, t, s, use):
                dve.wait_ge(s_gr[s], use.free)
                ch.step(dve.tensor_scalar(am[:, s, :], total, meta["emit"][:, col(t)], None, ALU.mult))
                dve.wait_ge(s_hs[s], use.ready)
                dve.wait_ge(s_sc[s], use.free16)
                ch.step(dve.tensor_tensor(hrow[:, s, :], total, hs[:, s, :], ALU.add))
                ch.step(dve.tensor_tensor(both[:, s, 0:F], hrow[:, s, :], hs[:, s, :], ALU.add))
                dve.sem_inc(s_out[s], 1)

            def tile(t, s, use):
                ch = Chain(dve, s_v[s], use.base(K))
                dve.wait_ge(s_msg[s], use.ready)
                ch.step(dve.scalar_tensor_tensor(out=acc[:, s, :], in0=acc[:, 1 - s, :], scalar=meta["same"][:, col(t)],
                                                 in1=msg[:, s, :], op0=ALU.mult, op1=ALU.add))
                ch.step(dve.scalar_tensor_tensor(out=lead[:, :], in0=acc[:, s, :], scalar=meta["lead_end"][:, col(t)],
                                                 in1=lead[:, :], op0=ALU.mult, op1=ALU.add))
                rows_of(ch, acc[:, s, :], t, s, use)
            each_tile(dve, tile)
            last = Use(dve, T // 2)
            dve.wait_ge(s_c, 1)
            ch = Chain(dve, s_v[0], K * (T // 2))
            ch.step(dve.tensor_tensor(acc[:, 0, :], cps[:, 0:F], lead[:, :], ALU.add))
            rows_of(ch, acc[:, 0, :], T, 0, last)

        @block.tensor
        def _(pe):
            def tile(t, s, use):
                pe.wait_ge(s_out[s], use.ready)
                for m in range(KH):
                    mm = pe.matmul(gram[:, m, 0:F + 1], am[:, s, 128 * m:128 * m + 128], both[:, s, 0:F + 1],
                                   start=False, stop=True, skip_group_check=True)
                mm.then_inc(s_gr[s], 1)
            each_tile(pe, tile)
            pe.matmul(cps[:, 0:F], carry[:, :], acc[:, 1, :], start=True, stop=True).then_inc(s_c, 1)
            tile(T, 0, Use(pe, T // 2))
    ph.end()


def rsqrt(act, ch, out, tmp, in_):
    ch.step(act.activation(tmp, in_, ACT.Ln))
    ch.step(act.activation(out, tmp, ACT.Exp, scale=-0.5))


def moments(nc, env):
    ph = Phase(nc, "mom")
    g = ph.sb("g", [128, KH, F + 4])
    z = ph.sb("z", [128, KH, F])
    cols = ph.sb("cols", [128, 12, KH])
    zp, cp = ph.ps("zp", [128, KH, 512]), ph.ps("cp", [128, 512])
    s_v, s_z, s_q, s_a, s_w = ph.sem("steps"), ph.sem("z"), ph.sem("sums"), ph.sem("rsqrt"), ph.sem("var")
    s_g = ph.sem("gram")
    w1 = env["w1"]
    with nc.Block() as block:
        @block.vector
        def _(dve):
            ch = Chain(dve, s_v)
            ch.step(dve.tensor_copy(g[:, :, 0:F + 1], env["gram"][:, :, 0:F + 1]))
            dve.sem_inc(s_g, 1)
            dve.wait_ge(s_z, 1)
            ch.step(dve.tensor_tensor(z[:, :, :], zp[:, :, 0:F], w1[:, :, :], ALU.mult))
            dve.sem_inc(s_g, 1)
            dve.wait_ge(s_q, 1)
            ch.step(dve.tensor_scalar(cols[:, 0:2, :], cp[:, 0:4].rearrange("p (a m) -> p a m", a=2), 1.0 / N, None, ALU.mult))
            ch.step(dve.tensor_tensor(cols[:, 2, :], cols[:, 0, :], cols[:, 0, :], ALU.mult))
            ch.step(dve.tensor_tensor(cols[:, 3, :], cols[:, 1, :], cols[:, 2, :], ALU.subtract))
            ch.step(dve.tensor_scalar(cols[:, 3, :], cols[:, 3, :], EPS, None, ALU.add))
            dve.sem_inc(s_w, 1)
            dve.wait_ge(s_a, 2)
            scale_shift(dve, ch, env, cols, 0)

        @block.scalar
        def _(act):
            ch = Chain(act, s_a)
            act.wait_ge(s_w, 1)
            rsqrt(act, ch, cols[:, 5, :], cols[:, 4, :], cols[:, 3, :])

        @block.tensor
        def _(pe):
            pe.wait_ge(s_g, 1)
            for m in range(KH):
                for k in range(KH):
                    mm = pe.matmul(zp[:, m, 0:F], g[:, k, 128 * m:128 * m + 128], w1[:, k, :], start=(k == 0), stop=(k == 1))
            mm.then_inc(s_z, 1)
            pe.wait_ge(s_g, 2)
            for m in range(KH):
                for k in range(KH):
                    pe.matmul(cp[:, m:m + 1], w1[:, k, 128 * m:128 * m + 128], g[:, k, F:F + 1], start=(k == 0), stop=(k == 1))
                for k in range(KH):
                    mm = pe.matmul(cp[:, 2 + m:3 + m], z[:, k, 128 * m:128 * m + 128], env["ones"][:, 0:1],
                                   start=(k == 0), stop=(k == 1))
            mm.then_inc(s_q, 1)
    ph.end()


def scale_shift(dve, ch, env, cols, layer):
    bn, out = env["bn"], env["affine"]
    b, gamma, beta = bn[:, 3 * layer, :], bn[:, 3 * layer + 1, :], bn[:, 3 * layer + 2, :]
    ch.step(dve.tensor_tensor(out[:, 2 * layer, :], cols[:, 5, :], gamma, ALU.mult))
    ch.step(dve.tensor_tensor(cols[:, 6, :], cols[:, 0, :], b, ALU.add))
    ch.step(dve.tensor_tensor(cols[:, 7, :], b, cols[:, 6, :], ALU.subtract))
    ch.step(dve.tensor_tensor(cols[:, 8, :], cols[:, 7, :], out[:, 2 * layer, :], ALU.mult))
    ch.step(dve.tensor_tensor(out[:, 2 * layer + 1, :], cols[:, 8, :], beta, ALU.add))


class At:

    def __init__(self, turn, unroll, a):
        self.turn, self.unroll, self.a = turn, unroll, a

    def count(self, per=1, plus=0):
        if isinstance(self.turn, int):
            return per * (self.turn * self.unroll + self.a) + plus
        return self.turn * (per * self.unroll) + (per * self.a + plus)

    def slot(self, ring):
        return self.a % ring

    def uses(self, ring, per=1, plus=0):
        if isinstance(self.turn, int):
            return per * ((self.turn * self.unroll + self.a) // ring) + plus
        return self.turn * (per * self.unroll // ring) + (per * (self.a // ring) + plus)

    @property
    def col(self):
        return bass.ds(self.count(), 1)

    @property
    def is_lead(self):
        return isinstance(self.turn, int) and self.turn * self.unroll + self.a == T


def wait(eng, sem, value):
    if not (isinstance(value, int) and value <= 0):
        eng.wait_ge(sem, value)


RING = 4


def run_stages(eng, steps, total, tiles=100, unroll=RING, behind=4):
    most = max(lag for lag, _ in steps)
    head = unroll * -(-(most + behind) // unroll)
    for t in range(head):
        for lag, step in steps:
            if 0 <= t - lag < total:
                step(At(0, unroll, t - lag))
    with eng.Fori(head // unroll, tiles // unroll) as turn:
        for a in range(unroll):
            for lag, step in steps:
                step(At(turn, unroll, a - lag))
    for t in range(tiles, total + most):
        for lag, step in steps:
            if 0 <= t - lag < total:
                step(At(0, unroll, t - lag))


def bn_rows(dve, ch, hold, stats, mv, rows):
    groups = rows.shape[1]
    for j in range(groups):
        ch.go(dve.bn_stats(stats[:, j, :], rows[:, j, :]))
    ch.done()
    dve.sem_inc(hold, 1)
    for j in range(groups):
        ch.go(dve.bn_aggr(mv[:, j, :], stats[:, j, :]))
    ch.done()




def mlp(nc, env):
    ph = Phase(nc, "mlp")
    h = ph.sb("h", [P, 2, 4, F])
    hT = ph.sb("hT", [128, 2, KH, CH])
    r = ph.sb("r", [128, 2, KH, CH])
    y = ph.sb("y", [128, 2, KH, CH])
    stats = ph.sb("stats", [128, KH, NCH, 6])
    mv = ph.sb("mv", [128, KH, 2])
    cols = ph.sb("cols", [128, 12, KH])
    tp, y1, y2 = ph.ps("tp", [128, 2, KH, 512]), ph.ps("y1", [128, KH, 512]), ph.ps("y2", [128, KH, 512])
    s_h, s_o = ph.pair("h"), ph.pair("y2_stored")
    s_t, s_hT, s_1, s_r, s_2, s_y, s_st = (ph.sem(n) for n in ("transposed", "hT", "y1", "r", "y2", "y2_copied", "stats"))
    s_v, s_a, s_w = ph.sem("steps"), ph.sem("rsqrt"), ph.sem("var")
    w1, w2, aff = env["w1"], env["w2"], env["affine"]
    h_v = env["H"].rearrange("(c p j) f -> c p j f", p=P, j=4)

    with nc.Block() as block:
        @block.sync
        def _(sp):
            def load(at):
                s = at.slot(2)
                wait(sp, s_t, at.count(1, -1))
                for a, n in CUTS:
                    sp.dma_start(h[a:a + n, s, :, :], h_v[at.col, a:a + n, :, :].rearrange("o p j f -> (o p) j f")).then_inc(s_h[s], 16)

            def store(at):
                s = at.slot(2)
                sp.wait_ge(s_y, at.count(KH, KH))
                sp.dma_start(env["Y2"][at.col, :, :].rearrange("o p n -> (o p) n"),
                             y[:, s, :, :].rearrange("p k n -> p (k n)")).then_inc(s_o[s], 16)
            run_stages(sp, [(4, store), (0, load)], NCH, NCH, unroll=2)
            for s in range(2):
                sp.wait_ge(s_o[s], 16 * (NCH // 2))

        @block.tensor
        def _(pe):
            def turn(at):
                s = at.slot(2)
                pe.wait_ge(s_h[s], at.uses(2, 32, 32))
                wait(pe, s_hT, at.count(KH, -KH))
                for k in range(KH):
                    for j in range(4):
                        mm = pe.transpose(tp[:, s, k, P * j:P * j + P], h[:, s, j, 128 * k:128 * k + 128], env["ident"][0:P, 0:P])
                mm.then_inc(s_t, 1)

            def first(at):
                s = at.slot(2)
                pe.wait_ge(s_hT, at.count(KH, KH))
                wait(pe, s_r, at.count(KH))
                for m in range(KH):
                    for k in range(KH):
                        mm = pe.matmul(y1[:, m, 0:CH], w1[:, k, 128 * m:128 * m + 128], hT[:, s, k, :],
                                       start=(k == 0), stop=(k == 1))
                    mm.then_inc(s_1, 1)

            def second(at):
                s = at.slot(2)
                pe.wait_ge(s_r, at.count(KH, KH))
                wait(pe, s_y, at.count(KH))
                for m in range(KH):
                    for k in range(KH):
                        mm = pe.matmul(y2[:, m, 0:CH], w2[:, k, 128 * m:128 * m + 128], r[:, s, k, :],
                                       start=(k == 0), stop=(k == 1))
                    mm.then_inc(s_2, 1)
            run_stages(pe, [(0, turn), (2, second), (1, first)], NCH, NCH, unroll=2)

        @block.scalar
        def _(act):
            def copy_out(at):
                s = at.slot(2)
                wait(act, s_o[s], at.uses(2, 16))
                wait(act, s_st, at.count(KH, -KH))
                for m in range(KH):
                    act.wait_ge(s_2, at.count(KH, m + 1))
                    act.copy(y[:, s, m, :], y2[:, m, 0:CH]).then_inc(s_y, 1)

            def relu(at):
                s = at.slot(2)
                wait(act, s_2, at.count(KH, -KH))
                for m in range(KH):
                    act.wait_ge(s_1, at.count(KH, m + 1))
                    act.activation(r[:, s, m, :], y1[:, m, 0:CH], ACT.Relu, bias=aff[:, 1, m:m + 1],
                                   scale=aff[:, 0, m:m + 1]).then_inc(s_r, 1)
            run_stages(act, [(2, copy_out), (1, relu)], NCH, NCH, unroll=2)
            ch = Chain(act, s_a)
            act.wait_ge(s_w, 1)
            rsqrt(act, ch, cols[:, 5, :], cols[:, 4, :], cols[:, 3, :])

        @block.vector
        def _(dve):
            def copies(at):
                s = at.slot(2)
                dve.wait_ge(s_t, at.count(1, 1))
                wait(dve, s_1, at.count(KH, -KH))
                for k in range(KH):
                    dve.tensor_copy(hT[:, s, k, :], tp[:, s, k, 0:CH]).then_inc(s_hT, 1)

            def stat(at):
                s = at.slot(2)
                for m in range(KH):
                    dve.wait_ge(s_y, at.count(KH, m + 1))
                    dve.bn_stats(stats[:, m, at.col, :].rearrange("p o n -> p (o n)"), y[:, s, m, :]).then_inc(s_st, 1)
            run_stages(dve, [(3, stat), (0, copies)], NCH, NCH, unroll=2)
            ch = Chain(dve, s_v)
            dve.wait_ge(s_st, KH * NCH)
            for m in range(KH):
                ch.step(dve.bn_aggr(mv[:, m, :], stats[:, m, :, :].rearrange("p c n -> p (c n)")))
            ch.step(dve.tensor_copy(cols[:, 0, :], mv[:, :, 0]))
            ch.step(dve.tensor_scalar(cols[:, 3, :], mv[:, :, 1], EPS, None, ALU.add))
            dve.sem_inc(s_w, 1)
            dve.wait_ge(s_a, 2)
            scale_shift(dve, ch, env, cols, 1)
    ph.end()


def nodes(nc, env, d):
    ph = Phase(nc, "nodes")
    J, HC, LONG = 2, CH // 2, 2 * RING
    y, z = ph.sb("y", [128, 2, KH, CH]), ph.sb("z", [128, RING, KH, HC])
    x, u = ph.sb("x", [P, RING, J, F]), ph.sb("u", [P, RING, J, F])
    x1, x2 = (ph.sb(n, [P, RING, J, F]) for n in ("x1", "x2"))
    x3 = ph.sb("x3", [P, LONG, J, F])
    x3T, ex = ph.sb("x3T", [128, RING, KH, HC]), ph.sb("exp", [P, RING, J, F])
    el, v, out = ph.sb("elu", [P, RING, J, F]), ph.sb("v", [P, RING, J, F]), ph.sb("out", [P, RING, J, F])
    st, mv = ph.sb("stats", [P, RING, J, 6]), ph.sb("mv", [P, RING, J, 2])
    q, lnq, r, nm = (ph.sb(n, [P, RING, 3, J]) for n in ("q", "lnq", "r", "nm"))
    st2, mv2 = ph.sb("stats2", [P, RING, J, 6]), ph.sb("mv2", [P, RING, J, 2])
    q2, lnq2, r2 = (ph.sb(n, [P, RING, J]) for n in ("q2", "lnq2", "r2"))
    zp, tp, xp = ph.ps("zp", [P, 2, J, F]), ph.ps("tp", [128, 2, KH, 256]), ph.ps("xp", [P, 2, J, F])
    s_y, s_x, o_1, o_2, o_o = (ph.pair(n) for n in ("y_loaded", "x_loaded", "x1_stored", "x2_stored", "out_stored"))
    (s_z, s_zp, s_u, s_q, s_r, s_nm, s_x1, s_x2, s_x3, s_t3, s_c3, s_xp, s_ex, s_el, s_v, s_q2, s_r2, s_out) = (
        ph.sem(n) for n in ("z", "zp", "u", "q", "r", "nm", "x1", "x2", "x3", "x3T", "x3T_copied", "xp", "exp", "elu", "v", "q2", "r2", "out"))
    c_a, c_b, c_ra, c_rb, s_hold, s_hold_p = (ph.sem(n) for n in ("steps_a", "steps_b", "rsqrt_a", "rsqrt_b", "hold", "hold_pool"))
    aff, w_self = env["affine"], env["w_self"]
    x_v, x1_v, x2_v, out_v = (a.rearrange("(c p j) f -> c p j f", p=P, j=4) for a in (d["x"], env["X1"], env["X2"], d["out"]))
    tiles = 2 * NCH

    with nc.Block() as block:
        @block.sync
        def _(sp):
            def load(at):
                c = at.slot(2)
                wait(sp, s_z, at.count(4, 4 - 8))
                sp.dma_start(y[:, c, :, :].rearrange("p k n -> p (k n)"),
                             env["Y2"][at.col, :, :].rearrange("o p n -> (o p) n")).then_inc(s_y[c], 16)
                wait(sp, s_u, at.count(2, 2 - 4))
                for a, n in CUTS:
                    sp.dma_start(x[a:a + n, 2 * c:2 * c + 2, :, :].rearrange("p h j f -> p (h j) f"),
                                 x_v[at.col, a:a + n, :, :].rearrange("o p j f -> (o p) j f")).then_inc(s_x[c], 16)

            def put(dst, at, src, sem):
                c = at.slot(2)
                for a, n in CUTS:
                    sp.dma_start(dst[at.col, a:a + n, :, :].rearrange("o p j f -> (o p) j f"),
                                 src[a:a + n, 2 * c:2 * c + 2, :, :].rearrange("p h j f -> p (h j) f")).then_inc(sem[c], 16)

            def store(at):
                sp.wait_ge(s_x1, at.count(2 * J, 2 * J))
                put(x1_v, at, x1, o_1)
                sp.wait_ge(s_x2, at.count(2 * J, 2 * J))
                put(x2_v, at, x2, o_2)

            def store_out(at):
                sp.wait_ge(s_out, at.count(2 * J, 2 * J))
                put(out_v, at, out, o_o)
            run_stages(sp, [(8, store_out), (4, store), (0, load)], NCH, NCH, unroll=2)
            for sem in (o_1, o_2, o_o):
                for c in range(2):
                    sp.wait_ge(sem[c], 32 * (NCH // 2))

        @block.tensor
        def _(pe):
            def turn_z(at):
                s, b = at.slot(RING), at.slot(2)
                pe.wait_ge(s_z, at.count(2, 2))
                wait(pe, s_u, at.count(1, -1))
                for j in range(J):
                    for k in range(KH):
                        mm = pe.transpose(zp[:, b, j, 128 * k:128 * k + 128], z[:, s, k, P * j:P * j + P], env["ident"][:, :])
                mm.then_inc(s_zp, 1)

            def turn_x3(at):
                s, b = at.slot(RING), at.slot(2)
                pe.wait_ge(s_x3, at.count(J, J))
                wait(pe, s_c3, at.count(1, -1))
                for k in range(KH):
                    for j in range(J):
                        mm = pe.transpose(tp[:, b, k, P * j:P * j + P], x3[:, at.slot(LONG), j, 128 * k:128 * k + 128], env["ident"][0:P, 0:P])
                mm.then_inc(s_t3, 1)

            def product(at):
                s, b = at.slot(RING), at.slot(2)
                pe.wait_ge(s_c3, at.count(1, 1))
                wait(pe, s_el, at.count(1, -1))
                for j in range(J):
                    for k in range(KH):
                        pe.matmul(xp[:, b, j, :], x3T[:, s, k, P * j:P * j + P], w_self[:, k, 0:F], start=(k == 0), stop=False)
                    mm = pe.matmul(xp[:, b, j, :], env["one3"][:, 0:P], env["bias3"][:, :], start=False, stop=True)
                mm.then_inc(s_xp, 1)
            run_stages(pe, [(8, product), (6, turn_x3), (1, turn_z)], tiles, tiles, LONG, LONG)

        @block.scalar
        def _(act):
            def relu(at):
                s, c, h = at.slot(RING), at.slot(RING) // 2, at.slot(2)
                act.wait_ge(s_y[c], at.uses(RING, 16, 16))
                wait(act, s_zp, at.count(1, 1 - RING))
                for m in range(KH):
                    act.activation(z[:, s, m, :], y[:, c, m, HC * h:HC * h + HC], ACT.Relu, bias=aff[:, 3, m:m + 1],
                                   scale=aff[:, 2, m:m + 1]).then_inc(s_z, 1)

            def rsqrt1(at):
                s = at.slot(RING)
                act.wait_ge(s_q, at.count(1, 1))
                wait(act, s_x1, at.count(J, J - J * RING))
                wait(act, s_x2, at.count(J, J - J * RING))
                wait(act, s_nm, at.count(1, 1 - RING))
                ch = Chain(act, c_ra, at.count(2))
                rsqrt(act, ch, r[:, s, :, :], lnq[:, s, :, :], q[:, s, :, :])
                act.sem_inc(s_r, 1)

            def third(at):
                s = at.slot(RING)
                act.wait_ge(s_nm, at.count(1, 1))
                wait(act, s_t3, at.count(1, 1 - LONG))
                wait(act, s_v, at.count(1, 1 - LONG))
                for j in range(J):
                    act.activation(x3[:, at.slot(LONG), j, :], u[:, s, j, :], ACT.Identity, bias=nm[:, s, 2, j:j + 1],
                                   scale=r[:, s, 2, j:j + 1]).then_inc(s_x3, 1)

            def copy_x3(at):
                s, b = at.slot(RING), at.slot(2)
                act.wait_ge(s_t3, at.count(1, 1))
                wait(act, s_xp, at.count(1, 1 - RING))
                act.copy(x3T[:, s, :, :], tp[:, b, :, 0:HC]).then_inc(s_c3, 1)

            def exps(at):
                s, b = at.slot(RING), at.slot(2)
                act.wait_ge(s_xp, at.count(1, 1))
                wait(act, s_el, at.count(1, 1 - RING))
                act.activation(ex[:, s, :, :], xp[:, b, :, :], ACT.Exp, bias=env["minus1"][0:P, :]).then_inc(s_ex, 1)

            def rsqrt2(at):
                s = at.slot(RING)
                act.wait_ge(s_q2, at.count(1, 1))
                wait(act, s_out, at.count(J, J - J * RING))
                ch = Chain(act, c_rb, at.count(2))
                rsqrt(act, ch, r2[:, s, :], lnq2[:, s, :], q2[:, s, :])
                act.sem_inc(s_r2, 1)
            run_stages(act, [(12, rsqrt2), (9, exps), (7, copy_x3), (5, third), (3, rsqrt1), (0, relu)], tiles, tiles, LONG, LONG)

        @block.vector
        def _(dve):
            def moments1(at):
                s, c, b = at.slot(RING), at.slot(RING) // 2, at.slot(2)
                ch = Chain(dve, c_a, at.count(1 + 2 * J + 3))
                dve.wait_ge(s_zp, at.count(1, 1))
                dve.wait_ge(s_x[c], at.uses(RING, 32, 32))
                wait(dve, s_x1, at.count(J, J - J * RING))
                wait(dve, s_x2, at.count(J, J - J * RING))
                wait(dve, s_x3, at.count(J, J - J * RING))
                ch.step(dve.tensor_tensor(u[:, s, :, :], zp[:, b, :, :], x[:, s, :, :], ALU.add))
                dve.sem_inc(s_u, 1)
                bn_rows(dve, ch, s_hold, st[:, s, :, :], mv[:, s, :, :], u[:, s, :, :])
                wait(dve, s_r, at.count(1, 1 - RING))
                for k, (m, a) in enumerate(((1.0, EPS), (1.0 + EPS, EPS * EPS), (1.0 + EPS + EPS * EPS, EPS ** 3))):
                    ch.go(dve.tensor_scalar(q[:, s, k, :], mv[:, s, :, 1], m, a, ALU.mult, ALU.add))
                ch.done()
                dve.sem_inc(s_q, 1)

            def means(at):
                s = at.slot(RING)
                dve.wait_ge(s_r, at.count(1, 1))
                dve.scalar_tensor_tensor(out=nm[:, s, :, :], in0=r[:, s, :, :], scalar=-1.0,
                                         in1=mv[:, s, :, 0].unsqueeze(1).broadcast_to([P, 3, J]), op0=ALU.mult, op1=ALU.mult).then_inc(s_nm, 1)

            def elus(at):
                s, b = at.slot(RING), at.slot(2)
                dve.wait_ge(s_ex, at.count(1, 1))
                wait(dve, s_v, at.count(1, 1 - RING))
                dve.scalar_tensor_tensor(out=el[:, s, :, :].rearrange("p j f -> p (j f)"), in0=ex[:, s, :, :].rearrange("p j f -> p (j f)"),
                                         scalar=1.0, in1=xp[:, b, :, :].rearrange("p j f -> p (j f)"), op0=ALU.min, op1=ALU.max).then_inc(s_el, 1)

            def moments2(at):
                s = at.slot(RING)
                ch = Chain(dve, c_b, at.count(1 + 2 * J))
                dve.wait_ge(s_v, at.count(1, 1))
                bn_rows(dve, ch, s_hold, st2[:, s, :, :], mv2[:, s, :, :], v[:, s, :, :])
                wait(dve, s_r2, at.count(1, 1 - RING))
                ch.step(dve.tensor_scalar(q2[:, s, :], mv2[:, s, :, 1], EPS, None, ALU.add))
                dve.sem_inc(s_q2, 1)

            def outs(at):
                s, c = at.slot(RING), at.slot(RING) // 2
                dve.wait_ge(s_r2, at.count(1, 1))
                wait(dve, o_o[c], at.uses(RING, 32))
                for j in range(J):
                    dve.tensor_scalar(out[:, s, j, :], v[:, s, j, :], mv2[:, s, j, 0:1], r2[:, s, j:j + 1],
                                      ALU.subtract, ALU.mult).then_inc(s_out, 1)
            run_stages(dve, [(13, outs), (11, moments2), (9, elus), (4, means), (2, moments1)], tiles, tiles, LONG, LONG)

        @block.gpsimd
        def _(pool):
            def first_two(at):
                s, c = at.slot(RING), at.slot(RING) // 2
                pool.wait_ge(s_nm, at.count(1, 1))
                for k, (dst, done, stored) in enumerate(((x1, s_x1, o_1), (x2, s_x2, o_2))):
                    wait(pool, stored[c], at.uses(RING, 32))
                    pool.sem_inc(s_hold_p, 1)
                    for j in range(J):
                        pool.tensor_scalar(dst[:, s, j, :], u[:, s, j, :], r[:, s, k, j:j + 1], nm[:, s, k, j:j + 1],
                                           ALU.mult, ALU.add).then_inc(done, 1)

            def add(at):
                s = at.slot(RING)
                pool.wait_ge(s_el, at.count(1, 1))
                pool.wait_ge(s_x3, at.count(J, J))
                wait(pool, s_out, at.count(J, J - J * RING))
                pool.tensor_tensor(v[:, s, :, :], el[:, s, :, :], x3[:, at.slot(LONG), :, :], ALU.add).then_inc(s_v, 1)
            run_stages(pool, [(10, add), (5, first_two)], tiles, tiles, LONG, LONG)
    ph.end()


def gat_edges(nc, env, d):
    ph = Phase(nc, "gat")
    meta, carry = env["meta"][0], env["meta"][0]["carry"]
    w, ws, w_self = env["w_gat"], env["w_gat_s"], env["w_self"]
    HW = F + 2 * H1
    gix, wix = ph.sb("gix", [P, RING, 2], I32), ph.sb("wix", [P, RING], I32)
    xd, xs = ph.sb("xd", [P, RING, F]), ph.sb("xs", [P, RING, F])
    xT = ph.sb("xT", [128, RING, 4, P])
    low, hg, msg = ph.sb("low", [P, RING, HW]), ph.sb("hg", [P, RING, HW]), ph.sb("msg", [P, RING, F + H1])
    sc = ph.sb("scores", [P, RING, 4, H1])
    acc, lead = ph.sb("acc", [P, RING, F + H1]), ph.sb("lead", [P, F + H1])
    den, rr = ph.sb("den", [P, RING, H1]), ph.sb("rr", [P, RING, H1])
    hn, g, e1, e2 = (ph.sb(n, [P, RING, F]) for n in ("hn", "g", "e1", "e2"))
    elu, u, x2, x3 = (ph.sb(n, [P, RING, F]) for n in ("elu", "u", "x2", "x3"))
    st, mv, q, lnq, r, nm = (ph.sb(n, [P, RING, k]) for n, k in (("st", 6), ("mv", 2), ("q", 2), ("lnq", 2), ("r", 2), ("nm", 2)))
    x3T = ph.sb("x3T", [128, RING, KH, P])
    t1, ex, el, v, out = (ph.sb(n, [P, RING, F]) for n in ("t1", "ex", "el", "v", "out"))
    neg = ph.sb("neg", [P, RING, 1])
    st3, mv3, q3, lnq3, r3, nm3 = (ph.sb(n, [P, RING, k]) for n, k in (("st3", 6), ("mv3", 2), ("q3", 1), ("lnq3", 1), ("r3", 1), ("nm3", 1)))
    tp, hp = ph.ps("tp", [128, 2, 4, 128]), ph.ps("hp", [P, 2, 512])
    tp3, xp, cps = ph.ps("tp3", [128, 4, 128]), ph.ps("xp", [P, 2, 512]), ph.ps("cps", [P, 512])
    s_d, s_s = [ph.sem(f"dst_rows{k}") for k in range(RING)], [ph.sem(f"src_rows{k}") for k in range(RING)]
    s_w2, s_w3, s_wo = ([ph.sem(f"{n}{k}") for k in range(RING)] for n in ("x2_stored", "x3_stored", "out_stored"))
    names = ("index", "windex", "transposed", "xT", "projected", "scored", "weights", "msgs", "normed", "exp1", "exp2",
             "u", "q", "r", "x3", "x2", "x3_transposed", "x3T", "xp", "exp3", "t1", "v", "q3", "out")
    (s_ix, s_wx, s_t, s_xT, s_hp, s_sc, s_e4, s_msg, s_g, s_e1, s_e2, s_u, s_q, s_r, s_x3, s_x2, s_t3, s_x3T, s_xp,
     s_ex, s_t1, s_v, s_q3, s_out) = (ph.sem(n) for n in names)
    c1, c2, c3, c4, c5, ca, cb = (ph.sem(f"steps{k}") for k in range(7))
    s_init, s_c, s_hold = ph.sem("init"), ph.sem("carried"), ph.sem("hold")

    with nc.Block() as block:
        @block.gpsimd
        def _(pool):
            dram = Rows(ph, pool, N)

            def fetch(at):
                s = at.slot(RING)
                wait(pool, s_t, at.count(1, 1 - RING))
                wait(pool, s_u, at.count(1, 1 - RING))
                pool.tensor_copy(gix[:, s, 1:2], meta["node"][:, at.col]).then_inc(s_ix, 1)
                if at.is_lead:
                    pool.wait_ge(s_ix, 2 * T + 1)
                    dram.gather(xs[:, s, :], env["X1"], gix[:, s, 1:2], s_s[s])
                    return
                pool.tensor_copy(gix[:, s, 0:1], meta["other"][:, at.col]).then_inc(s_ix, 1)
                pool.wait_ge(s_ix, at.count(2, 2))
                dram.gather(xd[:, s, :], env["X1"], gix[:, s, 0:1], s_d[s])
                dram.gather(xs[:, s, :], env["X1"], gix[:, s, 1:2], s_s[s])

            def put_x(at):
                s = at.slot(RING)
                wait(pool, s_wo[s], at.uses(RING, 16))
                pool.tensor_copy(wix[:, s:s + 1], meta["write"][:, at.col]).then_inc(s_wx, 1)
                pool.wait_ge(s_wx, at.count(1, 1))
                pool.wait_ge(s_x2, at.count(1, 1))
                dram.scatter(env["X2"], wix[:, s:s + 1], x2[:, s, :], s_w2[s])
                pool.wait_ge(s_x3, at.count(1, 1))
                dram.scatter(env["X3"], wix[:, s:s + 1], x3[:, s, :], s_w3[s])

            def put_out(at):
                s = at.slot(RING)
                pool.wait_ge(s_out, at.count(1, 1))
                dram.scatter(d["out"], wix[:, s:s + 1], out[:, s, :], s_wo[s])
            run_stages(pool, [(8, put_out), (5, put_x), (0, fetch)], T + 1)
            for s in range(RING):
                for sem in (s_w2, s_w3, s_wo):
                    pool.wait_ge(sem[s], 16 * (T // RING + (s == 0)))

        @block.tensor
        def _(pe):
            def turn_rows(at):
                if at.is_lead:
                    return
                s, b = at.slot(RING), at.slot(2)
                pe.wait_ge(s_d[s], at.uses(RING, 16, 16))
                pe.wait_ge(s_s[s], at.uses(RING, 16, 16))
                wait(pe, s_xT, at.count(1, -1))
                for k in range(KH):
                    pe.transpose(tp[:, b, k, 0:P], xd[:, s, 128 * k:128 * k + 128], env["ident"][0:P, 0:P])
                for k in range(KH):
                    mm = pe.transpose(tp[:, b, 2 + k, 0:P], xs[:, s, 128 * k:128 * k + 128], env["ident"][0:P, 0:P])
                mm.then_inc(s_t, 1)

            def project(at):
                s, b = at.slot(RING), at.slot(2)
                if at.is_lead:
                    pe.wait_ge(s_msg, T)
                    pe.matmul(cps[:, 0:F + H1], carry[:, :], acc[:, (T - 1) % RING, :], start=True, stop=True).then_inc(s_c, 1)
                    return
                pe.wait_ge(s_xT, at.count(1, 1))
                wait(pe, s_sc, at.count(1, -1))
                for k in range(KH):
                    pe.matmul(hp[:, b, 0:F + H1], xT[:, s, k, :], w[:, k, :], start=(k == 0), stop=(k == 1))
                for k in range(KH):
                    mm = pe.matmul(hp[:, b, F + H1:HW], xT[:, s, 2 + k, :], ws[:, k, :], start=(k == 0), stop=(k == 1),
                                   skip_group_check=True)
                mm.then_inc(s_hp, 1)

            def turn_x3(at):
                s, b = at.slot(RING), at.slot(2)
                pe.wait_ge(s_x3, at.count(1, 1))
                wait(pe, s_x3T, at.count(1, 0))
                for k in range(KH):
                    mm = pe.transpose(tp3[:, k, 0:P], x3[:, s, 128 * k:128 * k + 128], env["ident"][0:P, 0:P])
                mm.then_inc(s_t3, 1)

            def product(at):
                s, b = at.slot(RING), at.slot(2)
                pe.wait_ge(s_x3T, at.count(1, 1))
                wait(pe, s_t1, at.count(1, -1))
                for k in range(KH):
                    mm = pe.matmul(xp[:, b, 0:F], x3T[:, s, k, :], w_self[:, k, 0:F], start=(k == 0), stop=(k == 1))
                mm.then_inc(s_xp, 1)
            run_stages(pe, [(7, product), (6, turn_x3), (1, project), (0, turn_rows)], T + 1)

        @block.scalar
        def _(act):
            def copy_rows(at):
                if at.is_lead:
                    return
                s, b = at.slot(RING), at.slot(2)
                act.wait_ge(s_t, at.count(1, 1))
                wait(act, s_hp, at.count(1, 1 - RING))
                act.copy(xT[:, s, :, :], tp[:, b, :, 0:P]).then_inc(s_xT, 1)

            def weights(at):
                if at.is_lead:
                    return
                s = at.slot(RING)
                act.wait_ge(s_sc, at.count(1, 1))
                wait(act, s_msg, at.count(1, 1 - RING))
                act.activation(sc[:, s, 2, :], sc[:, s, 1, :], ACT.Exp, scale=-1.0).then_inc(s_e4, 1)

            def elus(at):
                s = at.slot(RING)
                act.wait_ge(s_g, at.count(1, 1))
                wait(act, s_u, at.count(1, 1 - RING))
                act.activation(e1[:, s, :], g[:, s, :], ACT.Exp).then_inc(s_e1, 1)
                act.wait_ge(s_e1, at.count(1, 1))
                act.activation(e2[:, s, :], e1[:, s, :], ACT.Exp, bias=env["minus1"][0:P, :]).then_inc(s_e2, 1)

            def norm2(at):
                s = at.slot(RING)
                act.wait_ge(s_q, at.count(1, 1))
                wait(act, s_x2, at.count(1, 1 - RING))
                wait(act, s_x3, at.count(1, 1 - RING))
                ch = Chain(act, ca, at.count(2))
                rsqrt(act, ch, r[:, s, :], lnq[:, s, :], q[:, s, :])
                act.sem_inc(s_r, 1)

            def copy_x3(at):
                s = at.slot(RING)
                act.wait_ge(s_t3, at.count(1, 1))
                wait(act, s_xp, at.count(1, 1 - RING))
                act.copy(x3T[:, s, :, :], tp3[:, 0:KH, 0:P]).then_inc(s_x3T, 1)

            def exps(at):
                s, b = at.slot(RING), at.slot(2)
                act.wait_ge(s_t1, at.count(1, 1))
                wait(act, s_v, at.count(1, 1 - RING))
                act.activation(ex[:, s, :], t1[:, s, :], ACT.Exp, bias=env["minus1"][0:P, :]).then_inc(s_ex, 1)

            def norm_out(at):
                s = at.slot(RING)
                act.wait_ge(s_q3, at.count(1, 1))
                ch = Chain(act, cb, at.count(3))
                rsqrt(act, ch, r3[:, s, :], lnq3[:, s, :], q3[:, s, :])
                ch.step(act.activation(nm3[:, s, :], neg[:, s, :], ACT.Copy, scale=r3[:, s, :]))
                wait(act, s_wo[s], at.uses(RING, 16))
                act.activation(out[:, s, :], v[:, s, :], ACT.Identity, bias=nm3[:, s, :], scale=r3[:, s, :]).then_inc(s_out, 1)
            run_stages(act, [(8, norm_out), (7, exps), (6, copy_x3), (4, norm2), (3, elus), (1, weights), (0, copy_rows)], T + 1)

        @block.vector
        def _(dve):
            dve.memset(acc[:, RING - 1, :], 0.0).then_inc(s_init, 1)
            dve.memset(lead[:, :], 0.0).then_inc(s_init, 1)
            dve.wait_ge(s_init, 2)

            def score(at):
                if at.is_lead:
                    return
                s, b = at.slot(RING), at.slot(2)
                ch = Chain(dve, c1, at.count(4))
                dve.wait_ge(s_hp, at.count(1, 1))
                ch.step(dve.tensor_scalar(low[:, s, :], hp[:, b, 0:HW], 0.0, None, ALU.min))
                ch.step(dve.scalar_tensor_tensor(out=hg[:, s, :], in0=hp[:, b, 0:HW], scalar=0.0, in1=low[:, s, :],
                                                 op0=ALU.max, op1=ALU.add))
                ch.step(dve.tensor_tensor(sc[:, s, 0, :], hg[:, s, F:F + H1], hg[:, s, F + H1:HW], ALU.add))
                ch.step(dve.scalar_tensor_tensor(out=sc[:, s, 1, :], in0=sc[:, s, 0, :], scalar=ALPHA, in1=sc[:, s, 0, :],
                                                 op0=ALU.mult, op1=ALU.max))
                dve.sem_inc(s_sc, 1)

            def sums(at):
                s = at.slot(RING)
                ch = Chain(dve, c2, at.count(4))
                if at.is_lead:
                    dve.wait_ge(s_c, 1)
                    ch.step(dve.tensor_tensor(acc[:, s, :], cps[:, 0:F + H1], lead[:, :], ALU.add))
                else:
                    dve.wait_ge(s_e4, at.count(1, 1))
                    ch.step(dve.tensor_scalar(msg[:, s, F:F + H1], sc[:, s, 2, :], 0.0, None, ALU.max))
                    ch.step(dve.tensor_tensor(msg[:, s, 0:F].rearrange("p (h c) -> p h c", h=H1),
                                              hg[:, s, 0:F].rearrange("p (h c) -> p h c", h=H1),
                                              msg[:, s, F:F + H1].unsqueeze(2).broadcast_to([P, H1, C1]), ALU.mult))
                    ch.step(dve.scalar_tensor_tensor(out=acc[:, s, :], in0=acc[:, (s - 1) % RING, :], scalar=meta["same"][:, at.col],
                                                     in1=msg[:, s, :], op0=ALU.mult, op1=ALU.add))
                    ch.step(dve.scalar_tensor_tensor(out=lead[:, :], in0=acc[:, s, :], scalar=meta["lead_end"][:, at.col],
                                                     in1=lead[:, :], op0=ALU.mult, op1=ALU.add))
                dve.sem_inc(s_msg, 1)
                ch = Chain(dve, c3, at.count(4))
                wait(dve, s_e1, at.count(1, 1 - RING))
                ch.step(dve.tensor_scalar(den[:, s, :], acc[:, s, F:F + H1], TINY, None, ALU.max))
                ch.step(dve.reciprocal(rr[:, s, :], den[:, s, :]))
                ch.step(dve.tensor_tensor(hn[:, s, :].rearrange("p (h c) -> p h c", h=H1),
                                          acc[:, s, 0:F].rearrange("p (h c) -> p h c", h=H1),
                                          rr[:, s, :].unsqueeze(2).broadcast_to([P, H1, C1]), ALU.mult))
                ch.step(dve.tensor_scalar(g[:, s, :], hn[:, s, :], 0.0, None, ALU.min))
                dve.sem_inc(s_g, 1)

            def residual(at):
                s = at.slot(RING)
                ch = Chain(dve, c4, at.count(6))
                dve.wait_ge(s_e2, at.count(1, 1))
                dve.wait_ge(s_s[s], at.uses(RING, 16, 16))
                ch.step(dve.scalar_tensor_tensor(out=elu[:, s, :], in0=hn[:, s, :], scalar=0.0, in1=e2[:, s, :],
                                                 op0=ALU.max, op1=ALU.add))
                wait(dve, s_x2, at.count(1, 1 - RING))
                wait(dve, s_x3, at.count(1, 1 - RING))
                ch.step(dve.scalar_tensor_tensor(out=u[:, s, :], in0=elu[:, s, :], scalar=-1.0, in1=xs[:, s, :],
                                                 op0=ALU.add, op1=ALU.add))
                dve.sem_inc(s_u, 1)
                ch.step(dve.bn_stats(st[:, s, :], u[:, s, :]))
                dve.sem_inc(s_hold, 1)
                ch.step(dve.bn_aggr(mv[:, s, :], st[:, s, :]))
                wait(dve, s_r, at.count(1, 1 - RING))
                ch.step(dve.tensor_scalar(q[:, s, 0:1], mv[:, s, 1:2], EPS, None, ALU.add))
                ch.step(dve.tensor_scalar(q[:, s, 1:2], mv[:, s, 1:2], 1.0 + EPS, EPS * EPS, ALU.mult, ALU.add))
                dve.sem_inc(s_q, 1)

            def norms(at):
                s = at.slot(RING)
                dve.wait_ge(s_r, at.count(1, 1))
                wait(dve, s_w2[s], at.uses(RING, 16))
                dve.tensor_scalar(x2[:, s, :], u[:, s, :], mv[:, s, 0:1], r[:, s, 0:1], ALU.subtract, ALU.mult).then_inc(s_x2, 1)
                wait(dve, s_w3[s], at.uses(RING, 16))
                wait(dve, s_v, at.count(1, 1 - RING))
                wait(dve, s_t3, at.count(1, 1 - RING))
                dve.tensor_scalar(x3[:, s, :], u[:, s, :], mv[:, s, 0:1], r[:, s, 1:2], ALU.subtract, ALU.mult).then_inc(s_x3, 1)

            def biased(at):
                s, b = at.slot(RING), at.slot(2)
                dve.wait_ge(s_xp, at.count(1, 1))
                wait(dve, s_ex, at.count(1, 1 - RING))
                dve.tensor_tensor(t1[:, s, :], xp[:, b, 0:F], env["bias_all"][0:P, :], ALU.add).then_inc(s_t1, 1)

            def last(at):
                s = at.slot(RING)
                ch = Chain(dve, c5, at.count(6))
                dve.wait_ge(s_ex, at.count(1, 1))
                dve.wait_ge(s_t1, at.count(1, 1))
                ch.step(dve.scalar_tensor_tensor(out=el[:, s, :], in0=ex[:, s, :], scalar=1.0, in1=t1[:, s, :], op0=ALU.min, op1=ALU.max))
                wait(dve, s_out, at.count(1, 1 - RING))
                ch.step(dve.tensor_tensor(v[:, s, :], el[:, s, :], x3[:, s, :], ALU.add))
                dve.sem_inc(s_v, 1)
                ch.step(dve.bn_stats(st3[:, s, :], v[:, s, :]))
                dve.sem_inc(s_hold, 1)
                ch.step(dve.bn_aggr(mv3[:, s, :], st3[:, s, :]))
                wait(dve, s_out, at.count(1, 1 - RING))
                ch.step(dve.tensor_scalar(neg[:, s, :], mv3[:, s, 0:1], -1.0, None, ALU.mult))
                ch.step(dve.tensor_scalar(q3[:, s, :], mv3[:, s, 1:2], EPS, None, ALU.add))
                dve.sem_inc(s_q3, 1)
            run_stages(dve, [(8, last), (7, biased), (5, norms), (4, residual), (2, sums), (1, score)], T + 1)
    ph.end()


def segment_max(nc, env, name, value, most, heads):
    ph = Phase(nc, name)
    meta, key = env["meta"][1], env["srec"][1][:, :, 1]
    low = 1.0e38
    cut, cut_back = ph.sb("cut", [P, T]), ph.sb("cut_back", [P, T])
    run = ph.sb("run", [P, T, heads])
    ends = ph.sb("ends", [P, 2 * heads + 2, 128])
    penalty = ph.sb("penalty", [P, 2, 2, P])
    cand = ph.sb("cand", [P, 2 * heads, P])
    both, full = ph.sb("both", [P, 2, 2 * heads]), ph.sb("full", [P, 2, heads])
    rows = ph.ps("rows", [P, 2 * heads + 4, 128])
    s_v, s_ends, s_rows = ph.sem("steps"), ph.sem("ends"), ph.sem("rows")

    with nc.Block() as block:
        @block.vector
        def _(dve):
            ch = Chain(dve, s_v)

            def spread(src):
                for h in range(heads):
                    ch.step(dve.tensor_tensor_scan(run[:, :, h], cut[:, :], src[:, :, h], -low, ALU.add, ALU.max))
                for h in range(heads):
                    ch.step(dve.tensor_tensor_scan(most[:, ::-1, h], cut_back[:, ::-1], run[:, ::-1, h], -low, ALU.add, ALU.max))
            ch.step(dve.tensor_scalar(cut[:, :], meta["same"][:, :], low, -low, ALU.mult, ALU.add))
            ch.step(dve.tensor_copy(cut_back[:, 0:T - 1], cut[:, 1:T]))
            ch.step(dve.memset(cut_back[:, T - 1:T], 0.0))
            spread(value)
            for h in range(heads):
                ch.step(dve.tensor_copy(ends[:, 2 * h, :], most[:, 0, h:h + 1].broadcast_to([P, 128])))
                ch.step(dve.tensor_copy(ends[:, 2 * h + 1, :], most[:, T - 1, h:h + 1].broadcast_to([P, 128])))
            ch.step(dve.tensor_copy(ends[:, 2 * heads, :], key[:, 0:1].broadcast_to([P, 128])))
            ch.step(dve.tensor_copy(ends[:, 2 * heads + 1, :], key[:, T - 1:T].broadcast_to([P, 128])))
            dve.sem_inc(s_ends, 1)
            dve.wait_ge(s_rows, 1)
            for mine, t in enumerate((0, T - 1)):
                for theirs in range(2):
                    ch.step(dve.tensor_scalar(penalty[:, mine, theirs, :], rows[:, 2 * heads + theirs, 0:P], key[:, t:t + 1], -low,
                                              ALU.not_equal, ALU.mult))
                for h in range(heads):
                    ch.step(dve.tensor_tensor(cand[:, 2 * h:2 * h + 2, :], rows[:, 2 * h:2 * h + 2, 0:P], penalty[:, mine, :, :], ALU.add))
                ch.step(dve.tensor_reduce(both[:, mine, :], cand[:, :, :], X, ALU.max))
                ch.step(dve.tensor_reduce(full[:, mine, :], both[:, mine, :].rearrange("p (h e) -> p h e", e=2), X, ALU.max))
                ch.step(dve.tensor_tensor(most[:, t, :], most[:, t, :], full[:, mine, :], ALU.max))
            spread(most)

        @block.tensor
        def _(pe):
            pe.wait_ge(s_ends, 1)
            for n in range(2 * heads + 2):
                mm = pe.transpose(rows[:, n, 0:P], ends[:, n, 0:P], env["ident"][0:P, 0:P])
            mm.then_inc(s_rows, 1)
    ph.end()


def running_sums(dve, ch, meta, acc, lead, msg, at, s):
    ch.step(dve.scalar_tensor_tensor(out=acc[:, s, :], in0=acc[:, (s - 1) % RING, :], scalar=meta["same"][:, at.col],
                                     in1=msg[:, s, :], op0=ALU.mult, op1=ALU.add))
    ch.step(dve.scalar_tensor_tensor(out=lead[:, :], in0=acc[:, s, :], scalar=meta["lead_end"][:, at.col],
                                     in1=lead[:, :], op0=ALU.mult, op1=ALU.add))


def attention_scores(nc, env, V, score):
    ph = Phase(nc, "att1")
    meta, rec = env["meta"][1], env["srec"][1]
    gix = ph.sb("gix", [P, RING, 2], I32)
    xd, xs = ph.sb("xd", [P, RING, F]), ph.sb("xs", [P, RING, F])
    xT = ph.sb("xT", [128, RING, 4, P])
    qs, prod, dot = ph.sb("qs", [P, RING, F]), ph.sb("prod", [P, RING, F]), ph.sb("dot", [P, RING, H2])
    tp, kq, vp = ph.ps("tp", [128, 2, 4, 128]), ph.ps("kq", [P, 2, 512]), ph.ps("vp", [P, 2, 512])
    s_d, s_s, s_o = ([ph.sem(f"{n}{k}") for k in range(RING)] for n in ("dst_rows", "src_rows", "kept"))
    s_ix, s_t, s_xT, s_p, s_qs, s_V, s_dot, c1 = (ph.sem(n) for n in ("index", "transposed", "xT", "projected", "q", "v", "scored", "steps"))
    w_kv, w_q = env["w_kv"], env["w_q"]

    with nc.Block() as block:
        @block.gpsimd
        def _(pool):
            dram = Rows(ph, pool, N)

            def fetch(at):
                s = at.slot(RING)
                wait(pool, s_t, at.count(1, 1 - RING))
                wait(pool, s_o[s], at.uses(RING, 32))
                pool.tensor_copy(gix[:, s, 0:1], meta["node"][:, at.col]).then_inc(s_ix, 1)
                pool.tensor_copy(gix[:, s, 1:2], meta["other"][:, at.col]).then_inc(s_ix, 1)
                pool.wait_ge(s_ix, at.count(2, 2))
                dram.gather(xd[:, s, :], env["X2"], gix[:, s, 0:1], s_d[s])
                dram.gather(xs[:, s, :], env["X2"], gix[:, s, 1:2], s_s[s])
            run_stages(pool, [(0, fetch)], T)

        @block.sync
        def _(sp):
            def keep(at):
                s = at.slot(RING)
                sp.wait_ge(s_d[s], at.uses(RING, 16, 16))
                for a, n in CUTS:
                    sp.dma_start(env["D2"][at.col, a:a + n, :].rearrange("o p f -> (o p) f"), xd[a:a + n, s, :]).then_inc(s_o[s], 16)
            run_stages(sp, [(0, keep)], T)
            for s in range(RING):
                sp.wait_ge(s_o[s], 32 * (T // RING))

        @block.tensor
        def _(pe):
            def turn_rows(at):
                s, b = at.slot(RING), at.slot(2)
                pe.wait_ge(s_d[s], at.uses(RING, 16, 16))
                pe.wait_ge(s_s[s], at.uses(RING, 16, 16))
                wait(pe, s_xT, at.count(1, -1))
                for n, rows in enumerate((xs, xd)):
                    for k in range(KH):
                        mm = pe.transpose(tp[:, b, 2 * n + k, 0:P], rows[:, s, 128 * k:128 * k + 128], env["ident"][0:P, 0:P])
                mm.then_inc(s_t, 1)

            def project(at):
                s, b = at.slot(RING), at.slot(2)
                pe.wait_ge(s_xT, at.count(1, 1))
                wait(pe, s_dot, at.count(1, -1))
                wait(pe, s_V, at.count(1, -1))
                for out, x0, w in ((kq[:, b, F:2 * F], 2, w_q[:, :, :]), (kq[:, b, 0:F], 0, w_kv[:, :, 0:F]), (vp[:, b, 0:F], 0, w_kv[:, :, F:2 * F])):
                    for k in range(KH):
                        mm = pe.matmul(out, xT[:, s, x0 + k, :], w[:, k, :], start=(k == 0), stop=(k == 1), skip_group_check=True)
                mm.then_inc(s_p, 1)
            run_stages(pe, [(1, project), (0, turn_rows)], T)

        @block.scalar
        def _(act):
            def copy_rows(at):
                s, b = at.slot(RING), at.slot(2)
                act.wait_ge(s_t, at.count(1, 1))
                wait(act, s_p, at.count(1, 1 - RING))
                act.copy(xT[:, s, :, :], tp[:, b, :, 0:P]).then_inc(s_xT, 1)

            def copy_out(at):
                s, b = at.slot(RING), at.slot(2)
                act.wait_ge(s_p, at.count(1, 1))
                wait(act, s_dot, at.count(1, 1 - RING))
                act.mul(qs[:, s, :], kq[:, b, F:2 * F], float(C2) ** 0.5).then_inc(s_qs, 1)
                act.copy(V[:, at.col, :].rearrange("p o f -> p (o f)"), vp[:, b, 0:F]).then_inc(s_V, 1)
            run_stages(act, [(1, copy_out), (0, copy_rows)], T)

        @block.vector
        def _(dve):
            def dots(at):
                s, b = at.slot(RING), at.slot(2)
                ch = Chain(dve, c1, at.count(3))
                dve.wait_ge(s_qs, at.count(1, 1))
                ch.step(dve.tensor_tensor(prod[:, s, :], kq[:, b, 0:F], qs[:, s, :], ALU.mult))
                ch.step(dve.tensor_reduce(dot[:, s, :], prod[:, s, :].rearrange("p (h c) -> p h c", h=H2), X, ALU.add))
                ch.step(dve.tensor_tensor(score[:, at.col, :].rearrange("p o h -> p (o h)"), dot[:, s, :],
                                          rec[:, at.col, 4:4 + H2].rearrange("p o h -> p (o h)"), ALU.add))
                dve.sem_inc(s_dot, 1)
            run_stages(dve, [(1, dots)], T)
    ph.end()


def attention_sums(nc, env, V, score, most):
    ph = Phase(nc, "att2")
    meta, carry, w_o = env["meta"][1], env["meta"][1]["carry"], env["w_o"]
    W = F + H2
    wix = ph.sb("wix", [P, RING], I32)
    xd, msg, acc, lead = ph.sb("xd", [P, RING, F]), ph.sb("msg", [P, RING, W]), ph.sb("acc", [P, RING, W]), ph.sb("lead", [P, W])
    den = ph.sb("den", [P, RING, H2])
    rr, on, onT = ph.sb("rr", [P, RING, H2]), ph.sb("on", [P, RING, F]), ph.sb("onT", [128, RING, KH, P])
    u, x3 = ph.sb("u", [P, RING, F]), ph.sb("x3", [P, RING, F])
    st, mv, q, lnq, r = (ph.sb(n, [P, RING, k]) for n, k in (("st", 6), ("mv", 2), ("q", 1), ("lnq", 1), ("r", 1)))
    tp, op, cps = ph.ps("tp", [128, 2, 4, 128]), ph.ps("op", [P, 2, 512]), ph.ps("cps", [P, 512])
    s_l, s_w = ([ph.sem(f"{n}{k}") for k in range(RING)] for n in ("kept_rows", "stored"))
    (s_wx, s_a, s_msg, s_on, s_t, s_onT, s_o, s_u, s_q, s_r, s_x3, s_init, s_c, s_hold, c0, c1, c2, c3, ca) = (
        ph.sem(n) for n in ("windex", "weights", "msgs", "normed", "transposed", "copied", "product", "u", "q", "r", "x3",
                            "init", "carried", "hold", "steps0", "steps1", "steps2", "steps3", "rsqrt"))

    with nc.Block() as block:
        @block.sync
        def _(sp):
            def load(at):
                s = at.slot(RING)
                wait(sp, s_u, at.count(1, 1 - RING))
                src = env["D2"][slice(0, 1) if at.is_lead else at.col, :, :].rearrange("o p f -> (o p) f")
                load_rows(sp, xd[:, s, :], src, s_l[s])
            run_stages(sp, [(0, load)], T + 1)

        @block.gpsimd
        def _(pool):
            dram = Rows(ph, pool, N)

            def put(at):
                s = at.slot(RING)
                wait(pool, s_w[s], at.uses(RING, 16))
                pool.tensor_copy(wix[:, s:s + 1], meta["write"][:, at.col]).then_inc(s_wx, 1)
                pool.wait_ge(s_wx, at.count(1, 1))
                pool.wait_ge(s_x3, at.count(1, 1))
                dram.scatter(env["X3"], wix[:, s:s + 1], x3[:, s, :], s_w[s])
            run_stages(pool, [(0, put)], T + 1)
            for s in range(RING):
                pool.wait_ge(s_w[s], 16 * (T // RING + (s == 0)))

        @block.tensor
        def _(pe):
            def turn(at):
                s, b = at.slot(RING), at.slot(2)
                if at.is_lead:
                    pe.wait_ge(s_msg, T)
                    pe.matmul(cps[:, 0:W], carry[:, :], acc[:, (T - 1) % RING, :], start=True, stop=True).then_inc(s_c, 1)
                pe.wait_ge(s_on, at.count(1, 1))
                wait(pe, s_onT, at.count(1, -1))
                for k in range(KH):
                    mm = pe.transpose(tp[:, b, k, 0:P], on[:, s, 128 * k:128 * k + 128], env["ident"][0:P, 0:P])
                mm.then_inc(s_t, 1)

            def product(at):
                s, b = at.slot(RING), at.slot(2)
                pe.wait_ge(s_onT, at.count(1, 1))
                wait(pe, s_u, at.count(1, -1))
                for k in range(KH):
                    mm = pe.matmul(op[:, b, 0:F], onT[:, s, k, :], w_o[:, k, :], start=(k == 0), stop=(k == 1))
                mm.then_inc(s_o, 1)
            run_stages(pe, [(1, product), (0, turn)], T + 1)

        @block.scalar
        def _(act):
            act.wait_ge(s_a, 1)
            act.activation(score[:, :, :], score[:, :, :], ACT.Exp).then_inc(s_a, 1)

            def copy(at):
                s, b = at.slot(RING), at.slot(2)
                act.wait_ge(s_t, at.count(1, 1))
                wait(act, s_o, at.count(1, 1 - RING))
                act.copy(onT[:, s, :, :], tp[:, b, 0:KH, 0:P]).then_inc(s_onT, 1)

            def norm(at):
                s = at.slot(RING)
                act.wait_ge(s_q, at.count(1, 1))
                wait(act, s_x3, at.count(1, 1 - RING))
                ch = Chain(act, ca, at.count(2))
                rsqrt(act, ch, r[:, s, :], lnq[:, s, :], q[:, s, :])
                act.sem_inc(s_r, 1)
            run_stages(act, [(2, norm), (0, copy)], T + 1)

        @block.vector
        def _(dve):
            dve.memset(acc[:, RING - 1, :], 0.0).then_inc(s_init, 1)
            dve.memset(lead[:, :], 0.0).then_inc(s_init, 1)
            ch = Chain(dve, c0)
            ch.step(dve.tensor_tensor(score[:, :, :], score[:, :, :], most[:, :, :], ALU.subtract))
            dve.sem_inc(s_a, 1)
            dve.wait_ge(s_a, 2)
            dve.wait_ge(s_init, 2)

            def sums(at):
                s = at.slot(RING)
                ch = Chain(dve, c1, at.count(4))
                if at.is_lead:
                    dve.wait_ge(s_c, 1)
                    ch.step(dve.tensor_tensor(acc[:, s, :], cps[:, 0:W], lead[:, :], ALU.add))
                else:
                    a = score[:, at.col, :].rearrange("p o h -> p (o h)")
                    ch.step(dve.tensor_copy(msg[:, s, F:W], a))
                    ch.step(dve.tensor_tensor(msg[:, s, 0:F].rearrange("p (h c) -> p h c", h=H2),
                                              V[:, at.col, :].rearrange("p o (h c) -> p (o h) c", h=H2),
                                              a.unsqueeze(2).broadcast_to([P, H2, C2]), ALU.mult))
                    running_sums(dve, ch, meta, acc, lead, msg, at, s)
                dve.sem_inc(s_msg, 1)
                ch = Chain(dve, c2, at.count(3))
                ch.step(dve.tensor_scalar(den[:, s, :], acc[:, s, F:W], TINY, None, ALU.max))
                ch.step(dve.reciprocal(rr[:, s, :], den[:, s, :]))
                wait(dve, s_t, at.count(1, 1 - RING))
                ch.step(dve.tensor_tensor(on[:, s, :].rearrange("p (h c) -> p h c", h=H2),
                                          acc[:, s, 0:F].rearrange("p (h c) -> p h c", h=H2),
                                          rr[:, s, :].unsqueeze(2).broadcast_to([P, H2, C2]), ALU.mult))
                dve.sem_inc(s_on, 1)

            def residual(at):
                s, b = at.slot(RING), at.slot(2)
                ch = Chain(dve, c3, at.count(4))
                dve.wait_ge(s_o, at.count(1, 1))
                dve.wait_ge(s_l[s], at.uses(RING, 32, 32))
                wait(dve, s_x3, at.count(1, 1 - RING))
                ch.step(dve.tensor_tensor(u[:, s, :], op[:, b, 0:F], xd[:, s, :], ALU.add))
                dve.sem_inc(s_u, 1)
                ch.step(dve.bn_stats(st[:, s, :], u[:, s, :]))
                dve.sem_inc(s_hold, 1)
                ch.step(dve.bn_aggr(mv[:, s, :], st[:, s, :]))
                wait(dve, s_r, at.count(1, 1 - RING))
                ch.step(dve.tensor_scalar(q[:, s, :], mv[:, s, 1:2], EPS, None, ALU.add))
                dve.sem_inc(s_q, 1)

            def norms(at):
                s = at.slot(RING)
                dve.wait_ge(s_r, at.count(1, 1))
                wait(dve, s_w[s], at.uses(RING, 16))
                dve.tensor_scalar(x3[:, s, :], u[:, s, :], mv[:, s, 0:1], r[:, s, :], ALU.subtract, ALU.mult).then_inc(s_x3, 1)
            run_stages(dve, [(3, norms), (2, residual), (0, sums)], T + 1)
    ph.end()


def attention(nc, env, d):
    with ExitStack() as ctx:
        V = ctx.enter_context(nc.sbuf_tensor("att_v", [P, T, F], F32))
        score = ctx.enter_context(nc.sbuf_tensor("att_score", [P, T, H2], F32))
        most = ctx.enter_context(nc.sbuf_tensor("att_most", [P, T, H2], F32))
        attention_scores(nc, env, V, score)
        segment_max(nc, env, "attm", score, most, H2)
        attention_sums(nc, env, V, score, most)


def self_scores(nc, env, V, edge, loop):
    ph = Phase(nc, "self1")
    meta, w = env["meta"][1], env["w_self"]
    gix = ph.sb("gix", [P, RING, 2], I32)
    xd, xs = ph.sb("xd", [P, RING, F]), ph.sb("xs", [P, RING, F])
    xT = ph.sb("xT", [128, RING, 4, P])
    a_s, hd, sc = ph.sb("a_s", [P, RING, H1]), ph.sb("hd", [P, RING, F + 8]), ph.sb("sc", [P, RING, 2, H1])
    tp, sp_, dp = ph.ps("tp", [128, 2, 4, 128]), ph.ps("src", [P, 2, 512]), ph.ps("dst", [P, 2, 512])
    s_d, s_s, s_o, s_o2 = ([ph.sem(f"{n}{k}") for k in range(RING)] for n in ("dst_rows", "src_rows", "kept", "kept_h"))
    s_ix, s_t, s_xT, s_p, s_V, s_hd, s_sc, c1 = (ph.sem(n) for n in ("index", "transposed", "xT", "projected", "v", "hd", "scored", "steps"))

    with nc.Block() as block:
        @block.gpsimd
        def _(pool):
            dram = Rows(ph, pool, N)

            def fetch(at):
                s = at.slot(RING)
                wait(pool, s_t, at.count(1, 1 - RING))
                wait(pool, s_o[s], at.uses(RING, 32))
                pool.tensor_copy(gix[:, s, 0:1], meta["node"][:, at.col]).then_inc(s_ix, 1)
                pool.tensor_copy(gix[:, s, 1:2], meta["other"][:, at.col]).then_inc(s_ix, 1)
                pool.wait_ge(s_ix, at.count(2, 2))
                dram.gather(xd[:, s, :], env["X3"], gix[:, s, 0:1], s_d[s])
                dram.gather(xs[:, s, :], env["X3"], gix[:, s, 1:2], s_s[s])
            run_stages(pool, [(0, fetch)], T)

        @block.sync
        def _(sp):
            def keep(at):
                s = at.slot(RING)
                sp.wait_ge(s_d[s], at.uses(RING, 16, 16))
                for a, n in CUTS:
                    sp.dma_start(env["D3"][at.col, a:a + n, 0:F].rearrange("o p f -> (o p) f"), xd[a:a + n, s, :]).then_inc(s_o[s], 16)

            def keep_h(at):
                s = at.slot(RING)
                sp.wait_ge(s_hd, at.count(1, 1))
                for a, n in CUTS:
                    sp.dma_start(env["D3"][at.col, a:a + n, F:2 * F].rearrange("o p f -> (o p) f"), hd[a:a + n, s, 0:F]).then_inc(s_o2[s], 16)
            run_stages(sp, [(2, keep_h), (0, keep)], T)
            for s in range(RING):
                sp.wait_ge(s_o[s], 32 * (T // RING))
                sp.wait_ge(s_o2[s], 32 * (T // RING))

        @block.tensor
        def _(pe):
            def turn_rows(at):
                s, b = at.slot(RING), at.slot(2)
                pe.wait_ge(s_d[s], at.uses(RING, 16, 16))
                pe.wait_ge(s_s[s], at.uses(RING, 16, 16))
                wait(pe, s_xT, at.count(1, -1))
                for n, rows in enumerate((xs, xd)):
                    for k in range(KH):
                        mm = pe.transpose(tp[:, b, 2 * n + k, 0:P], rows[:, s, 128 * k:128 * k + 128], env["ident"][0:P, 0:P])
                mm.then_inc(s_t, 1)

            def project(at):
                s, b = at.slot(RING), at.slot(2)
                pe.wait_ge(s_xT, at.count(1, 1))
                wait(pe, s_V, at.count(2, -2))
                wait(pe, s_hd, at.count(1, -1))
                for out, x0, n in ((sp_[:, b, 0:F + 4], 0, F + 4), (dp[:, b, 0:F + 8], 2, F + 8)):
                    for k in range(KH):
                        mm = pe.matmul(out, xT[:, s, x0 + k, :], w[:, k, 0:n], start=(k == 0), stop=(k == 1))
                mm.then_inc(s_p, 1)
            run_stages(pe, [(1, project), (0, turn_rows)], T)

        @block.scalar
        def _(act):
            def copy_rows(at):
                s, b = at.slot(RING), at.slot(2)
                act.wait_ge(s_t, at.count(1, 1))
                wait(act, s_p, at.count(1, 1 - RING))
                act.copy(xT[:, s, :, :], tp[:, b, :, 0:P]).then_inc(s_xT, 1)

            def copy_out(at):
                s, b = at.slot(RING), at.slot(2)
                act.wait_ge(s_p, at.count(1, 1))
                wait(act, s_sc, at.count(1, 1 - RING))
                act.copy(V[:, at.col, :].rearrange("p o f -> p (o f)"), sp_[:, b, 0:F]).then_inc(s_V, 1)
                act.copy(a_s[:, s, :], sp_[:, b, F:F + H1]).then_inc(s_V, 1)
                wait(act, s_o2[s], at.uses(RING, 32))
                act.copy(hd[:, s, :], dp[:, b, 0:F + 8]).then_inc(s_hd, 1)
            run_stages(act, [(1, copy_out), (0, copy_rows)], T)

        @block.vector
        def _(dve):
            def scores(at):
                s = at.slot(RING)
                ch = Chain(dve, c1, at.count(4))
                dve.wait_ge(s_V, at.count(2, 2))
                dve.wait_ge(s_hd, at.count(1, 1))
                ch.step(dve.tensor_tensor(sc[:, s, 0, :], a_s[:, s, :], hd[:, s, F + 4:F + 8], ALU.add))
                ch.step(dve.tensor_tensor(sc[:, s, 1, :], hd[:, s, F:F + 4], hd[:, s, F + 4:F + 8], ALU.add))
                for n, out in enumerate((edge, loop)):
                    ch.step(dve.scalar_tensor_tensor(out=out[:, at.col, :].rearrange("p o h -> p (o h)"), in0=sc[:, s, n, :], scalar=ALPHA,
                                                     in1=sc[:, s, n, :], op0=ALU.mult, op1=ALU.max))
                dve.sem_inc(s_sc, 1)
            run_stages(dve, [(1, scores)], T)
    ph.end()


def self_sums(nc, env, d, V, edge, loop, most):
    ph = Phase(nc, "self2")
    meta, carry = env["meta"][1], env["meta"][1]["carry"]
    W = F + H1
    finite = ph.sb("finite", [P, T, H1])
    wix = ph.sb("wix", [P, RING], I32)
    xd, msg, acc, lead = ph.sb("xd", [P, RING, 2 * F]), ph.sb("msg", [P, RING, W]), ph.sb("acc", [P, RING, W]), ph.sb("lead", [P, W])
    own, tot = ph.sb("own", [P, RING, F]), ph.sb("tot", [P, RING, F])
    den, rr = ph.sb("den", [P, RING, H1]), ph.sb("rr", [P, RING, H1])
    agg, t1, ex, el, v, out = (ph.sb(n, [P, RING, F]) for n in ("agg", "t1", "ex", "el", "v", "out"))
    st, mv, q, lnq, r = (ph.sb(n, [P, RING, k]) for n, k in (("st", 6), ("mv", 2), ("q", 1), ("lnq", 1), ("r", 1)))
    cps = ph.ps("cps", [P, 512])
    s_l, s_w = ([ph.sem(f"{n}{k}") for k in range(RING)] for n in ("kept_rows", "stored"))
    (s_wx, s_a, s_msg, s_t1, s_ex, s_v, s_q, s_r, s_out, s_init, s_c, s_hold, c0, c1, c2, c3, ca) = (
        ph.sem(n) for n in ("windex", "weights", "msgs", "t1", "exp", "v", "q", "r", "out",
                            "init", "carried", "hold", "steps0", "steps1", "steps2", "steps3", "rsqrt"))

    with nc.Block() as block:
        @block.sync
        def _(sp):
            def load(at):
                s = at.slot(RING)
                wait(sp, s_v, at.count(1, 1 - RING))
                src = env["D3"][slice(0, 1) if at.is_lead else at.col, :, :].rearrange("o p f -> (o p) f")
                load_rows(sp, xd[:, s, :], src, s_l[s])
            run_stages(sp, [(0, load)], T + 1)

        @block.gpsimd
        def _(pool):
            dram = Rows(ph, pool, N)

            def put(at):
                s = at.slot(RING)
                wait(pool, s_w[s], at.uses(RING, 16))
                pool.tensor_copy(wix[:, s:s + 1], meta["write"][:, at.col]).then_inc(s_wx, 1)
                pool.wait_ge(s_wx, at.count(1, 1))
                pool.wait_ge(s_out, at.count(1, 1))
                dram.scatter(d["out"], wix[:, s:s + 1], out[:, s, :], s_w[s])
            run_stages(pool, [(0, put)], T + 1)
            for s in range(RING):
                pool.wait_ge(s_w[s], 16 * (T // RING + (s == 0)))

        @block.tensor
        def _(pe):
            pe.wait_ge(s_msg, T)
            pe.matmul(cps[:, 0:W], carry[:, :], acc[:, (T - 1) % RING, :], start=True, stop=True).then_inc(s_c, 1)

        @block.scalar
        def _(act):
            act.wait_ge(s_a, 1)
            act.activation(edge[:, :, :], edge[:, :, :], ACT.Exp).then_inc(s_a, 1)
            act.activation(loop[:, :, :], loop[:, :, :], ACT.Exp).then_inc(s_a, 1)

            def exps(at):
                s = at.slot(RING)
                act.wait_ge(s_t1, at.count(1, 1))
                wait(act, s_v, at.count(1, 1 - RING))
                act.activation(ex[:, s, :], t1[:, s, :], ACT.Exp, bias=env["minus1"][0:P, :]).then_inc(s_ex, 1)

            def norm(at):
                s = at.slot(RING)
                act.wait_ge(s_q, at.count(1, 1))
                wait(act, s_out, at.count(1, 1 - RING))
                ch = Chain(act, ca, at.count(2))
                rsqrt(act, ch, r[:, s, :], lnq[:, s, :], q[:, s, :])
                act.sem_inc(s_r, 1)
            run_stages(act, [(1, norm), (0, exps)], T + 1)

        @block.vector
        def _(dve):
            dve.memset(acc[:, RING - 1, :], 0.0).then_inc(s_init, 1)
            dve.memset(lead[:, :], 0.0).then_inc(s_init, 1)
            ch = Chain(dve, c0)
            ch.step(dve.tensor_tensor(finite[:, :, :], most[:, :, :], most[:, :, :], ALU.subtract))
            ch.step(dve.tensor_scalar(finite[:, :, :], finite[:, :, :], 0.0, None, ALU.is_equal))
            ch.step(dve.tensor_scalar(most[:, :, :], most[:, :, :], -BIG, BIG, ALU.max, ALU.min))
            ch.step(dve.tensor_tensor(most[:, :, :], most[:, :, :], finite[:, :, :], ALU.mult))
            ch.step(dve.tensor_tensor(edge[:, :, :], edge[:, :, :], most[:, :, :], ALU.subtract))
            ch.step(dve.tensor_tensor(loop[:, :, :], loop[:, :, :], most[:, :, :], ALU.subtract))
            dve.sem_inc(s_a, 1)
            dve.wait_ge(s_a, 3)
            dve.wait_ge(s_init, 2)

            def heads(ap):
                return ap.rearrange("p (h c) -> p h c", h=H1)

            def each_head(ap):
                return ap.unsqueeze(2).broadcast_to([P, H1, C1])

            def sums(at):
                s = at.slot(RING)
                ch = Chain(dve, c1, at.count(4))
                if at.is_lead:
                    dve.wait_ge(s_c, 1)
                    ch.step(dve.tensor_tensor(acc[:, s, :], cps[:, 0:W], lead[:, :], ALU.add))
                else:
                    a = edge[:, at.col, :].rearrange("p o h -> p (o h)")
                    ch.step(dve.tensor_copy(msg[:, s, F:W], a))
                    ch.step(dve.tensor_tensor(heads(msg[:, s, 0:F]), V[:, at.col, :].rearrange("p o (h c) -> p (o h) c", h=H1),
                                              each_head(a), ALU.mult))
                    running_sums(dve, ch, meta, acc, lead, msg, at, s)
                dve.sem_inc(s_msg, 1)
                mine = loop[:, 0, :] if at.is_lead else loop[:, at.col, :].rearrange("p o h -> p (o h)")
                ch = Chain(dve, c2, at.count(7))
                dve.wait_ge(s_l[s], at.uses(RING, 32, 32))
                ch.step(dve.tensor_tensor(heads(own[:, s, :]), heads(xd[:, s, F:2 * F]), each_head(mine), ALU.mult))
                ch.step(dve.tensor_tensor(tot[:, s, :], own[:, s, :], acc[:, s, 0:F], ALU.add))
                ch.step(dve.tensor_tensor(den[:, s, :], acc[:, s, F:W], mine, ALU.add))
                ch.step(dve.tensor_scalar(den[:, s, :], den[:, s, :], TINY, None, ALU.max))
                ch.step(dve.reciprocal(rr[:, s, :], den[:, s, :]))
                ch.step(dve.tensor_tensor(heads(agg[:, s, :]), heads(tot[:, s, :]), each_head(rr[:, s, :]), ALU.mult))
                wait(dve, s_ex, at.count(1, 1 - RING))
                ch.step(dve.tensor_tensor(t1[:, s, :], agg[:, s, :], env["bias_all"][0:P, :], ALU.add))
                dve.sem_inc(s_t1, 1)

            def residual(at):
                s = at.slot(RING)
                ch = Chain(dve, c3, at.count(5))
                dve.wait_ge(s_ex, at.count(1, 1))
                ch.step(dve.scalar_tensor_tensor(out=el[:, s, :], in0=ex[:, s, :], scalar=1.0, in1=t1[:, s, :], op0=ALU.min, op1=ALU.max))
                wait(dve, s_out, at.count(1, 1 - RING))
                ch.step(dve.tensor_tensor(v[:, s, :], el[:, s, :], xd[:, s, 0:F], ALU.add))
                dve.sem_inc(s_v, 1)
                ch.step(dve.bn_stats(st[:, s, :], v[:, s, :]))
                dve.sem_inc(s_hold, 1)
                ch.step(dve.bn_aggr(mv[:, s, :], st[:, s, :]))
                wait(dve, s_r, at.count(1, 1 - RING))
                ch.step(dve.tensor_scalar(q[:, s, :], mv[:, s, 1:2], EPS, None, ALU.add))
                dve.sem_inc(s_q, 1)

            def norms(at):
                s = at.slot(RING)
                dve.wait_ge(s_r, at.count(1, 1))
                wait(dve, s_w[s], at.uses(RING, 16))
                dve.tensor_scalar(out[:, s, :], v[:, s, :], mv[:, s, 0:1], r[:, s, :], ALU.subtract, ALU.mult).then_inc(s_out, 1)
            run_stages(dve, [(2, norms), (1, residual), (0, sums)], T + 1)
    ph.end()


def self_loops(nc, env, d):
    with ExitStack() as ctx:
        V = ctx.enter_context(nc.sbuf_tensor("self_v", [P, T, F], F32))
        edge, loop, top, most = (ctx.enter_context(nc.sbuf_tensor(f"self_{n}", [P, T, H1], F32)) for n in ("edge", "loop", "top", "most"))
        self_scores(nc, env, V, edge, loop)
        larger(nc, edge, loop, top)
        segment_max(nc, env, "selfm", top, most, H1)
        self_sums(nc, env, d, V, edge, loop, most)


def larger(nc, edge, loop, top):
    ph = Phase(nc, "larger")
    done = ph.sem("done")
    with nc.Block() as block:
        @block.vector
        def _(dve):
            dve.tensor_tensor(top[:, :, :], edge[:, :, :], loop[:, :, :], ALU.max).then_inc(done, 1)
            dve.wait_ge(done, 1)
    ph.end()


def graph_net(nc, d, upto="all", debug=None):
    with ExitStack() as ctx:
        def sb(name, shape, dt=F32):
            return ctx.enter_context(nc.sbuf_tensor(name, shape, dt))
        scratch = (lambda n, s: (debug or {}).get(n) if (debug or {}).get(n) is not None else nc.dram_tensor(n, s, F32, kind="Internal").ap())
        env = {
            "ident": sb("ident", [128, 128]), "ident_bf": sb("ident_bf", [128, 128], BF16),
            "before": sb("before", [128, 128]), "after": sb("after", [128, 128]), "ones": sb("ones", [128, 128]),
            "iota_row": sb("iota_row", [128, 256], BF16), 
            "zrow": sb("zrow", [128, 512], BF16), "zcol": sb("zcol", [128, 128]), "zwide": sb("zwide", [128, F + 4]),
            "onep": sb("onep", [128, 1]), "minus1": sb("minus1", [128, 1]),
            "one3": sb("one3", [3, 128], BF16), "bias3": sb("bias3", [3, F], BF16), "bias_all": sb("bias_all", [128, F]),
            "bn": sb("bn", [128, 6, KH]), "affine": sb("affine", [128, 4, KH]),
            "w1": sb("w1", [128, KH, F]), "w2": sb("w2", [128, KH, F]),
            "w_gat": sb("w_gat", [128, KH, F + 4]), "w_gat_s": sb("w_gat_s", [128, KH, 4]),
            "w_self": sb("w_self", [128, KH, F + 8]), "w_kv": sb("w_kv", [128, KH, 2 * F]),
            "w_q": sb("w_q", [128, KH, F]), "w_o": sb("w_o", [128, KH, F]),
            "H": scratch("H", [N, F]), "X1": scratch("X1", [N, F]), "X2": scratch("X2", [N, F]),
            "Y2": scratch("Y2", [NCH, 128, KH * CH]), "D2": scratch("D2", [T, P, F]), "D3": scratch("D3", [T, P, 2 * F]),
            "sorted": [scratch("by_src", [E, RC]), scratch("by_dst", [E, RC])],
        }
        env["X3"] = env["H"]
        meta = [{
            "same": sb(f"same{k}", [P, T]), "lead_end": sb(f"lead_end{k}", [P, T]), "emit": sb(f"emit{k}", [P, T + 1]),
            "node": sb(f"node{k}", [P, T + 1], I32), "other": sb(f"other{k}", [P, T], I32),
            "write": sb(f"write{k}", [P, T + 1], I32), "carry": sb(f"carry{k}", [P, P]),
        } for k in range(2)]
        env["meta"] = meta
        env["srec"] = [sb(f"srec{k}", [P, T, RC]) for k in range(2)]
        order = ["setup", "hist", "rank", "seg", "gin", "mom", "mlp", "nodes", "gat", "att", "self"]
        last = len(order) if upto == "all" else order.index(upto) + 1
        with ExitStack() as early:
            env["gram"] = early.enter_context(nc.psum_tensor("gram", [128, KH, 512], F32))
            with ExitStack() as sort:
                env["rec"] = sort.enter_context(nc.sbuf_tensor("rec", [P, T, RC], F32))
                env["digit"] = sort.enter_context(nc.sbuf_tensor("digit", [P, 2, 2, T], F32))
                env["base"] = sort.enter_context(nc.sbuf_tensor("base", [128, 2, 2, 256], F32))
                env["keyf"] = sort.enter_context(nc.sbuf_tensor("keyf", [P, 2, T], F32))
                setup(nc, env, d)
                if last > 1:
                    histogram(nc, env)
                if last > 2:
                    rank(nc, env, d)
            if last > 3:
                segments(nc, env)
            if last > 4:
                gin_edges(nc, env, d)
            if last > 5:
                moments(nc, env)
        if last > 6:
            mlp(nc, env)
        if last > 7:
            nodes(nc, env, d)
        if last > 8:
            gat_edges(nc, env, d)
        if last > 9:
            attention(nc, env, d)
        if last > 10:
            self_loops(nc, env, d)


_IN = ("x", "src", "dst", "edge_attr_8", "edge_weight", "L0_gnn_eps", "L0_gnn_W1", "L0_gnn_b1", "L0_gnn_g1", "L0_gnn_be1",
       "L0_gnn_W2", "L0_gnn_b2", "L0_gnn_g2", "L0_gnn_be2", "L3_gnn_W", "L3_gnn_bias")


def lay_out(inputs):
    a = {n: np.ascontiguousarray(np.asarray(inputs[n])) for n in _IN}
    a["W_gat"] = np.ascontiguousarray(np.asarray(inputs["L1_gnn_W"]).transpose(1, 0, 2).reshape(F, F))
    att = np.asarray(inputs["L1_gnn_a"])
    a["a_src"] = np.ascontiguousarray(att[:, 0, :C1].reshape(F))
    a["a_dst"] = np.ascontiguousarray(att[:, 0, C1:].reshape(F))
    a["att_src"] = np.ascontiguousarray(np.asarray(inputs["L3_gnn_att_src"]).reshape(F))
    a["att_dst"] = np.ascontiguousarray(np.asarray(inputs["L3_gnn_att_dst"]).reshape(F))
    for n in "qkvo":
        a[f"W{n}T"] = np.ascontiguousarray(np.asarray(inputs[f"L2_gnn_W{n}"]).T)
    return a


def kernel(**inputs):
    import concourse.bacc as bacc
    from concourse.bass_utils import run_bass_kernel_spmd

    nc = bacc.Bacc("TRN2", target_bir_lowering=False, num_devices=1)
    arrays = lay_out(inputs)
    d = {n: nc.dram_tensor(n, a.shape, mybir.dt.from_np(a.dtype), kind="ExternalInput").ap() for n, a in arrays.items()}
    d["out"] = nc.dram_tensor("out", (N, F), F32, kind="ExternalOutput").ap()
    graph_net(nc, d)
    return run_bass_kernel_spmd(nc, [arrays], core_ids=[0]).results[0]["out"]
```
